# Optimizing a Trainium2 kernel written in Bass

```python
import numpy as np
import jax
import jax.numpy as jnp

def _softmax(x, axis=-1):
    return jax.nn.softmax(x, axis=axis)

def _gelu(x):
    return jax.nn.gelu(x, approximate=True)

def _silu(x):
    return jax.nn.silu(x)

def _sigmoid(x):
    return jax.nn.sigmoid(x)

def _layernorm(x, axis=-1, eps=1e-05):
    m = jnp.mean(x, axis=axis, keepdims=True)
    v = jnp.var(x, axis=axis, keepdims=True)
    return (x - m) / jnp.sqrt(v + eps)

def _scatter_add(tgt, idx, src, axis=0):
    return tgt.at[idx].add(src)

def _segment_sum(src, seg, n):
    return jax.ops.segment_sum(src, seg, n)
kernel_name = 'mk_gnn_resnorm_d4_gnn_r32_0d95a0'

def setup_inputs(seed: int=0):
    np.random.seed(seed)
    _w = jnp.asarray

    def _rec_inputs():
        import jax
        import jax.numpy as jnp
        _gk = jax.random.key(seed)
        x = -0.000202 + 1 * jax.random.normal(jax.random.fold_in(_gk, 1), (50000, 128), jnp.float32)
        src = jax.random.randint(jax.random.fold_in(_gk, 2), (50000,), 0, 50000, jnp.int32)
        dst = jax.random.randint(jax.random.fold_in(_gk, 3), (50000,), 0, 50000, jnp.int32)
        _o = jnp.argsort(dst, stable=True)
        src = src[_o]
        dst = dst[_o]
        edge_attr_32 = -1.78115e-05 + 1.00007 * jax.random.normal(jax.random.fold_in(_gk, 11), (50000, 32), jnp.float32)
        edge_attr_32_n2 = -1.78115e-05 + 1.00007 * jax.random.normal(jax.random.fold_in(_gk, 12), (50000, 32), jnp.float32)
        edge_type_16 = jax.random.randint(jax.random.fold_in(_gk, 14), (50000,), 0, 16, jnp.int32)
        return (x, src, dst, edge_attr_32, edge_attr_32_n2, edge_type_16)
    x, src, dst, edge_attr_32, edge_attr_32_n2, edge_type_16 = _rec_inputs()

    def _L0_gnn_setup():
        import jax, jax.numpy as jnp
        import numpy as np
        N_NODES = 50000
        N_EDGES = 25000
        D = 128
        LN_EPS = 1e-05
        key = jax.random.key(seed)
        ks = jax.random.split(key, 8)
        h = jax.random.normal(ks[0], (N_NODES, D), dtype=jnp.float32)
        edge_index = jax.random.randint(ks[1], (2, N_EDGES), 0, N_NODES, dtype=jnp.int32)
        s = 1.0 / np.sqrt(D)
        W1 = jax.random.uniform(ks[2], (D, D), jnp.float32, -s, s)
        b1 = jax.random.uniform(ks[3], (D,), jnp.float32, -s, s)
        W2 = jax.random.uniform(ks[4], (D, D), jnp.float32, -s, s)
        b2 = jax.random.uniform(ks[5], (D,), jnp.float32, -s, s)
        eps = jnp.zeros((), jnp.float32)
        gamma = jnp.ones((D,), jnp.float32)
        beta = jnp.zeros((D,), jnp.float32)
        return {'h': h, 'edge_index': edge_index, 'eps': eps, 'W1': W1, 'b1': b1, 'W2': W2, 'b2': b2, 'gamma': gamma, 'beta': beta}
    _L0_gnn_all = _L0_gnn_setup()
    _L0_gnn_in = {k: v for k, v in _L0_gnn_all.items() if k in ('eps', 'W1', 'b1', 'W2', 'b2', 'gamma', 'beta')}
    del _L0_gnn_all

    def _L1_gnn_setup():
        import jax, jax.numpy as jnp
        import numpy as np
        N_NODES = 3125

        def gcn_conv(x, edge_index, W, b):
            N = x.shape[0]
            loop = jnp.arange(N, dtype=edge_index.dtype)
            src = jnp.concatenate([edge_index[0], loop])
            dst = jnp.concatenate([edge_index[1], loop])
            deg = jax.ops.segment_sum(jnp.ones_like(dst, dtype=x.dtype), dst, num_segments=N)
            dinv = jnp.where(deg > 0, jax.lax.rsqrt(deg), 0.0)
            norm = dinv[src] * dinv[dst]
            h = x @ W
            msg = h[src] * norm[:, None]
            out = jax.ops.segment_sum(msg, dst, num_segments=N)
            return out + b
        key = jax.random.key(seed)
        k1, k2, k3, k4 = jax.random.split(key, 4)
        x = jax.random.normal(k1, (N_NODES, 128), dtype=jnp.float32)
        edge_index = jax.random.randint(k2, (2, 18750), 0, N_NODES, dtype=jnp.int64)
        W1 = jax.random.normal(k3, (128, 256), dtype=jnp.float32) * (1.0 / np.sqrt(128))
        b1 = jnp.zeros((256,), dtype=jnp.float32)
        W2 = jax.random.normal(k4, (256, 128), dtype=jnp.float32) * (1.0 / np.sqrt(256))
        b2 = jnp.zeros((128,), dtype=jnp.float32)
        return {'x': x, 'edge_index': edge_index, 'W1': W1, 'b1': b1, 'W2': W2, 'b2': b2}
    _L1_gnn_all = _L1_gnn_setup()
    _L1_gnn_in = {k: v for k, v in _L1_gnn_all.items() if k in ('W1', 'b1', 'W2', 'b2')}
    del _L1_gnn_all

    def _L2_gnn_setup():
        import jax, jax.numpy as jnp
        import numpy as np
        N_NODES = 50000
        D_FEAT = 128
        N_EDGES = 18750
        ALPHA = 0.1

        def _appnp_k1(x, edge_index):
            n = x.shape[0]
            loops = jnp.arange(n, dtype=edge_index.dtype)
            src = jnp.concatenate([edge_index[0], loops])
            dst = jnp.concatenate([edge_index[1], loops])
            ones = jnp.ones(src.shape[0], dtype=x.dtype)
            deg = jax.ops.segment_sum(ones, dst, num_segments=n)
            dinv = jnp.where(deg > 0, jax.lax.rsqrt(deg), 0.0)
            norm = dinv[src] * dinv[dst]
            agg = jax.ops.segment_sum(x[src] * norm[:, None], dst, num_segments=n)
            return (1.0 - ALPHA) * agg + ALPHA * x
        key = jax.random.key(seed)
        k1, k2 = jax.random.split(key)
        x = jax.random.normal(k1, (N_NODES, D_FEAT), dtype=jnp.float32)
        edge_index = jax.random.randint(k2, (2, N_EDGES), 0, N_NODES, dtype=jnp.int64)
        return {'x': x, 'edge_index': edge_index}
    _L2_gnn_all = _L2_gnn_setup()
    _L2_gnn_in = {k: v for k, v in _L2_gnn_all.items() if k in ()}
    del _L2_gnn_all

    def _L3_gnn_setup():
        import jax, jax.numpy as jnp
        import numpy as np
        N = 50000
        E = 12500
        D_NODE = 128
        D_EDGE = 32
        D_OUT = 128
        R = 16
        B = 8
        key = jax.random.key(seed)
        ks = jax.random.split(key, 12)
        s = 0.05
        return {'vfts': jax.random.normal(ks[0], (N, D_NODE), dtype=jnp.float32), 'adjs': jax.random.randint(ks[1], (2, E), 0, N, dtype=jnp.int32), 'rels': jax.random.randint(ks[2], (E,), 0, R, dtype=jnp.int32), 'embed_rels': jax.random.normal(ks[3], (E, D_EDGE), dtype=jnp.float32), 'embed_rels_target': jax.random.normal(ks[4], (E, D_EDGE), dtype=jnp.float32), 'weight': jax.random.normal(ks[5], (B, D_NODE, D_OUT), dtype=jnp.float32) * s, 'comp': jax.random.normal(ks[6], (R, B), dtype=jnp.float32) * s, 'attn_w1': jax.random.normal(ks[7], (2 * D_NODE + 2 * D_EDGE, D_OUT), dtype=jnp.float32) * s, 'attn_b1': jnp.zeros((D_OUT,), dtype=jnp.float32), 'attn_w2': jax.random.normal(ks[8], (D_OUT, 1), dtype=jnp.float32) * s, 'attn_b2': jnp.zeros((1,), dtype=jnp.float32), 'update': jax.random.normal(ks[9], (D_NODE, D_OUT), dtype=jnp.float32) * s}
    _L3_gnn_all = _L3_gnn_setup()
    _L3_gnn_in = {k: v for k, v in _L3_gnn_all.items() if k in ('weight', 'comp', 'attn_w1', 'attn_b1', 'attn_w2', 'attn_b2', 'update')}
    del _L3_gnn_all
    return {'x': x, 'src': src, 'dst': dst, 'edge_attr_32': edge_attr_32, 'edge_attr_32_n2': edge_attr_32_n2, 'edge_type_16': edge_type_16, 'L0_gnn_eps': _L0_gnn_in['eps'], 'L0_gnn_W1': _L0_gnn_in['W1'], 'L0_gnn_b1': _L0_gnn_in['b1'], 'L0_gnn_W2': _L0_gnn_in['W2'], 'L0_gnn_b2': _L0_gnn_in['b2'], 'L0_gnn_gamma': _L0_gnn_in['gamma'], 'L0_gnn_beta': _L0_gnn_in['beta'], 'L1_gnn_W1': _L1_gnn_in['W1'], 'L1_gnn_b1': _L1_gnn_in['b1'], 'L1_gnn_W2': _L1_gnn_in['W2'], 'L1_gnn_b2': _L1_gnn_in['b2'], 'L3_gnn_weight': _L3_gnn_in['weight'], 'L3_gnn_comp': _L3_gnn_in['comp'], 'L3_gnn_attn_w1': _L3_gnn_in['attn_w1'], 'L3_gnn_attn_b1': _L3_gnn_in['attn_b1'], 'L3_gnn_attn_w2': _L3_gnn_in['attn_w2'], 'L3_gnn_attn_b2': _L3_gnn_in['attn_b2'], 'L3_gnn_update': _L3_gnn_in['update']}

def reference(x, src, dst, edge_attr_32, edge_attr_32_n2, edge_type_16, L0_gnn_eps, L0_gnn_W1, L0_gnn_b1, L0_gnn_W2, L0_gnn_b2, L0_gnn_gamma, L0_gnn_beta, L1_gnn_W1, L1_gnn_b1, L1_gnn_W2, L1_gnn_b2, L3_gnn_weight, L3_gnn_comp, L3_gnn_attn_w1, L3_gnn_attn_b1, L3_gnn_attn_w2, L3_gnn_attn_b2, L3_gnn_update):
    import jax
    import jax.numpy as jnp

    def _L0_gnn_ref(h, edge_index, eps, W1, b1, W2, b2, gamma, beta):
        import jax, jax.numpy as jnp
        import numpy as np
        N_NODES = 50000
        N_EDGES = 25000
        D = 128
        LN_EPS = 1e-05
        src, dst = (edge_index[0], edge_index[1])
        agg = jax.ops.segment_sum(h[src], dst, num_segments=h.shape[0])
        z = (1.0 + eps) * h + agg
        z = jax.nn.relu(z @ W1 + b1) @ W2 + b2
        r = z + h
        mu = jnp.mean(r, axis=-1, keepdims=True)
        var = jnp.mean((r - mu) ** 2, axis=-1, keepdims=True)
        ln = (r - mu) * jax.lax.rsqrt(var + LN_EPS) * gamma + beta
        return jax.nn.relu(ln)

    def _L1_gnn_ref(x, edge_index, W1, b1, W2, b2):
        import jax, jax.numpy as jnp
        import numpy as np
        N_NODES = 3125

        def gcn_conv(x, edge_index, W, b):
            N = x.shape[0]
            loop = jnp.arange(N, dtype=edge_index.dtype)
            src = jnp.concatenate([edge_index[0], loop])
            dst = jnp.concatenate([edge_index[1], loop])
            deg = jax.ops.segment_sum(jnp.ones_like(dst, dtype=x.dtype), dst, num_segments=N)
            dinv = jnp.where(deg > 0, jax.lax.rsqrt(deg), 0.0)
            norm = dinv[src] * dinv[dst]
            h = x @ W
            msg = h[src] * norm[:, None]
            out = jax.ops.segment_sum(msg, dst, num_segments=N)
            return out + b
        h = jax.nn.relu(gcn_conv(x, edge_index, W1, b1))
        h = jax.nn.relu(gcn_conv(h, edge_index, W2, b2))
        return h

    def _L2_gnn_ref(x, edge_index):
        import jax, jax.numpy as jnp
        import numpy as np
        N_NODES = 50000
        D_FEAT = 128
        N_EDGES = 18750
        ALPHA = 0.1

        def _appnp_k1(x, edge_index):
            n = x.shape[0]
            loops = jnp.arange(n, dtype=edge_index.dtype)
            src = jnp.concatenate([edge_index[0], loops])
            dst = jnp.concatenate([edge_index[1], loops])
            ones = jnp.ones(src.shape[0], dtype=x.dtype)
            deg = jax.ops.segment_sum(ones, dst, num_segments=n)
            dinv = jnp.where(deg > 0, jax.lax.rsqrt(deg), 0.0)
            norm = dinv[src] * dinv[dst]
            agg = jax.ops.segment_sum(x[src] * norm[:, None], dst, num_segments=n)
            return (1.0 - ALPHA) * agg + ALPHA * x
        h = _appnp_k1(x, edge_index)
        return x + jax.nn.relu(h)

    def _L3_gnn_ref(vfts, adjs, rels, embed_rels, embed_rels_target, weight, comp, attn_w1, attn_b1, attn_w2, attn_b2, update):
        import jax, jax.numpy as jnp
        import numpy as np
        N = 50000
        E = 12500
        D_NODE = 128
        D_EDGE = 32
        D_OUT = 128
        R = 16
        B = 8
        src, dst = (adjs[0], adjs[1])
        erps = jnp.concatenate((vfts[src], vfts[dst], embed_rels, embed_rels_target), axis=1)
        h = jax.nn.relu(erps @ attn_w1 + attn_b1)
        alphas = jax.nn.sigmoid(h @ attn_w2 + attn_b2)
        w_rel = (comp @ weight.reshape(B, D_NODE * D_OUT)).reshape(R, D_NODE, D_OUT)
        srcs_dense = jnp.einsum('nd,rdo->rno', vfts, w_rel)
        srcs = alphas[rels] * srcs_dense[rels, src]
        vrps = jnp.zeros((vfts.shape[0], D_OUT), dtype=vfts.dtype)
        vrps = vrps.at[dst].add(srcs)
        dsts = vfts @ update
        vrps = vrps.at[dst].add(dsts[dst])
        return jax.nn.relu(vrps)
    edge_index = jnp.stack([src, dst])
    x = _layernorm(x + _L0_gnn_ref(x, edge_index, L0_gnn_eps, L0_gnn_W1, L0_gnn_b1, L0_gnn_W2, L0_gnn_b2, L0_gnn_gamma, L0_gnn_beta), axis=-1)
    x = _layernorm(x + _L1_gnn_ref(x, edge_index, L1_gnn_W1, L1_gnn_b1, L1_gnn_W2, L1_gnn_b2), axis=-1)
    x = _layernorm(x + _L2_gnn_ref(x, edge_index), axis=-1)
    x = _layernorm(x + _L3_gnn_ref(x, edge_index, edge_type_16, edge_attr_32, edge_attr_32_n2, L3_gnn_weight, L3_gnn_comp, L3_gnn_attn_w1, L3_gnn_attn_b1, L3_gnn_attn_w2, L3_gnn_attn_b2, L3_gnn_update), axis=-1)
    return x

_drawn_inputs = setup_inputs


def setup_inputs(seed=0):
    import zlib

    import numpy as np

    out = dict(_drawn_inputs(seed))
    spreads = {'L0_gnn_gamma': (1.0, 0.2),
     'L0_gnn_beta': (0.0, 0.1),
     'L1_gnn_b1': (0.0, 0.1),
     'L1_gnn_b2': (0.0, 0.1),
     'L3_gnn_attn_b1': (0.0, 2.0)}
    factors = {'edge_attr_32': 23.673,
     'edge_attr_32_n2': 8.0,
     'L0_gnn_b1': 5.406,
     'L3_gnn_attn_w1': 8.0,
     'L3_gnn_attn_w2': 8.0}
    for name, (base, spread) in spreads.items():
        noise = np.random.default_rng([zlib.crc32(name.encode()), seed]).standard_normal(out[name].shape)
        drawn = base * np.exp(spread * noise) if base else spread * noise
        out[name] = jnp.asarray(drawn.astype(out[name].dtype))
    for name, factor in factors.items():
        out[name] = (out[name] * factor).astype(out[name].dtype)
    return out
```

```python
from contextlib import ExitStack

import concourse.bass as bass
from concourse import mybir

F32 = mybir.dt.float32
I32 = mybir.dt.int32
ALU = mybir.AluOpType
ACT = mybir.ActivationFunctionType
AX = mybir.AxisListType

P = 128
G = 4
WIN = 3
RING = 8
UNROLL = 8
HEAD = 10
LAG_LO, LAG_HI = 1, 2
FAR = float(1 << 20)
LN_EPS = 1e-5


def build(nc, x, src, dst, ea1, ea2, etype, eps, W1, b1, W2, b2, gamma, beta,
          cW1, cb1, cW2, cb2, rel_w, comp, aw1, ab1, aw2, ab2, update, out):
    N, D = x.shape
    E = src.shape[0]
    R, B = comp.shape
    NG = -(-N // (P * G))
    NT = NG * G
    H2 = cW1.shape[1] // P
    EA = ea1.shape[1]
    assert D == P and NG == -(-E // (P * G)) and NG <= P and (NG - HEAD) % UNROLL == 0 and N == E
    FULL = N // P - (NG - 1) * G
    REST = N - (N // P) * P

    def table(name, width=D):
        return nc.dram_tensor(name, (NT * P, width), F32).ap()

    y1_t, yz_t, y2_t, x3_t, msg_t = (table(n) for n in ("y1_t", "yz_t", "y2_t", "x3_t", "msg_t"))
    dstp_t = nc.dram_tensor("dst_rows", (NT, P), F32).ap()

    def grouped(ap2, q, rows=P * G):
        return ap2[bass.ds(q * (P * G), rows), :].rearrange("(t p) d -> p t d", p=P)

    def sweep(step, depth):
        def at(s):
            step(s, s % UNROLL, lambda lag: 0 <= s - lag < NG)
        def run(eng):
            for s in range(HEAD):
                at(s)
            with eng.Fori(HEAD, NG - (UNROLL - 1), UNROLL) as s0:
                for u in range(UNROLL):
                    step(s0 + u, (HEAD + u) % UNROLL, lambda lag: True)
            for s in range(NG, NG + depth):
                at(s)
        return run

    def nth(q, slot, ring, inc=16):
        return (q - slot) * (inc // ring) + inc

    with ExitStack() as whole:
        def hold(name, shape, dt=F32):
            return whole.enter_context(nc.sbuf_tensor(name, shape, dt))

        landed = [whole.enter_context(nc.semaphore(f"gathered{i}")) for i in range(RING)]
        base = [16 * G, 16 * G * WIN] + [0] * (RING - 2)

        def count_gathers(ring, first=0):
            for q in range(NG):
                base[first + q % ring] += 16 * G

        def phase(ctx):
            held = []

            def sem(name):
                held.append(ctx.enter_context(nc.semaphore(name)))
                return held[-1]

            def clear():
                for s in held:
                    nc.gpsimd.sem_clear(s)
                nc.all_engine_barrier()

            def open_block():
                ctx.callback(clear)
                return ctx.enter_context(nc.Block())
            return sem, open_block

        ident = hold("ident", [P, P])
        iota_row = hold("iota_row", [P, P])
        dst_win = hold("dst_win", [P, NT * WIN])
        src_idx = hold("src_idx", [P, NT], I32)
        dst_idx = hold("dst_idx", [P, NT], I32)
        typ = hold("typ", [P, NT])
        win_at = hold("win_at", [1, NT], I32)
        cnt = hold("cnt", [P, NT])
        dinv = hold("dinv", [P, NT])
        sdeg = hold("sdeg", [P, NT])
        ones = hold("ones", [P, P])
        pidx = hold("pidx", [P, 1])
        ope = hold("ope", [P, 1])
        w1 = hold("w1", [P, D])
        w2 = hold("w2", [P, D])
        b1c = hold("b1c", [P, 1])
        b2r = hold("b2r", [1, D])
        gam = hold("gam", [P, D])
        bet = hold("bet", [P, D])
        cw1 = hold("cw1", [P, H2 * P])
        cw2 = hold("cw2", [P, H2, D])
        cb1c = hold("cb1c", [P, H2])
        cb2r = hold("cb2r", [P, D])
        upd = hold("upd", [P, D])

        with ExitStack() as ctx:
            sem, open_block = phase(ctx)

            def sb(name, shape, dt=F32):
                return ctx.enter_context(nc.sbuf_tensor(name, shape, dt))

            nat = [sb(n, [NG, G, P], I32) for n in ("nat_dst", "nat_src", "nat_typ")]
            natf = [sb(n, [NG, G, P]) for n in ("natf_dst", "natf_src", "natf_typ")]
            dst_col = sb("dst_col", [P, NT])
            src_col = sb("src_col", [P, NT])
            iota_i = sb("iota_i", [P, P], I32)
            pidx_i = sb("pidx_i", [P, 1], I32)
            jfirst_i = sb("jfirst_i", [P, G], I32)
            jfirst = sb("jfirst", [P, G])
            klo_i = sb("klo_i", [P, 1], I32)
            klo = sb("klo", [P, 1])
            klim = sb("klim", [P, 2])
            less = sb("less", [P, max(NT, P)])
            kh = sb("kh", [P, G])
            khi = sb("khi", [P, G], I32)
            rows = sb("rows", [P, G, P])
            under = sb("under", [P, G])
            k0 = sb("k0", [P, G])
            k0i = sb("k0i", [P, G], I32)
            wki = sb("wki", [P, G * WIN], I32)
            wrows = sb("wrows", [P, G * WIN, P])
            epsc = sb("epsc", [P, 1])
            tp = [ctx.enter_context(nc.psum_tensor(f"tp{i}", [P, G, P], F32)) for i in range(3)]
            wtp = [ctx.enter_context(nc.psum_tensor(f"wtp{i}", [P, G, P], F32)) for i in range(3)]
            piv = ctx.enter_context(nc.psum_tensor("piv", [P, 512], F32))

            weights_in = sem("weights_in")
            pads_set = sem("pads_set")
            lists_in = sem("lists_in")
            consts_i = sem("consts_i")
            dve_step = sem("dve_step")
            ident_ready, lists_f, cols_ready, kh_ready, k0_ready, wk_ready, wrel_ready = (
                sem(n) for n in ("ident_ready", "lists_f", "cols_ready", "kh_ready", "k0_ready",
                                 "wk_ready", "wrel_ready"))
            turned = sem("turned")
            dst_rows_out = sem("dst_rows_out")
            pivots = sem("pivots")
            rows_in, wrows_in = landed[0], landed[1]
            wturned = sem("wturned")
            win_in = sem("win_in")
            weights_all = 16 * (11 + H2)
            block = open_block()

            @block.sync
            def _(sp):
                sp.wait_ge(pads_set, 3)
                for a, t in zip((dst, src, etype), nat):
                    whole_rows = (E // P) - (G - 1) * NG
                    for c in range(G - 1):
                        sp.dma_start(t[:, c, :], a[c * NG * P:(c + 1) * NG * P].rearrange("(k e) -> k e", e=P)
                                     ).then_inc(lists_in, 16)
                    o = (G - 1) * NG * P
                    sp.dma_start(t[0:whole_rows, G - 1, :],
                                 a[o:o + whole_rows * P].rearrange("(k e) -> k e", e=P)).then_inc(lists_in, 16)
                    o += whole_rows * P
                    sp.dma_start(t[whole_rows:whole_rows + 1, G - 1, 0:REST],
                                 a[o:o + REST].rearrange("(k e) -> k e", k=1)).then_inc(lists_in, 16)

                def weight(to, of):
                    sp.dma_start(to, of).then_inc(weights_in, 16)

                col = lambda a: a.rearrange("(p c) -> p c", c=1)
                row = lambda a: a.rearrange("(p c) -> p c", p=1)
                spread = lambda a: row(a).to_broadcast([P, D])
                weight(w1[:], W1)
                weight(w2[:], W2)
                weight(b1c[:], col(b1))
                weight(b2r[:], row(b2))
                weight(gam[:], spread(gamma))
                weight(bet[:], spread(beta))
                weight(epsc[:], eps.to_broadcast([P, 1]))
                weight(cw1[:], cW1)
                weight(cw2[:], cW2.rearrange("(h p) d -> p h d", p=P))
                for h in range(H2):
                    weight(cb1c[:, h:h + 1], col(cb1[h * P:(h + 1) * P]))
                weight(cb2r[:], spread(cb2))
                weight(upd[:], update)
                sp.wait_ge(lists_f, 1)
                sp.dma_start(dstp_t.rearrange("(c k) e -> k c e", k=NG), natf[0][:]).then_inc(dst_rows_out, 16)
                sp.wait_ge(weights_in, weights_all)
                sp.wait_ge(k0_ready, 1)
                sp.dma_start(win_at[0:1, :], k0i[0:NG, :]).then_inc(win_in, 16)
                sp.wait_ge(win_in, 16)

            @block.gpsimd
            def _(pool):
                nc.gpsimd.iota(iota_i[:], pattern=[[1, P]], base=0, channel_multiplier=0).then_inc(consts_i, 1)
                nc.gpsimd.iota(pidx_i[:], pattern=[[0, 1]], base=0, channel_multiplier=1).then_inc(consts_i, 1)
                nc.gpsimd.iota(jfirst_i[:], pattern=[[P, G]], base=0, channel_multiplier=P * G).then_inc(consts_i, 1)
                nc.gpsimd.iota(klo_i[:], pattern=[[0, 1]], base=0, channel_multiplier=G).then_inc(consts_i, 1)
                nc.gpsimd.memset(nat[0][:], int(FAR)).then_inc(pads_set, 1)
                nc.gpsimd.memset(nat[1][:], 0).then_inc(pads_set, 1)
                nc.gpsimd.memset(nat[2][:], 0).then_inc(pads_set, 1)
                pool.wait_ge(dst_rows_out, 16)
                pool.wait_ge(kh_ready, 1)
                for c in range(G):
                    nc.gpsimd.indirect_dma_start(
                        out=rows[0:NG, c, :], out_offset=None, in_=dstp_t[:, :],
                        in_offset=bass.IndirectOffsetOnAxis(ap=khi[0:NG, c:c + 1], axis=0),
                        bounds_check=NT - 1, oob_is_err=False).then_inc(rows_in, 16)
                pool.wait_ge(wk_ready, 1)
                for c in range(G * WIN):
                    nc.gpsimd.indirect_dma_start(
                        out=wrows[0:NG, c, :], out_offset=None, in_=dstp_t[:, :],
                        in_offset=bass.IndirectOffsetOnAxis(ap=wki[0:NG, c:c + 1], axis=0),
                        bounds_check=NT - 1, oob_is_err=False).then_inc(wrows_in, 16)
                pool.wait_ge(wrows_in, 16 * G * WIN)

            @block.vector
            def _(dve):
                n = [0]

                def then(ins, *ready):
                    n[0] += 1
                    ins.then_inc(dve_step, 1)
                    dve.wait_ge(dve_step, n[0])
                    for s in ready:
                        dve.sem_inc(s, 1)

                dve.wait_ge(consts_i, 4)
                then(nc.vector.tensor_copy(iota_row[:], iota_i[:]))
                then(nc.vector.tensor_copy(pidx[:], pidx_i[:]))
                then(nc.vector.tensor_scalar(ident[:], iota_row[:], pidx[:, 0:1], None, ALU.is_equal), ident_ready)
                then(nc.vector.tensor_copy(jfirst[:], jfirst_i[:]))
                then(nc.vector.tensor_copy(klo[:], klo_i[:]))
                then(nc.vector.memset(ones[:], 1.0))
                dve.wait_ge(lists_in, 16 * 3 * (G + 1))
                for i in range(3):
                    then(nc.vector.tensor_copy(natf[i][:], nat[i][:]), *([lists_f] if i == 2 else []))
                dve.wait_ge(turned, 3)
                for to, of in ((dst_col, tp[0]), (src_col, tp[1]), (typ, tp[2])):
                    then(nc.vector.tensor_copy(to[:].rearrange("e (c k) -> e c k", c=G), of[:, :, 0:NG]))
                then(nc.vector.tensor_copy(src_idx[:], src_col[:]), cols_ready)
                then(nc.vector.tensor_scalar(dst_idx[:], dst_col[:], float(N - 1), None, ALU.min))
                dve.wait_ge(pivots, 1)
                for c in range(G):
                    then(nc.vector.tensor_scalar(less[:, 0:NT], piv[:, 0:NT], jfirst[:, c:c + 1], None, ALU.is_lt))
                    then(nc.vector.tensor_reduce(kh[:, c:c + 1], less[:, 0:NT], AX.X, ALU.add))
                then(nc.vector.tensor_scalar(kh[:], kh[:], -1.0, 0.0, ALU.add, ALU.max))
                then(nc.vector.tensor_copy(khi[:], kh[:]), kh_ready)
                then(nc.vector.memset(under[:], 0.0))
                dve.wait_ge(rows_in, 16 * G)
                for c in range(G):
                    then(nc.vector.tensor_scalar(less[0:NG, 0:P], rows[0:NG, c, :], jfirst[0:NG, c:c + 1], None,
                                                 ALU.is_lt))
                    then(nc.vector.tensor_reduce(under[0:NG, c:c + 1], less[0:NG, 0:P], AX.X, ALU.add))
                then(nc.vector.scalar_tensor_tensor(out=k0[:], in0=under[:], scalar=float(P), in1=kh[:],
                                                    op0=ALU.is_ge, op1=ALU.add))
                then(nc.vector.tensor_scalar(klim[:, 0:1], klo[:], -float(G * LAG_LO), 0.0, ALU.add, ALU.max))
                then(nc.vector.tensor_scalar(klim[:, 1:2], klo[:], float(G * (LAG_HI + 1) - WIN),
                                             float(NT - WIN), ALU.add, ALU.min))
                then(nc.vector.tensor_scalar(k0[:], k0[:], klim[:, 0:1], klim[:, 1:2], ALU.max, ALU.min))
                then(nc.vector.tensor_copy(k0i[:], k0[:]), k0_ready)
                for c in range(G):
                    for i in range(WIN):
                        then(nc.vector.tensor_scalar(wki[:, c * WIN + i:c * WIN + i + 1], k0[:, c:c + 1],
                                                     float(i), None, ALU.add))
                dve.sem_inc(wk_ready, 1)
                dve.wait_ge(wrows_in, 16 * G * WIN)
                for c in range(G):
                    then(nc.vector.tensor_scalar(wrows[0:NG, c * WIN:(c + 1) * WIN, :],
                                                 wrows[0:NG, c * WIN:(c + 1) * WIN, :],
                                                 jfirst[0:NG, c:c + 1], None, ALU.subtract))
                dve.sem_inc(wrel_ready, 1)
                dve.wait_ge(wturned, 1)
                for c in range(G * WIN):
                    nc.vector.tensor_copy(dst_win[:, c:NT * WIN:G * WIN], wtp[c // G][:, c % G, 0:NG])
                dve.wait_ge(weights_in, weights_all)
                then(nc.vector.tensor_scalar(ope[:], epsc[:], 1.0, None, ALU.add))

            @block.tensor
            def _(pe):
                pe.wait_ge(lists_f, 1)
                pe.wait_ge(ident_ready, 1)
                for i in range(3):
                    for c in range(G):
                        ins = nc.tensor.transpose(tp[i][:, c, 0:NG], natf[i][:, c, :], ident[0:NG, 0:NG])
                    ins.then_inc(turned, 1)
                pe.wait_ge(cols_ready, 1)
                nc.tensor.matmul(piv[:, 0:NT], ones[0:1, :], dst_col[0:1, :], start=True,
                                 stop=True).then_inc(pivots, 1)
                pe.wait_ge(wrel_ready, 1)
                for c in range(G * WIN):
                    ins = nc.tensor.transpose(wtp[c // G][:, c % G, 0:NG], wrows[0:NG, c, :], ident[0:NG, 0:NG])
                ins.then_inc(wturned, 1)

        def idx_gather(pool, q, m, idx_ring, idx_all, tabs, idx_in, slot_sem, turn):
            nc.gpsimd.tensor_copy(idx_ring[:, m * G:(m + 1) * G], idx_all[:, bass.ds(q * G, G)]).then_inc(idx_in, 1)
            pool.wait_ge(idx_in, q + 1)
            pool.sem_inc(turn, 1)
            for t in range(G):
                k = m * G + t
                nc.gpsimd.indirect_dma_start(
                    out=tabs[0][:, k, 0:D], out_offset=None, in_=tabs[1][:, :],
                    in_offset=bass.IndirectOffsetOnAxis(ap=idx_ring[:, k:k + 1], axis=0),
                    bounds_check=N - 1, oob_is_err=False).then_inc(slot_sem, 16)

        def window_sums(q, sel, ring, sums, done):
            regs = [nc.tensor.value_load(win_at[0:1, bass.ds(q * G + t, 1)], min_val=0, max_val=NT - WIN)
                    for t in range(G)]
            for t in range(G):
                for i in range(WIN):
                    ins = nc.tensor.matmul(sums[t], sel[:, t * WIN + i, :],
                                           ring[:, bass.ds((regs[t] + i) % (RING * G), 1), :].rearrange("p a d -> p (a d)"),
                                           start=(i == 0), stop=(i == WIN - 1))
            ins.then_inc(done, 1)

        def build_sel(q, sel, done):
            nc.vector.tensor_tensor(
                sel[:], dst_win[:, bass.ds(q * (G * WIN), G * WIN)].unsqueeze(2).to_broadcast([P, G * WIN, P]),
                iota_row[:].unsqueeze(1).to_broadcast([P, G * WIN, P]), ALU.is_equal).then_inc(done, 1)

        def row_stats(dve, q, rows, st, mv, rvar, step, passed):
            for t in range(G):
                nc.vector.bn_stats(st[:, t, :], rows[:, t, :]).then_inc(step, 1)
            dve.wait_ge(step, q * 10 + 4)
            dve.sem_inc(passed, 1)
            for t in range(G):
                nc.vector.bn_aggr(mv[:, t, :], st[:, t, :]).then_inc(step, 1)
            dve.wait_ge(step, q * 10 + 8)
            nc.vector.tensor_scalar(rvar[:], mv[:, :, 1], LN_EPS, None, ALU.add).then_inc(step, 1)
            dve.wait_ge(step, q * 10 + 9)
            nc.vector.reciprocal(rvar[:], rvar[:]).then_inc(step, 1)

        def tiles(a):
            return a[:].unsqueeze(1).to_broadcast([P, G, D])

        def flat(a):
            return a.rearrange("p t d -> p (t d)")

        def gin_layer():
          W = D + 1
          with ExitStack() as ctx:
            sem, open_block = phase(ctx)

            def sb(name, shape, dt=F32):
                return ctx.enter_context(nc.sbuf_tensor("gin_" + name, shape, dt))

            def ps(name, shape):
                return ctx.enter_context(nc.psum_tensor("gin_" + name, shape, F32))

            ring = sb("ring", [P, RING * G, W])
            idx = sb("idx", [P, RING * G], I32)
            xin = sb("xin", [P, RING, G, D])
            sel = [sb(f"sel{i}", [P, G * WIN, P]) for i in range(2)]
            z = [sb(f"z{i}", [P, G, D]) for i in range(2)]
            zT = [sb(f"zT{i}", [P, G * P]) for i in range(2)]
            hT = [sb(f"hT{i}", [P, G * P]) for i in range(2)]
            r = [sb(f"r{i}", [P, G, D]) for i in range(2)]
            xn = [sb(f"xn{i}", [P, G, D]) for i in range(2)]
            u = [sb(f"u{i}", [P, G, D]) for i in range(2)]
            yo = [sb(f"yo{i}", [P, G, D]) for i in range(2)]
            small = lambda n, k=1: [sb(f"{n}{i}", [P, G * k]) for i in range(2)]
            stA, stB = ([sb(f"st{n}{i}", [P, G, 6]) for i in range(2)] for n in "AB")
            mvA, mvB = ([sb(f"mv{n}{i}", [P, G, 2]) for i in range(2)] for n in "AB")
            rvA, rvB, rsA, rsB, nmA, nmB, rdB = (small(n) for n in ("rvA", "rvB", "rsA", "rsB", "nmA", "nmB", "rdB"))
            deg, rdeg = small("deg"), small("rdeg")
            sums = [ps(f"sums{i}", [P, 2, 512]) for i in range(2)]
            zTp, hTp, rp = ps("zTp", [P, G * P]), ps("hTp", [P, G * P]), ps("rp", [P, G, D])
            (ring_ones, idx_in, turn, sel_ready, sums_ready, z_steps, zT_turned, zT_ready, h_done, hT_ready,
             r_done, r_ready, statA, rsA_ready, nmA_ready, xn_ready, mix, statB, rsB_ready, nmB_ready, y_ready,
             deg_ready, dinv_ready, x_tail) = (sem("gin_" + n) for n in (
                "ring_ones", "idx_in", "turn", "sel_ready", "sums_ready", "z_steps", "zT_turned", "zT_ready",
                "h_done", "hT_ready", "r_done", "r_ready", "statA", "rsA_ready", "nmA_ready", "xn_ready", "mix",
                "statB", "rsB_ready", "nmB_ready", "y_ready", "deg_ready", "dinv_ready", "x_tail"))
            gathered = landed
            x_in = [sem(f"gin_x_in{i}") for i in range(RING)]
            y_out = [sem(f"gin_y_out{i}") for i in range(2)]
            passed, act_passed = sem("gin_dve_passed"), sem("gin_act_passed")
            block = open_block()
            LOAD, SUM, TURN, HID, RES, NORM_A, MIX, NORM_B, STORE = 1, 2, 3, 4, 5, 7, 8, 9, 10

            @block.sync
            def _(sp):
                def step(s, m, on):
                    if on(LOAD):
                        q, slot = s - LOAD, (m - LOAD) % RING
                        if on(LOAD + RING):
                            sp.wait_ge(mix, 3 * (q - RING) + 3)
                        if isinstance(q, int) and q == NG - 1:
                            sp.dma_start(xin[:, slot, 0:FULL, :], grouped(x, q, FULL * P)).then_inc(x_in[slot], 16)
                            sp.dma_start(xin[0:REST, slot, FULL, :], x[(q * G + FULL) * P:N, :]).then_inc(x_tail, 16)
                        else:
                            sp.dma_start(xin[:, slot, :, :], grouped(x, q)).then_inc(x_in[slot], 16)
                    if on(STORE):
                        q, b = s - STORE, (m - STORE) % 2
                        sp.wait_ge(y_ready, G * (q + 1))
                        sp.dma_start(grouped(y1_t, q), yo[b][:]).then_inc(y_out[b], 16)
                sweep(step, STORE)(sp)
                for b in range(2):
                    sp.wait_ge(y_out[b], 16 * NG // 2)

            @block.gpsimd
            def _(pool):
                nc.gpsimd.memset(ring[:, :, D:W], 1.0).then_inc(ring_ones, 1)

                def step(s, m, on):
                    if on(0):
                        if on(RING):
                            pool.wait_ge(sums_ready, s - RING + LAG_LO + 1)
                        idx_gather(pool, s, m, idx, src_idx, (ring, x), idx_in, gathered[m], turn)
                sweep(step, 0)(pool)

            @block.tensor
            def _(pe):
                pe.wait_ge(ring_ones, 1)

                def step(s, m, on):
                    if on(SUM):
                        q, b = s - SUM, m % 2
                        if on(0):
                            pe.wait_ge(gathered[m], base[m] + nth(s, m, RING, 16 * G))
                        pe.wait_ge(sel_ready, q + 1)
                        if on(SUM + 2):
                            pe.wait_ge(z_steps, 3 * (q - 1))
                        window_sums(q, sel[b], ring, [sums[b][:, t // 2, t % 2 * W:(t % 2 + 1) * W] for t in range(G)],
                                    sums_ready)
                    if on(TURN):
                        q, b = s - TURN, (m - TURN) % 2
                        pe.wait_ge(z_steps, 3 * q + 2)
                        if on(TURN + 1):
                            pe.wait_ge(zT_ready, q)
                        for t in range(G):
                            ins = nc.tensor.transpose(zTp[:, t * P:(t + 1) * P], z[b][:, t, :], ident[:])
                        ins.then_inc(zT_turned, 1)
                    if on(HID):
                        q, b = s - HID, (m - HID) % 2
                        pe.wait_ge(zT_ready, q + 1)
                        if on(HID + 1):
                            pe.wait_ge(hT_ready, q)
                        nc.tensor.matmul(hTp[:], w1[:], zT[b][:], start=True, stop=True).then_inc(h_done, 1)
                    if on(RES):
                        q, b = s - RES, (m - RES) % 2
                        pe.wait_ge(hT_ready, q + 1)
                        if on(RES + 1):
                            pe.wait_ge(r_ready, q)
                        for t in range(G):
                            nc.tensor.matmul(rp[:, t, :], ones[0:1, :], b2r[:], start=True, stop=False)
                            ins = nc.tensor.matmul(rp[:, t, :], hT[b][:, t * P:(t + 1) * P], w2[:], start=False,
                                                   stop=True)
                        ins.then_inc(r_done, 1)
                sweep(step, RES)(pe)

            @block.scalar
            def _(act):
                def step(s, m, on):
                    if on(NORM_A):
                        q, b = s - NORM_A, (m - NORM_A) % 2
                        act.wait_ge(nmA_ready, q + 1)
                        if on(NORM_A + 2):
                            act.wait_ge(mix, 3 * (q - 2) + 1)
                        for t in range(G):
                            nc.scalar.activation(xn[b][:, t, :], r[b][:, t, :], ACT.Identity, bias=nmA[b][:, t:t + 1],
                                                 scale=rsA[b][:, t:t + 1]).then_inc(xn_ready, 1)
                    if on(NORM_B):
                        q, b = s - NORM_B, (m - NORM_B) % 2
                        act.wait_ge(nmB_ready, 2 * (q + 1))
                        if on(NORM_B + 2):
                            act.wait_ge(y_out[b], nth(q - 2, b, 2))
                        for t in range(G):
                            nc.scalar.activation(yo[b][:, t, :], u[b][:, t, :], ACT.Identity, bias=nmB[b][:, t:t + 1],
                                                 scale=rdB[b][:, t:t + 1]).then_inc(y_ready, 1)
                    if on(TURN):
                        q, b = s - TURN, (m - TURN) % 2
                        act.wait_ge(zT_turned, q + 1)
                        if on(TURN + 2):
                            act.wait_ge(h_done, q - 1)
                        nc.scalar.copy(zT[b][:], zTp[:]).then_inc(zT_ready, 1)
                        act.wait_ge(deg_ready, 2 * q + 2)
                        act.sem_inc(act_passed, 1)
                        nc.scalar.activation(dinv[:, bass.ds(q * G, G)], rdeg[b][:], ACT.Sqrt).then_inc(dinv_ready, 1)
                        nc.scalar.activation(sdeg[:, bass.ds(q * G, G)], deg[b][:],
                                             ACT.Sqrt).then_inc(dinv_ready, 1)
                    if on(HID):
                        q, b = s - HID, (m - HID) % 2
                        act.wait_ge(h_done, q + 1)
                        if on(HID + 2):
                            act.wait_ge(r_done, q - 1)
                        nc.scalar.activation(hT[b][:], hTp[:], ACT.Relu, bias=b1c[:, 0:1]).then_inc(hT_ready, 1)
                    if on(NORM_A - 1):
                        q, b = s - NORM_A + 1, (m - NORM_A + 1) % 2
                        act.wait_ge(statA, 10 * (q + 1))
                        nc.scalar.activation(rsA[b][:], rvA[b][:], ACT.Sqrt).then_inc(rsA_ready, 1)
                    if on(MIX):
                        q, b = s - MIX, (m - MIX) % 2
                        act.wait_ge(statB, 10 * (q + 1))
                        nc.scalar.activation(rsB[b][:], rvB[b][:], ACT.Sqrt).then_inc(rsB_ready, 1)
                sweep(step, NORM_B)(act)

            @block.vector
            def _(dve):
                def step(s, m, on):
                    if on(NORM_A):
                        q, b = s - NORM_A, (m - NORM_A) % 2
                        dve.wait_ge(rsA_ready, q + 1)
                        nc.vector.scalar_tensor_tensor(out=nmA[b][:], in0=mvA[b][:, :, 0], scalar=-1.0, in1=rsA[b][:],
                                                       op0=ALU.mult, op1=ALU.mult).then_inc(nmA_ready, 1)
                    if on(NORM_B):
                        q, b = s - NORM_B, (m - NORM_B) % 2
                        dve.wait_ge(rsB_ready, q + 1)
                        dve.wait_ge(dinv_ready, 2 * (q + 1))
                        if on(NORM_B + 2):
                            dve.wait_ge(y_ready, G * (q - 1))
                        nc.vector.tensor_tensor(rdB[b][:], rsB[b][:], dinv[:, bass.ds(q * G, G)],
                                                ALU.mult).then_inc(nmB_ready, 1)
                        dve.wait_ge(nmB_ready, 2 * q + 1)
                        nc.vector.scalar_tensor_tensor(out=nmB[b][:], in0=mvB[b][:, :, 0], scalar=-1.0, in1=rdB[b][:],
                                                       op0=ALU.mult, op1=ALU.mult).then_inc(nmB_ready, 1)
                    if on(SUM):
                        q, b = s - SUM, m % 2
                        if on(SUM + 2):
                            dve.wait_ge(sums_ready, q - 1)
                        build_sel(q, sel[b], sel_ready)
                    if on(TURN):
                        q, b, slot = s - TURN, (m - TURN) % 2, (m - TURN) % RING
                        dve.wait_ge(sums_ready, q + 1)
                        dve.wait_ge(x_in[slot], nth(q, slot, RING))
                        if isinstance(q, int) and q == NG - 1:
                            dve.wait_ge(x_tail, 16)
                        if on(TURN + 2):
                            dve.wait_ge(zT_turned, q - 1)
                            dve.wait_ge(dinv_ready, 2 * (q - 1))
                        pair = lambda h: sums[b][:, h, 0:2 * W].rearrange("p (t w) -> p t w", w=W)
                        for h in range(2):
                            nc.vector.scalar_tensor_tensor(
                                out=z[b][:, 2 * h:2 * h + 2, :], in0=xin[:, slot, 2 * h:2 * h + 2, :],
                                scalar=ope[:, 0:1], in1=pair(h)[:, :, 0:D], op0=ALU.mult,
                                op1=ALU.add).then_inc(z_steps, 1)
                        nc.vector.tensor_copy(
                            cnt[:, bass.ds(q * G, G)].rearrange("p (h t) -> p h t", t=2),
                            sums[b][:, :, 0:2 * W].rearrange("p h (t w) -> p h t w", w=W)[:, :, :, D]).then_inc(z_steps, 1)
                        dve.wait_ge(z_steps, 3 * q + 3)
                        nc.vector.tensor_scalar(deg[b][:], cnt[:, bass.ds(q * G, G)], 1.0, None,
                                                ALU.add).then_inc(deg_ready, 1)
                        dve.wait_ge(deg_ready, 2 * q + 1)
                        nc.vector.reciprocal(rdeg[b][:], deg[b][:]).then_inc(deg_ready, 1)
                    if on(NORM_A - 1):
                        q, b, slot = s - NORM_A + 1, (m - NORM_A + 1) % 2, (m - NORM_A + 1) % RING
                        dve.wait_ge(r_done, q + 1)
                        if on(NORM_A + 1):
                            dve.wait_ge(xn_ready, G * (q - 1))
                        nc.vector.tensor_tensor(r[b][:], rp[:], xin[:, slot, :, :], ALU.add).then_inc(r_ready, 1)
                        dve.wait_ge(r_ready, q + 1)
                        row_stats(dve, q, r[b], stA[b], mvA[b], rvA[b], statA, passed)
                    if on(MIX):
                        q, b, slot = s - MIX, (m - MIX) % 2, (m - MIX) % RING
                        dve.wait_ge(xn_ready, G * (q + 1))
                        if on(MIX + 2):
                            dve.wait_ge(y_ready, G * (q - 1))
                        nc.vector.tensor_tensor(u[b][:], xn[b][:], tiles(gam), ALU.mult).then_inc(mix, 1)
                        dve.wait_ge(mix, 3 * q + 1)
                        nc.vector.tensor_tensor(u[b][:], u[b][:], tiles(bet), ALU.add).then_inc(mix, 1)
                        dve.wait_ge(mix, 3 * q + 2)
                        nc.vector.scalar_tensor_tensor(out=u[b][:], in0=u[b][:], scalar=0.0, in1=xin[:, slot, :, :],
                                                       op0=ALU.max, op1=ALU.add).then_inc(mix, 1)
                        dve.wait_ge(mix, 3 * q + 3)
                        row_stats(dve, q, u[b], stB[b], mvB[b], rvB[b], statB, passed)
                sweep(step, NORM_B)(dve)

        gin_layer()
        count_gathers(RING)
        def gcn_hidden():
          with ExitStack() as ctx:
            sem, open_block = phase(ctx)

            def sb(name, shape, dt=F32):
                return ctx.enter_context(nc.sbuf_tensor("gcn_" + name, shape, dt))

            def ps(name, shape):
                return ctx.enter_context(nc.psum_tensor("gcn_" + name, shape, F32))

            ring = sb("ring", [P, RING * G, D])
            idx = sb("idx", [P, RING * G], I32)
            yin = sb("yin", [P, RING, G, D])
            sel = [sb(f"sel{i}", [P, G * WIN, P]) for i in range(2)]
            own = [sb(f"own{i}", [P, G, D]) for i in range(2)]
            a = [sb(f"a{i}", [P, G, D]) for i in range(2)]
            aT = [sb(f"aT{i}", [P, G * P]) for i in range(2)]
            hT = [sb(f"hT{i}", [P, H2, G * P]) for i in range(2)]
            yo = [sb(f"yo{i}", [P, G, D]) for i in range(2)]
            sums = [ps(f"sums{i}", [P, G, D]) for i in range(2)]
            aTp, hTp, zp = ps("aTp", [P, G * P]), ps("hTp", [P, H2, G * P]), ps("zp", [P, G, D])
            (idx_in, turn, sel_ready, sums_ready, own_ready, a_ready, aT_turned, aT_ready, h_done, hT_ready, z_done,
             y_ready) = (sem("gcn_" + n) for n in (
                "idx_in", "turn", "sel_ready", "sums_ready", "own_ready", "a_ready", "aT_turned", "aT_ready",
                "h_done", "hT_ready", "z_done", "y_ready"))
            gathered = landed
            y_in = [sem(f"gcn_y_in{i}") for i in range(RING)]
            y_out = [sem(f"gcn_y_out{i}") for i in range(2)]
            act_passed = sem("gcn_act_passed")
            block = open_block()
            LOAD, SUM, TURN, HID, OUT, STORE = 1, 2, 3, 4, 5, 6

            @block.sync
            def _(sp):
                def step(s, m, on):
                    if on(LOAD):
                        q, slot = s - LOAD, (m - LOAD) % RING
                        if on(LOAD + RING):
                            sp.wait_ge(own_ready, G * (q - RING + 1))
                        sp.dma_start(yin[:, slot, :, :], grouped(y1_t, q)).then_inc(y_in[slot], 16)
                    if on(STORE):
                        q, b = s - STORE, (m - STORE) % 2
                        sp.wait_ge(y_ready, G * (q + 1))
                        sp.dma_start(grouped(yz_t, q), yo[b][:]).then_inc(y_out[b], 16)
                sweep(step, STORE)(sp)
                for b in range(2):
                    sp.wait_ge(y_out[b], 16 * NG // 2)

            @block.gpsimd
            def _(pool):
                def step(s, m, on):
                    if on(0):
                        if on(RING):
                            pool.wait_ge(sums_ready, s - RING + LAG_LO + 1)
                        idx_gather(pool, s, m, idx, src_idx, (ring, y1_t), idx_in, gathered[m], turn)
                sweep(step, 0)(pool)

            @block.tensor
            def _(pe):
                def step(s, m, on):
                    if on(SUM):
                        q, b = s - SUM, m % 2
                        if on(0):
                            pe.wait_ge(gathered[m], base[m] + nth(s, m, RING, 16 * G))
                        pe.wait_ge(sel_ready, q + 1)
                        if on(SUM + 2):
                            pe.wait_ge(a_ready, G * (q - 1))
                        window_sums(q, sel[b], ring, [sums[b][:, t, :] for t in range(G)], sums_ready)
                    if on(TURN):
                        q, b = s - TURN, (m - TURN) % 2
                        pe.wait_ge(a_ready, G * (q + 1))
                        if on(TURN + 1):
                            pe.wait_ge(aT_ready, q)
                        for t in range(G):
                            ins = nc.tensor.transpose(aTp[:, t * P:(t + 1) * P], a[b][:, t, :], ident[:])
                        ins.then_inc(aT_turned, 1)
                    if on(HID):
                        q, b = s - HID, (m - HID) % 2
                        pe.wait_ge(aT_ready, q + 1)
                        if on(HID + 1):
                            pe.wait_ge(hT_ready, H2 * q)
                        for h in range(H2):
                            nc.tensor.matmul(hTp[:, h, :], cw1[:, h * P:(h + 1) * P], aT[b][:], start=True,
                                             stop=True).then_inc(h_done, 1)
                    if on(OUT):
                        q, b = s - OUT, (m - OUT) % 2
                        pe.wait_ge(hT_ready, H2 * (q + 1))
                        if on(OUT + 1):
                            pe.wait_ge(y_ready, G * q)
                        for t in range(G):
                            for h in range(H2):
                                ins = nc.tensor.matmul(zp[:, t, :], hT[b][:, h, t * P:(t + 1) * P], cw2[:, h, :],
                                                       start=(h == 0), stop=(h == H2 - 1))
                        ins.then_inc(z_done, 1)
                sweep(step, OUT)(pe)

            @block.scalar
            def _(act):
                def step(s, m, on):
                    if on(SUM):
                        q, b, slot = s - SUM, m % 2, (m - SUM) % RING
                        act.wait_ge(y_in[slot], nth(q, slot, RING))
                        if on(SUM + 2):
                            act.wait_ge(a_ready, G * (q - 1))
                        act.sem_inc(act_passed, 1)
                        for t in range(G):
                            nc.scalar.activation(own[b][:, t, :], yin[:, slot, t, :], ACT.Copy,
                                                 scale=dinv[:, bass.ds(q * G + t, 1)]).then_inc(own_ready, 1)
                    if on(TURN):
                        q, b = s - TURN, (m - TURN) % 2
                        act.wait_ge(aT_turned, q + 1)
                        if on(TURN + 2):
                            act.wait_ge(h_done, H2 * (q - 1))
                        nc.scalar.copy(aT[b][:], aTp[:]).then_inc(aT_ready, 1)
                    if on(HID):
                        q, b = s - HID, (m - HID) % 2
                        if on(HID + 2):
                            act.wait_ge(z_done, q - 1)
                        for h in range(H2):
                            act.wait_ge(h_done, H2 * q + h + 1)
                            nc.scalar.activation(hT[b][:, h, :], hTp[:, h, :], ACT.Relu,
                                                 bias=cb1c[:, h:h + 1]).then_inc(hT_ready, 1)
                    if on(OUT):
                        q, b = s - OUT, (m - OUT) % 2
                        act.wait_ge(z_done, q + 1)
                        if on(OUT + 2):
                            act.wait_ge(y_out[b], nth(q - 2, b, 2))
                        act.sem_inc(act_passed, 1)
                        for t in range(G):
                            nc.scalar.activation(yo[b][:, t, :], zp[:, t, :], ACT.Copy,
                                                 scale=dinv[:, bass.ds(q * G + t, 1)]).then_inc(y_ready, 1)
                sweep(step, OUT)(act)

            @block.vector
            def _(dve):
                def step(s, m, on):
                    if on(SUM):
                        q, b = s - SUM, m % 2
                        if on(SUM + 2):
                            dve.wait_ge(sums_ready, q - 1)
                        build_sel(q, sel[b], sel_ready)
                    if on(TURN):
                        q, b = s - TURN, (m - TURN) % 2
                        dve.wait_ge(sums_ready, q + 1)
                        dve.wait_ge(own_ready, G * (q + 1))
                        if on(TURN + 2):
                            dve.wait_ge(aT_turned, q - 1)
                        for t in range(G):
                            nc.vector.scalar_tensor_tensor(
                                out=a[b][:, t, :], in0=sums[b][:, t, :], scalar=dinv[:, bass.ds(q * G + t, 1)],
                                in1=own[b][:, t, :], op0=ALU.mult, op1=ALU.add).then_inc(a_ready, 1)
                sweep(step, TURN)(dve)

        gcn_hidden()
        count_gathers(RING)

        def propagate(pre, from_t, res_t, to_t, keep):
          bias_form = keep is None
          with ExitStack() as ctx:
            sem, open_block = phase(ctx)

            def sb(name, shape, dt=F32):
                return ctx.enter_context(nc.sbuf_tensor(pre + name, shape, dt))

            def ps(name, shape):
                return ctx.enter_context(nc.psum_tensor(pre + name, shape, F32))

            ring = sb("ring", [P, RING * G, D])
            idx = sb("idx", [P, RING * G], I32)
            yin = sb("yin", [P, RING, G, D])
            rin = sb("rin", [P, RING, G, D]) if bias_form else yin
            sel = [sb(f"sel{i}", [P, G * WIN, P]) for i in range(2)]
            a = [sb(f"a{i}", [P, G, D]) for i in range(2)]
            v = [sb(f"v{i}", [P, G, D]) for i in range(2)]
            xr = sb("xr", [P, 4, G, D])
            u = [sb(f"u{i}", [P, G, D]) for i in range(2)]
            yo = [sb(f"yo{i}", [P, G, D]) for i in range(2)]
            small = lambda n: [sb(f"{n}{i}", [P, G]) for i in range(2)]
            st = [sb(f"st{i}", [P, G, 6]) for i in range(2)]
            mv = [sb(f"mv{i}", [P, G, 2]) for i in range(2)]
            rv, rs, rd, nm = small("rv"), small("rs"), small("rd"), small("nm")
            dscale = sb("dscale", [P, NT])
            rscale = sb("rscale", [P, NT])
            copies = 1.0 if bias_form else 2.0
            sums = [ps(f"sums{i}", [P, G, D]) for i in range(2)]
            (idx_in, turn, sel_ready, sums_ready, xr_ready, a_ready, v_ready, mix, stat, rs_ready, nm_ready, y_ready,
             scale_ready) = (sem(pre + n) for n in (
                "idx_in", "turn", "sel_ready", "sums_ready", "xr_ready", "a_ready", "v_ready", "mix", "stat",
                "rs_ready", "nm_ready", "y_ready", "scale_ready"))
            gathered = landed
            y_in = [sem(f"{pre}y_in{i}") for i in range(RING)]
            r_in = [sem(f"{pre}r_in{i}") for i in range(RING)] if bias_form else y_in
            y_out = [sem(f"{pre}y_out{i}") for i in range(2)]
            passed, act_passed = sem(pre + "dve_passed"), sem(pre + "act_passed")
            block = open_block()
            LOAD, SUM, ADD, MIX, NORM, STORE = 1, 2, 3, 4, 6, 7

            @block.sync
            def _(sp):
                def step(s, m, on):
                    if on(LOAD):
                        q, slot = s - LOAD, (m - LOAD) % RING
                        if on(LOAD + RING):
                            sp.wait_ge(xr_ready, G * (q - RING + 1))
                            sp.wait_ge(a_ready, q - RING + 1)
                        sp.dma_start(yin[:, slot, :, :], grouped(from_t, q)).then_inc(y_in[slot], 16)
                        if bias_form:
                            sp.dma_start(rin[:, slot, :, :], grouped(res_t, q)).then_inc(r_in[slot], 16)
                    if on(STORE):
                        q, b = s - STORE, (m - STORE) % 2
                        sp.wait_ge(y_ready, G * (q + 1))
                        sp.dma_start(grouped(to_t, q), yo[b][:]).then_inc(y_out[b], 16)
                sweep(step, STORE)(sp)
                for b in range(2):
                    sp.wait_ge(y_out[b], 16 * NG // 2)

            @block.gpsimd
            def _(pool):
                def step(s, m, on):
                    if on(0):
                        if on(RING):
                            pool.wait_ge(sums_ready, s - RING + LAG_LO + 1)
                        idx_gather(pool, s, m, idx, src_idx, (ring, from_t), idx_in, gathered[m], turn)
                sweep(step, 0)(pool)

            @block.tensor
            def _(pe):
                def step(s, m, on):
                    if on(SUM):
                        q, b = s - SUM, m % 2
                        if on(0):
                            pe.wait_ge(gathered[m], base[m] + nth(s, m, RING, 16 * G))
                        pe.wait_ge(sel_ready, q + 1)
                        if on(SUM + 2):
                            pe.wait_ge(a_ready, q - 1)
                        window_sums(q, sel[b], ring, [sums[b][:, t, :] for t in range(G)], sums_ready)
                sweep(step, SUM)(pe)

            @block.scalar
            def _(act):
                act.wait_ge(scale_ready, 2)

                def step(s, m, on):
                    if on(NORM):
                        q, b = s - NORM, (m - NORM) % 2
                        act.wait_ge(nm_ready, 2 * (q + 1))
                        if on(NORM + 2):
                            act.wait_ge(y_out[b], nth(q - 2, b, 2))
                        for t in range(G):
                            nc.scalar.activation(yo[b][:, t, :], u[b][:, t, :], ACT.Identity, bias=nm[b][:, t:t + 1],
                                                 scale=rd[b][:, t:t + 1]).then_inc(y_ready, 1)
                    if on(SUM):
                        q, slot = s - SUM, (m - SUM) % RING
                        act.wait_ge(r_in[slot], nth(q, slot, RING))
                        if on(SUM + 4):
                            act.wait_ge(mix, 2 * (q - 3))
                        act.sem_inc(act_passed, 1)
                        for t in range(G):
                            nc.scalar.activation(xr[:, slot % 4, t, :], rin[:, slot, t, :], ACT.Copy,
                                                 scale=rscale[:, bass.ds(q * G + t, 1)]).then_inc(xr_ready, 1)
                    if on(ADD):
                        q, b = s - ADD, (m - ADD) % 2
                        act.wait_ge(a_ready, q + 1)
                        if on(ADD + 2):
                            act.wait_ge(mix, 2 * (q - 2) + 1)
                        act.sem_inc(act_passed, 1)
                        for t in range(G):
                            nc.scalar.activation(v[b][:, t, :], a[b][:, t, :], ACT.Copy,
                                                 scale=dscale[:, bass.ds(q * G + t, 1)]).then_inc(v_ready, 1)
                    if on(MIX):
                        q, b = s - MIX, (m - MIX) % 2
                        act.wait_ge(stat, 10 * (q + 1))
                        nc.scalar.activation(rs[b][:], rv[b][:], ACT.Sqrt).then_inc(rs_ready, 1)
                sweep(step, NORM)(act)

            @block.vector
            def _(dve):
                nc.vector.tensor_scalar(dscale[:], dinv[:], 1.0 if bias_form else keep, None,
                                        ALU.mult).then_inc(scale_ready, 1)
                nc.vector.tensor_scalar(rscale[:], sdeg[:], copies, None, ALU.mult).then_inc(scale_ready, 1)

                def step(s, m, on):
                    if on(NORM - 1):
                        q, b = s - NORM + 1, (m - NORM + 1) % 2
                        dve.wait_ge(rs_ready, q + 1)
                        if on(NORM + 1):
                            dve.wait_ge(y_ready, G * (q - 1))
                        if bias_form:
                            nc.vector.tensor_tensor(rd[b][:], rs[b][:], dinv[:, bass.ds(q * G, G)],
                                                    ALU.mult).then_inc(nm_ready, 1)
                        else:
                            nc.vector.tensor_copy(rd[b][:], rs[b][:]).then_inc(nm_ready, 1)
                        dve.wait_ge(nm_ready, 2 * q + 1)
                        nc.vector.scalar_tensor_tensor(out=nm[b][:], in0=mv[b][:, :, 0], scalar=-1.0, in1=rd[b][:],
                                                       op0=ALU.mult, op1=ALU.mult).then_inc(nm_ready, 1)
                    if on(SUM):
                        q, b = s - SUM, m % 2
                        if on(SUM + 2):
                            dve.wait_ge(sums_ready, q - 1)
                        build_sel(q, sel[b], sel_ready)
                    if on(ADD):
                        q, b, slot = s - ADD, (m - ADD) % 2, (m - ADD) % RING
                        dve.wait_ge(sums_ready, q + 1)
                        dve.wait_ge(y_in[slot], nth(q, slot, RING))
                        if on(ADD + 2):
                            dve.wait_ge(v_ready, G * (q - 1))
                        nc.vector.tensor_tensor(a[b][:], sums[b][:], yin[:, slot, :, :], ALU.add).then_inc(a_ready, 1)
                    if on(MIX):
                        q, b, slot = s - MIX, (m - MIX) % 2, (m - MIX) % RING
                        dve.wait_ge(v_ready, G * (q + 1))
                        dve.wait_ge(xr_ready, G * (q + 1))
                        if on(MIX + 2):
                            dve.wait_ge(y_ready, G * (q - 1))
                        if bias_form:
                            nc.vector.tensor_tensor(u[b][:], v[b][:], tiles(cb2r), ALU.add).then_inc(mix, 1)
                        else:
                            nc.vector.scalar_tensor_tensor(out=u[b][:], in0=xr[:, slot % 4, :, :], scalar=(1.0 - keep) / copies,
                                                           in1=v[b][:], op0=ALU.mult, op1=ALU.add).then_inc(mix, 1)
                        dve.wait_ge(mix, 2 * q + 1)
                        nc.vector.scalar_tensor_tensor(out=u[b][:], in0=u[b][:], scalar=0.0,
                                                       in1=xr[:, slot % 4, :, :], op0=ALU.max,
                                                       op1=ALU.add).then_inc(mix, 1)
                        dve.wait_ge(mix, 2 * q + 2)
                        row_stats(dve, q, u[b], st[b], mv[b], rv[b], stat, passed)
                sweep(step, NORM - 1)(dve)

        propagate("gcn2_", yz_t, y1_t, y2_t, None)
        count_gathers(RING)
        propagate("appnp_", y2_t, y2_t, x3_t, 0.9)
        count_gathers(RING)

        def messages():
          SLOTS = 4
          with ExitStack() as ctx:
            sem, open_block = phase(ctx)

            def sb(name, shape, dt=F32):
                return ctx.enter_context(nc.sbuf_tensor("msg_" + name, shape, dt))

            def ps(name, shape):
                return ctx.enter_context(nc.psum_tensor("msg_" + name, shape, F32))

            rs, rd, ra = sb("rs", [R, D]), sb("rd", [R, D]), sb("ra", [R, 2 * EA + 1])
            rT = sb("rT", [P, 3, R])
            rh = sb("rh", [R, D])
            score, alpha, ab2c = (sb(n, [R, 1]) for n in ("score", "alpha", "ab2c"))
            aw2r = sb("aw2r", [R, D])
            comp_s, acomp = sb("comp_s", [R, B]), sb("acomp", [R, B])
            fold_i, fold = sb("fold_i", [P, G, R], I32), sb("fold", [P, G, R])
            band_i, band, inside = sb("band_i", [P, G], I32), sb("band", [P, G]), sb("inside", [P, G])
            table4 = sb("table4", [G * R, G, B])
            wa_s, wa_d = sb("wa_s", [D, D]), sb("wa_d", [D, D])
            wa_e = sb("wa_e", [2 * EA + 1, D])
            relw = sb("relw", [P, B, D])
            xs = sb("xs", [P, SLOTS * G, D])
            sidx = sb("sidx", [P, SLOTS * G], I32)
            hot = [sb(f"hot{i}", [P, G, R]) for i in range(2)]
            hotT = [sb(f"hotT{i}", [G * R, P]) for i in range(2)]
            xsT = sb("xsT", [P, 4, G * P])
            coef = sb("coef", [P, 4, G, B])
            mo = [sb(f"mo{i}", [P, G, D]) for i in range(2)]
            xT_p = [ps(f"xT_p{i}", [P, G * P]) for i in range(2)]
            hot_p, coef_p = ps("hot_p", [P, 512]), ps("coef_p", [P, 512])
            rel = [ps(f"rel{i}", [P, B, D]) for i in range(2)]
            (w_in, consts, dve_step, r_turned, r_copied, r_hid, r_alpha, folded, idx_in, turn, passed, hot_ready,
             turned, xT_ready, hotT_ready, coef_done, coef_ready, rel_done, acc) = (sem("msg_" + n) for n in (
                "w_in", "consts", "dve_step", "r_turned", "r_copied", "r_hid", "r_alpha", "folded", "idx_in",
                "turn", "passed", "hot_ready", "turned", "xT_ready", "hotT_ready", "coef_done", "coef_ready",
                "rel_done", "acc"))
            turned_hot = sem("msg_turned_hot")
            m_out = [sem(f"msg_out{i}") for i in range(2)]
            src_in, r_in = landed[:SLOTS], landed[SLOTS]
            block = open_block()
            HOT, TURN, COEF, REL, STORE = 1, 2, 3, 4, 5
            WEIGHTS = 11

            @block.sync
            def _(sp):
                row = lambda a: a.rearrange("(p c) -> p c", p=1)
                for to, of in ((wa_s[:], aw1[0:D, :]), (wa_d[:], aw1[D:2 * D, :]), (wa_e[0:2 * EA, :], aw1[2 * D:, :]),
                               (wa_e[2 * EA:2 * EA + 1, :], row(ab1)), (ra[:, 0:EA], ea1[0:R, :]),
                               (ra[:, EA:2 * EA], ea2[0:R, :]), (comp_s[:], comp),
                               (aw2r[:], aw2.rearrange("d o -> o d").to_broadcast([R, D])),
                               (ab2c[:], row(ab2).to_broadcast([R, 1])),
                               (relw[:, 0:B // 2, :], rel_w[0:B // 2].rearrange("b d o -> d b o")),
                               (relw[:, B // 2:B, :], rel_w[B // 2:B].rearrange("b d o -> d b o"))):
                    sp.dma_start(to, of).then_inc(w_in, 16)

                def step(s, m, on):
                    if on(STORE):
                        q, b = s - STORE, (m - STORE) % 2
                        sp.wait_ge(acc, B * G * (q + 1))
                        sp.dma_start(grouped(msg_t, q), mo[b][:]).then_inc(m_out[b], 16)
                sweep(step, STORE)(sp)
                for b in range(2):
                    sp.wait_ge(m_out[b], 16 * NG // 2)

            @block.gpsimd
            def _(pool):
                for rows, idx in ((rs, src_idx), (rd, dst_idx)):
                    nc.gpsimd.indirect_dma_start(
                        out=rows[:], out_offset=None, in_=x3_t[:, :],
                        in_offset=bass.IndirectOffsetOnAxis(ap=idx[0:R, 0:1], axis=0),
                        bounds_check=N - 1, oob_is_err=False).then_inc(r_in, 16)
                nc.gpsimd.iota(fold_i[:], pattern=[[0, G], [1, R]], base=0, channel_multiplier=0).then_inc(consts, 1)
                nc.gpsimd.iota(band_i[:], pattern=[[-R, G]], base=0, channel_multiplier=1).then_inc(consts, 1)

                def step(s, m, on):
                    if on(0):
                        slot = m % SLOTS
                        if on(SLOTS):
                            pool.wait_ge(turned, s - SLOTS + 1)
                        idx_gather(pool, s, slot, sidx, src_idx, (xs, x3_t), idx_in, src_in[slot], turn)
                sweep(step, 0)(pool)

            @block.tensor
            def _(pe):
                pe.wait_ge(r_in, base[SLOTS] + 32)
                pe.wait_ge(w_in, 16 * WEIGHTS)
                pe.wait_ge(dve_step, 2)
                nc.tensor.transpose(xT_p[0][:, 0:R], rs[:], ident[0:R, 0:R])
                nc.tensor.transpose(xT_p[0][:, R:2 * R], rd[:], ident[0:R, 0:R])
                nc.tensor.transpose(xT_p[0][0:2 * EA + 1, 2 * R:3 * R], ra[:], ident[0:R, 0:R]).then_inc(r_turned, 1)
                pe.wait_ge(r_copied, 2)
                nc.tensor.matmul(xT_p[1][0:R, 0:D], rT[:, 0, :], wa_s[:], start=True, stop=False)
                nc.tensor.matmul(xT_p[1][0:R, 0:D], rT[:, 1, :], wa_d[:], start=False, stop=False)
                nc.tensor.matmul(xT_p[1][0:R, 0:D], rT[0:2 * EA + 1, 2, :], wa_e[:], start=False,
                                 stop=True).then_inc(r_hid, 1)
                pe.wait_ge(folded, 1)
                nc.tensor.matmul(coef_p[0:G * R, 0:B], fold[0:R, :, :].rearrange("p t r -> p (t r)"), acomp[:],
                                 start=True, stop=True).then_inc(r_hid, 1)

                def step(s, m, on):
                    if on(TURN):
                        q, b, slot = s - TURN, (m - TURN) % 2, (m - TURN) % SLOTS
                        pe.wait_ge(src_in[slot], base[slot] + nth(q, slot, SLOTS, 16 * G))
                        if on(TURN + 2):
                            pe.wait_ge(xT_ready, q - 1)
                        for t in range(G):
                            ins = nc.tensor.transpose(xT_p[b][:, t * P:(t + 1) * P], xs[:, slot * G + t, :], ident[:])
                        ins.then_inc(turned, 1)
                        pe.wait_ge(hot_ready, q + 1)
                        if on(TURN + 1):
                            pe.wait_ge(hotT_ready, q)
                        pe.sem_inc(passed, 1)
                        nc.tensor.transpose(hot_p[0:G * R, 0:P], hot[b][:].rearrange("p t r -> p (t r)"),
                                            ident[:]).then_inc(turned_hot, 1)
                    if on(COEF):
                        q, b = s - COEF, (m - COEF) % 2
                        pe.wait_ge(hotT_ready, q + 1)
                        if on(COEF + 1):
                            pe.wait_ge(coef_ready, q)
                        else:
                            pe.wait_ge(folded, 2)
                        nc.tensor.matmul(coef_p[:, 0:G * B], hotT[b][:], table4[:].rearrange("p t b -> p (t b)"),
                                         start=True, stop=True).then_inc(coef_done, 1)
                    if on(REL):
                        q, c = s - REL, (m - REL) % 4
                        pe.wait_ge(xT_ready, q + 1)
                        for t in range(G):
                            if on(REL + 1) or t >= 2:
                                pe.wait_ge(acc, B * (G * q + t - 1))
                            for h in range(2):
                                ins = nc.tensor.matmul(
                                    rel[t % 2][:, h * B // 2:(h + 1) * B // 2, :].rearrange("p b d -> p (b d)"),
                                    xsT[:, c, t * P:(t + 1) * P],
                                    relw[:, h * B // 2:(h + 1) * B // 2, :].rearrange("p b d -> p (b d)"),
                                    start=True, stop=True)
                            ins.then_inc(rel_done, 1)
                sweep(step, REL)(pe)

            @block.scalar
            def _(act):
                act.wait_ge(r_turned, 1)
                nc.scalar.copy(rT[:, 0:2, :], xT_p[0][:, 0:2 * R].rearrange("p (a r) -> p a r", a=2)).then_inc(r_copied, 1)
                nc.scalar.copy(rT[0:2 * EA + 1, 2, :], xT_p[0][0:2 * EA + 1, 2 * R:3 * R]).then_inc(r_copied, 1)
                act.wait_ge(r_hid, 1)
                nc.scalar.activation(rh[:], xT_p[1][0:R, 0:D], ACT.Relu).then_inc(r_alpha, 1)
                act.wait_ge(dve_step, 8)
                act.wait_ge(w_in, 16 * WEIGHTS)
                nc.scalar.activation(alpha[:], score[:], ACT.Sigmoid, bias=ab2c[:, 0:1]).then_inc(r_alpha, 1)

                def step(s, m, on):
                    if on(TURN):
                        q, b, c = s - TURN, (m - TURN) % 2, (m - TURN) % 4
                        act.wait_ge(turned, q + 1)
                        if on(TURN + 4):
                            act.wait_ge(rel_done, G * (q - 3))
                        nc.scalar.copy(xsT[:, c, :], xT_p[b][:]).then_inc(xT_ready, 1)
                        act.wait_ge(turned_hot, q + 1)
                        if on(TURN + 2):
                            act.wait_ge(coef_done, q - 1)
                        nc.scalar.copy(hotT[b][:], hot_p[0:G * R, 0:P]).then_inc(hotT_ready, 1)
                    if on(COEF):
                        q, c = s - COEF, (m - COEF) % 4
                        act.wait_ge(coef_done, q + 1)
                        if on(COEF + 4):
                            act.wait_ge(acc, B * G * (q - 3))
                        nc.scalar.copy(coef[:, c, :, :], coef_p[:, 0:G * B].rearrange("p (t b) -> p t b", t=G)
                                       ).then_inc(coef_ready, 1)
                sweep(step, COEF)(act)

            @block.vector
            def _(dve):
                n = [0]

                def then(ins):
                    n[0] += 1
                    ins.then_inc(dve_step, 1)
                    dve.wait_ge(dve_step, n[0])

                then(nc.vector.memset(ra[:, 2 * EA:2 * EA + 1], 1.0))
                dve.wait_ge(consts, 2)
                then(nc.vector.tensor_copy(fold[:], fold_i[:]))
                then(nc.vector.tensor_copy(band[:], band_i[:]))
                then(nc.vector.tensor_scalar(fold[:], fold[:], pidx[:, 0:1], None, ALU.is_equal))
                then(nc.vector.tensor_scalar(inside[:], band[:], 0.0, None, ALU.is_ge))
                then(nc.vector.scalar_tensor_tensor(out=inside[:], in0=band[:], scalar=float(R), in1=inside[:],
                                                    op0=ALU.is_lt, op1=ALU.mult))
                dve.wait_ge(r_alpha, 1)
                dve.wait_ge(w_in, 16 * WEIGHTS)
                then(nc.vector.tensor_tensor(rh[:], rh[:], aw2r[:], ALU.mult))
                then(nc.vector.tensor_reduce(score[:], rh[:], AX.X, ALU.add))
                dve.wait_ge(r_alpha, 2)
                nc.vector.tensor_scalar(acomp[:], comp_s[:], alpha[:, 0:1], None, ALU.mult).then_inc(folded, 1)
                dve.wait_ge(r_hid, 2)
                for t in range(G):
                    ins = nc.vector.tensor_scalar(table4[:, t, :], coef_p[0:G * R, 0:B], inside[0:G * R, t:t + 1], None,
                                                  ALU.mult)
                ins.then_inc(folded, 1)

                def step(s, m, on):
                    if on(HOT):
                        q, b = s - HOT, (m - HOT) % 2
                        if on(HOT + 2):
                            dve.wait_ge(turned_hot, q - 1)
                        nc.vector.tensor_tensor(
                            hot[b][:], typ[:, bass.ds(q * G, G)].unsqueeze(2).to_broadcast([P, G, R]),
                            iota_row[:, 0:R].unsqueeze(1).to_broadcast([P, G, R]), ALU.is_equal).then_inc(hot_ready, 1)
                    if on(REL):
                        q, b, c = s - REL, (m - REL) % 2, (m - REL) % 4
                        dve.wait_ge(coef_ready, q + 1)
                        if on(REL + 2):
                            dve.wait_ge(m_out[b], nth(q - 2, b, 2))
                        for t in range(G):
                            dve.wait_ge(rel_done, G * q + t + 1)
                            nc.vector.tensor_scalar(mo[b][:, t, :], rel[t % 2][:, 0, :], coef[:, c, t, 0:1], None,
                                                    ALU.mult).then_inc(acc, 1)
                            for i in range(1, B):
                                dve.wait_ge(acc, B * (G * q + t) + i)
                                nc.vector.scalar_tensor_tensor(
                                    out=mo[b][:, t, :], in0=rel[t % 2][:, i, :], scalar=coef[:, c, t, i:i + 1],
                                    in1=mo[b][:, t, :], op0=ALU.mult, op1=ALU.add).then_inc(acc, 1)
                sweep(step, REL)(dve)

        messages()

        def collect():
          with ExitStack() as ctx:
            sem, open_block = phase(ctx)

            def sb(name, shape, dt=F32):
                return ctx.enter_context(nc.sbuf_tensor("col_" + name, shape, dt))

            def ps(name, shape):
                return ctx.enter_context(nc.psum_tensor("col_" + name, shape, F32))

            ring = sb("ring", [P, RING * G, D])
            xin = sb("xin", [P, RING, G, D])
            sel = [sb(f"sel{i}", [P, G * WIN, P]) for i in range(2)]
            xT = [sb(f"xT{i}", [P, G * P]) for i in range(2)]
            mc = [sb(f"mc{i}", [P, G, D]) for i in range(4)]
            u = [sb(f"u{i}", [P, G, D]) for i in range(2)]
            yo = [sb(f"yo{i}", [P, G, D]) for i in range(2)]
            small = lambda n: [sb(f"{n}{i}", [P, G]) for i in range(2)]
            st = [sb(f"st{i}", [P, G, 6]) for i in range(2)]
            mv = [sb(f"mv{i}", [P, G, 2]) for i in range(2)]
            rv, rs, nm = small("rv"), small("rs"), small("nm")
            sums = [ps(f"sums{i}", [P, G, D]) for i in range(2)]
            xTp, dp = ps("xTp", [P, G * P]), ps("dp", [P, G, D])
            (sel_ready, sums_ready, mc_ready, x_turned, xT_ready, d_done, d_read, mix, stat, rs_ready,
             nm_ready, y_ready, y_tail) = (sem("col_" + n) for n in (
                "sel_ready", "sums_ready", "mc_ready", "x_turned", "xT_ready", "d_done", "d_read", "mix",
                "stat", "rs_ready", "nm_ready", "y_ready", "y_tail"))
            msg_in = [sem(f"col_msg_in{i}") for i in range(RING)]
            x_in = [sem(f"col_x_in{i}") for i in range(RING)]
            y_out = [sem(f"col_y_out{i}") for i in range(2)]
            passed = sem("col_dve_passed")
            block = open_block()
            LOAD, SUM, TURN, UPD, MIX, NORM, STORE = 1, 2, 3, 4, 5, 7, 8

            @block.sync
            def _(sp):
                def step(s, m, on):
                    if on(0):
                        if on(RING):
                            sp.wait_ge(sums_ready, s - RING + LAG_LO + 1)
                        sp.dma_start(ring[:, m * G:(m + 1) * G, :], grouped(msg_t, s)).then_inc(msg_in[m], 16)
                    if on(LOAD):
                        q, slot = s - LOAD, (m - LOAD) % RING
                        if on(LOAD + RING):
                            sp.wait_ge(mix, q - RING + 1)
                        sp.dma_start(xin[:, slot, :, :], grouped(x3_t, q)).then_inc(x_in[slot], 16)
                    if on(STORE):
                        q, b = s - STORE, (m - STORE) % 2
                        sp.wait_ge(y_ready, G * (q + 1))
                        if isinstance(q, int) and q == NG - 1:
                            sp.dma_start(grouped(out, q, FULL * P), yo[b][:, 0:FULL, :]).then_inc(y_out[b], 16)
                            sp.dma_start(out[(q * G + FULL) * P:N, :], yo[b][0:REST, FULL, :]).then_inc(y_tail, 16)
                        else:
                            sp.dma_start(grouped(out, q), yo[b][:]).then_inc(y_out[b], 16)
                sweep(step, STORE)(sp)
                for b in range(2):
                    sp.wait_ge(y_out[b], 16 * NG // 2)
                sp.wait_ge(y_tail, 16)

            @block.tensor
            def _(pe):
                def step(s, m, on):
                    if on(SUM):
                        q, b = s - SUM, m % 2
                        if on(0):
                            pe.wait_ge(msg_in[m], nth(s, m, RING))
                        pe.wait_ge(sel_ready, q + 1)
                        if on(SUM + 2):
                            pe.wait_ge(mc_ready, q - 1)
                        window_sums(q, sel[b], ring, [sums[b][:, t, :] for t in range(G)], sums_ready)
                    if on(TURN):
                        q, slot = s - TURN, (m - TURN) % RING
                        pe.wait_ge(x_in[slot], nth(q, slot, RING))
                        if on(TURN + 1):
                            pe.wait_ge(xT_ready, q)
                        for t in range(G):
                            ins = nc.tensor.transpose(xTp[:, t * P:(t + 1) * P], xin[:, slot, t, :], ident[:])
                        ins.then_inc(x_turned, 1)
                    if on(UPD):
                        q, b = s - UPD, (m - UPD) % 2
                        pe.wait_ge(xT_ready, q + 1)
                        if on(UPD + 1):
                            pe.wait_ge(d_read, G * q)
                        for t in range(G):
                            ins = nc.tensor.matmul(dp[:, t, :], xT[b][:, t * P:(t + 1) * P], upd[:], start=True, stop=True)
                        ins.then_inc(d_done, 1)
                sweep(step, UPD)(pe)

            @block.scalar
            def _(act):
                def step(s, m, on):
                    if on(NORM):
                        q, b = s - NORM, (m - NORM) % 2
                        act.wait_ge(nm_ready, q + 1)
                        if on(NORM + 2):
                            act.wait_ge(y_out[b], nth(q - 2, b, 2))
                        for t in range(G):
                            nc.scalar.activation(yo[b][:, t, :], u[b][:, t, :], ACT.Identity, bias=nm[b][:, t:t + 1],
                                                 scale=rs[b][:, t:t + 1]).then_inc(y_ready, 1)
                    if on(TURN):
                        q, b, c = s - TURN, (m - TURN) % 2, (m - TURN) % 4
                        act.wait_ge(sums_ready, q + 1)
                        if on(TURN + 4):
                            act.wait_ge(d_read, G * (q - 3))
                        nc.scalar.copy(mc[c][:], sums[b][:]).then_inc(mc_ready, 1)
                        act.wait_ge(x_turned, q + 1)
                        if on(TURN + 2):
                            act.wait_ge(d_done, q - 1)
                        nc.scalar.copy(xT[b][:], xTp[:]).then_inc(xT_ready, 1)
                    if on(MIX):
                        q, b = s - MIX, (m - MIX) % 2
                        act.wait_ge(stat, 10 * (q + 1))
                        nc.scalar.activation(rs[b][:], rv[b][:], ACT.Sqrt).then_inc(rs_ready, 1)
                sweep(step, NORM)(act)

            @block.vector
            def _(dve):
                def step(s, m, on):
                    if on(NORM - 1):
                        q, b = s - NORM + 1, (m - NORM + 1) % 2
                        dve.wait_ge(rs_ready, q + 1)
                        nc.vector.scalar_tensor_tensor(out=nm[b][:], in0=mv[b][:, :, 0], scalar=-1.0, in1=rs[b][:],
                                                       op0=ALU.mult, op1=ALU.mult).then_inc(nm_ready, 1)
                    if on(SUM):
                        q, b = s - SUM, m % 2
                        if on(SUM + 2):
                            dve.wait_ge(sums_ready, q - 1)
                        build_sel(q, sel[b], sel_ready)
                    if on(MIX):
                        q, b, c, slot = s - MIX, (m - MIX) % 2, (m - MIX) % 4, (m - MIX) % RING
                        dve.wait_ge(d_done, q + 1)
                        dve.wait_ge(mc_ready, q + 1)
                        if on(MIX + 2):
                            dve.wait_ge(y_ready, G * (q - 1))
                        for t in range(G):
                            nc.vector.scalar_tensor_tensor(
                                out=u[b][:, t, :], in0=dp[:, t, :], scalar=cnt[:, bass.ds(q * G + t, 1)],
                                in1=mc[c][:, t, :], op0=ALU.mult, op1=ALU.add).then_inc(d_read, 1)
                        dve.wait_ge(d_read, G * (q + 1))
                        dve.wait_ge(x_in[slot], nth(q, slot, RING))
                        nc.vector.scalar_tensor_tensor(out=u[b][:], in0=u[b][:], scalar=0.0, in1=xin[:, slot, :, :],
                                                       op0=ALU.max, op1=ALU.add).then_inc(mix, 1)
                        dve.wait_ge(mix, q + 1)
                        row_stats(dve, q, u[b], st[b], mv[b], rv[b], stat, passed)
                sweep(step, NORM - 1)(dve)

        collect()


_OUT = ((50000, 128), "float32")


def kernel(**inputs):
    import numpy as _np
    import concourse.bacc as _bacc
    from concourse import mybir as _mybir
    from concourse.bass_utils import run_bass_kernel_spmd as _run

    nc = _bacc.Bacc("TRN2", target_bir_lowering=False, num_devices=1)
    names = ["x", "src", "dst", "edge_attr_32", "edge_attr_32_n2", "edge_type_16", "L0_gnn_eps", "L0_gnn_W1",
             "L0_gnn_b1", "L0_gnn_W2", "L0_gnn_b2", "L0_gnn_gamma", "L0_gnn_beta", "L1_gnn_W1", "L1_gnn_b1",
             "L1_gnn_W2", "L1_gnn_b2", "L3_gnn_weight", "L3_gnn_comp", "L3_gnn_attn_w1", "L3_gnn_attn_b1",
             "L3_gnn_attn_w2", "L3_gnn_attn_b2", "L3_gnn_update"]
    arrays, args = {}, []
    for name in names:
        a = _np.ascontiguousarray(inputs[name])
        if name == "L0_gnn_eps":
            a = a.reshape(1, 1)
        arrays["in_" + name] = a
        args.append(nc.dram_tensor("in_" + name, a.shape, _mybir.dt.from_np(a.dtype), kind="ExternalInput").ap())
    out = nc.dram_tensor("out_0", inputs["x"].shape, F32, kind="ExternalOutput").ap()
    build(nc, *args, out)
    r = _run(nc, [arrays], core_ids=[0])
    return r.results[0]["out_0"]
```

```python
from contextlib import ExitStack

import concourse.bass as bass
from concourse import mybir

F32 = mybir.dt.float32
I32 = mybir.dt.int32
ALU = mybir.AluOpType
ACT = mybir.ActivationFunctionType
AX = mybir.AxisListType

P = 128
G = 4
WIN = 3
RING = 8
UNROLL = 8
HEAD = 10
LAG_LO, LAG_HI = 1, 2
FAR = float(1 << 20)
LN_EPS = 1e-5


def build(nc, x, src, dst, ea1, ea2, etype, eps, W1, b1, W2, b2, gamma, beta,
          cW1, cb1, cW2, cb2, rel_w, comp, aw1, ab1, aw2, ab2, update, out):
    N, D = x.shape
    E = src.shape[0]
    R, B = comp.shape
    NG = -(-N // (P * G))
    NT = NG * G
    H2 = cW1.shape[1] // P
    EA = ea1.shape[1]
    assert D == P and B == 8 and NG == -(-E // (P * G)) and NG <= P and (NG - HEAD) % UNROLL == 0 and N == E
    FULL = N // P - (NG - 1) * G
    REST = N - (N // P) * P

    def table(name, width=D):
        return nc.dram_tensor(name, (NT * P, width), F32).ap()

    y1_t, yz_t, y2_t, x3_t, msg_t = (table(n) for n in ("y1_t", "yz_t", "y2_t", "x3_t", "msg_t"))
    agg_t = table("agg_t", D + 1)
    dstp_t = nc.dram_tensor("dst_rows", (NT, P), F32).ap()

    def grouped(ap2, q, rows=P * G):
        return ap2[bass.ds(q * (P * G), rows), :].rearrange("(t p) d -> p t d", p=P)

    def sweep(step, depth):
        def at(s):
            step(s, s % UNROLL, lambda lag: 0 <= s - lag < NG)
        def run(eng):
            for s in range(HEAD):
                at(s)
            with eng.Fori(HEAD, NG - (UNROLL - 1), UNROLL) as s0:
                for u in range(UNROLL):
                    step(s0 + u, (HEAD + u) % UNROLL, lambda lag: True)
            for s in range(NG, NG + depth):
                at(s)
        return run

    def nth(q, slot, ring, inc=16):
        return (q - slot) * (inc // ring) + inc

    with ExitStack() as whole:
        def hold(name, shape, dt=F32):
            return whole.enter_context(nc.sbuf_tensor(name, shape, dt))

        landed = [whole.enter_context(nc.semaphore(f"gathered{i}")) for i in range(RING)]
        any_rows, any_now, any_put = (whole.enter_context(nc.semaphore(n)) for n in ("any_rows", "any_now", "any_put"))
        base = [16 * G, 16 * G * WIN] + [0] * (RING - 2)

        def count_gathers(ring, first=0):
            for q in range(NG):
                base[first + q % ring] += 16 * G

        def phase(ctx):
            held = []

            def sem(name):
                held.append(ctx.enter_context(nc.semaphore(name)))
                return held[-1]

            def clear():
                for s in held:
                    nc.gpsimd.sem_clear(s)
                nc.all_engine_barrier()

            def open_block():
                ctx.callback(clear)
                return ctx.enter_context(nc.Block())
            return sem, open_block

        ident = hold("ident", [P, P])
        iota_row = hold("iota_row", [P, P])
        dst_win = hold("dst_win", [P, NT * WIN])
        src_idx = hold("src_idx", [P, NT], I32)
        dst_idx = hold("dst_idx", [P, NT], I32)
        dst_col = hold("dst_col", [P, NT])
        typ = hold("typ", [P, NT])
        general = hold("general", [1, 1], I32)
        win_off = hold("win_off", [1, NT * WIN], I32)
        cnt = hold("cnt", [P, NT])
        dinv = hold("dinv", [P, NT])
        sdeg = hold("sdeg", [P, NT])
        ones = hold("ones", [P, P])
        pidx = hold("pidx", [P, 1])
        ope = hold("ope", [P, 1])
        w1 = hold("w1", [P, D])
        w2 = hold("w2", [P, D])
        b1c = hold("b1c", [P, 1])
        b2r = hold("b2r", [1, D])
        gam = hold("gam", [P, D])
        bet = hold("bet", [P, D])
        cw1 = hold("cw1", [P, H2 * P])
        cw2 = hold("cw2", [P, H2, D])
        cb1c = hold("cb1c", [P, H2])
        cb2r = hold("cb2r", [P, D])
        upd = hold("upd", [P, D])

        with ExitStack() as ctx:
            sem, open_block = phase(ctx)

            def sb(name, shape, dt=F32):
                return ctx.enter_context(nc.sbuf_tensor(name, shape, dt))

            nat = [sb(n, [NG, G, P], I32) for n in ("nat_dst", "nat_src", "nat_typ")]
            natf = [sb(n, [NG, G, P]) for n in ("natf_dst", "natf_src", "natf_typ")]
            src_col = sb("src_col", [P, NT])
            iota_i = sb("iota_i", [P, P], I32)
            pidx_i = sb("pidx_i", [P, 1], I32)
            jfirst_i = sb("jfirst_i", [P, G], I32)
            jfirst = sb("jfirst", [P, G])
            klo_i = sb("klo_i", [P, 1], I32)
            klo = sb("klo", [P, 1])
            klim = sb("klim", [P, 2])
            total = sb("total", [P, WIN + 1])
            less = sb("less", [P, max(NT, P)])
            kh = sb("kh", [P, G])
            khi = sb("khi", [P, G], I32)
            rows = sb("rows", [P, G, P])
            under = sb("under", [P, G])
            k0 = sb("k0", [P, G])
            woff = sb("woff", [P, G * WIN], I32)
            own_i, step_i = sb("own_i", [1, NT, WIN], I32), sb("step_i", [1, NT, WIN], I32)
            wki = sb("wki", [P, G * WIN], I32)
            wrows = sb("wrows", [P, G * WIN, P])
            epsc = sb("epsc", [P, 1])
            tp = [ctx.enter_context(nc.psum_tensor(f"tp{i}", [P, G, P], F32)) for i in range(3)]
            wtp = [ctx.enter_context(nc.psum_tensor(f"wtp{i}", [P, G, P], F32)) for i in range(3)]
            piv = ctx.enter_context(nc.psum_tensor("piv", [P, 512], F32))

            weights_in = sem("weights_in")
            pads_set = sem("pads_set")
            lists_in = sem("lists_in")
            consts_i = sem("consts_i")
            dve_step = sem("dve_step")
            ident_ready, lists_f, cols_ready, kh_ready, k0_ready, wk_ready, wrel_ready = (
                sem(n) for n in ("ident_ready", "lists_f", "cols_ready", "kh_ready", "k0_ready",
                                 "wk_ready", "wrel_ready"))
            turned = sem("turned")
            dst_rows_out = sem("dst_rows_out")
            pivots = sem("pivots")
            total_ready, summed, general_ready, own_set = (sem(n) for n in ("total_ready", "summed", "general_ready",
                                                                             "own_set"))
            rows_in, wrows_in = landed[0], landed[1]
            wturned = sem("wturned")
            win_in = sem("win_in")
            weights_all = 16 * (11 + H2)
            block = open_block()

            @block.sync
            def _(sp):
                sp.wait_ge(pads_set, 3)
                for a, t in zip((dst, src, etype), nat):
                    whole_rows = (E // P) - (G - 1) * NG
                    for c in range(G - 1):
                        sp.dma_start(t[:, c, :], a[c * NG * P:(c + 1) * NG * P].rearrange("(k e) -> k e", e=P)
                                     ).then_inc(lists_in, 16)
                    o = (G - 1) * NG * P
                    sp.dma_start(t[0:whole_rows, G - 1, :],
                                 a[o:o + whole_rows * P].rearrange("(k e) -> k e", e=P)).then_inc(lists_in, 16)
                    o += whole_rows * P
                    sp.dma_start(t[whole_rows:whole_rows + 1, G - 1, 0:REST],
                                 a[o:o + REST].rearrange("(k e) -> k e", k=1)).then_inc(lists_in, 16)

                def weight(to, of):
                    sp.dma_start(to, of).then_inc(weights_in, 16)

                col = lambda a: a.rearrange("(p c) -> p c", c=1)
                row = lambda a: a.rearrange("(p c) -> p c", p=1)
                spread = lambda a: row(a).to_broadcast([P, D])
                weight(w1[:], W1)
                weight(w2[:], W2)
                weight(b1c[:], col(b1))
                weight(b2r[:], row(b2))
                weight(gam[:], spread(gamma))
                weight(bet[:], spread(beta))
                weight(epsc[:], eps.to_broadcast([P, 1]))
                weight(cw1[:], cW1)
                weight(cw2[:], cW2.rearrange("(h p) d -> p h d", p=P))
                for h in range(H2):
                    weight(cb1c[:, h:h + 1], col(cb1[h * P:(h + 1) * P]))
                weight(cb2r[:], spread(cb2))
                weight(upd[:], update)
                sp.wait_ge(lists_f, 1)
                sp.dma_start(dstp_t.rearrange("(c k) e -> k c e", k=NG), natf[0][:]).then_inc(dst_rows_out, 16)
                sp.wait_ge(weights_in, weights_all)
                sp.wait_ge(k0_ready, 1)
                sp.dma_start(win_off[0:1, :], woff[0:NG, :]).then_inc(win_in, 16)
                sp.wait_ge(win_in, 16)

            @block.gpsimd
            def _(pool):
                nc.gpsimd.iota(iota_i[:], pattern=[[1, P]], base=0, channel_multiplier=0).then_inc(consts_i, 1)
                nc.gpsimd.iota(pidx_i[:], pattern=[[0, 1]], base=0, channel_multiplier=1).then_inc(consts_i, 1)
                nc.gpsimd.iota(jfirst_i[:], pattern=[[P, G]], base=0, channel_multiplier=P * G).then_inc(consts_i, 1)
                nc.gpsimd.iota(klo_i[:], pattern=[[0, 1]], base=0, channel_multiplier=G).then_inc(consts_i, 1)
                nc.gpsimd.iota(own_i[:], pattern=[[1, NT], [0, WIN]], base=0, channel_multiplier=0).then_inc(consts_i, 1)
                nc.gpsimd.iota(step_i[:], pattern=[[0, NT], [1, WIN]], base=0, channel_multiplier=0).then_inc(consts_i, 1)
                nc.gpsimd.memset(nat[0][:], int(FAR)).then_inc(pads_set, 1)
                nc.gpsimd.memset(nat[1][:], 0).then_inc(pads_set, 1)
                nc.gpsimd.memset(nat[2][:], 0).then_inc(pads_set, 1)
                pool.wait_ge(dst_rows_out, 16)
                pool.wait_ge(kh_ready, 1)
                for c in range(G):
                    nc.gpsimd.indirect_dma_start(
                        out=rows[0:NG, c, :], out_offset=None, in_=dstp_t[:, :],
                        in_offset=bass.IndirectOffsetOnAxis(ap=khi[0:NG, c:c + 1], axis=0),
                        bounds_check=NT - 1, oob_is_err=False).then_inc(rows_in, 16)
                pool.wait_ge(wk_ready, 1)
                for c in range(G * WIN):
                    nc.gpsimd.indirect_dma_start(
                        out=wrows[0:NG, c, :], out_offset=None, in_=dstp_t[:, :],
                        in_offset=bass.IndirectOffsetOnAxis(ap=wki[0:NG, c:c + 1], axis=0),
                        bounds_check=NT - 1, oob_is_err=False).then_inc(wrows_in, 16)
                pool.wait_ge(wrows_in, 16 * G * WIN)

            @block.vector
            def _(dve):
                n = [0]

                def then(ins, *ready):
                    n[0] += 1
                    ins.then_inc(dve_step, 1)
                    dve.wait_ge(dve_step, n[0])
                    for s in ready:
                        dve.sem_inc(s, 1)

                dve.wait_ge(consts_i, 6)
                then(nc.vector.tensor_copy(iota_row[:], iota_i[:]))
                then(nc.vector.tensor_copy(pidx[:], pidx_i[:]))
                then(nc.vector.tensor_scalar(ident[:], iota_row[:], pidx[:, 0:1], None, ALU.is_equal), ident_ready)
                then(nc.vector.tensor_copy(jfirst[:], jfirst_i[:]))
                then(nc.vector.tensor_copy(klo[:], klo_i[:]))
                then(nc.vector.memset(ones[:], 1.0))
                dve.wait_ge(lists_in, 16 * 3 * (G + 1))
                for i in range(3):
                    then(nc.vector.tensor_copy(natf[i][:], nat[i][:]), *([lists_f] if i == 2 else []))
                dve.wait_ge(turned, 3)
                for to, of in ((dst_col, tp[0]), (src_col, tp[1]), (typ, tp[2])):
                    then(nc.vector.tensor_copy(to[:].rearrange("e (c k) -> e c k", c=G), of[:, :, 0:NG]))
                then(nc.vector.tensor_copy(src_idx[:], src_col[:]), cols_ready)
                then(nc.vector.tensor_scalar(dst_idx[:], dst_col[:], float(N - 1), None, ALU.min))
                dve.wait_ge(pivots, 1)
                for c in range(G):
                    then(nc.vector.tensor_scalar(less[:, 0:NT], piv[:, 0:NT], jfirst[:, c:c + 1], None, ALU.is_lt))
                    then(nc.vector.tensor_reduce(kh[:, c:c + 1], less[:, 0:NT], AX.X, ALU.add))
                then(nc.vector.tensor_scalar(kh[:], kh[:], -1.0, 0.0, ALU.add, ALU.max))
                then(nc.vector.tensor_copy(khi[:], kh[:]), kh_ready)
                then(nc.vector.memset(under[:], 0.0))
                dve.wait_ge(rows_in, 16 * G)
                for c in range(G):
                    then(nc.vector.tensor_scalar(less[0:NG, 0:P], rows[0:NG, c, :], jfirst[0:NG, c:c + 1], None,
                                                 ALU.is_lt))
                    then(nc.vector.tensor_reduce(under[0:NG, c:c + 1], less[0:NG, 0:P], AX.X, ALU.add))
                then(nc.vector.scalar_tensor_tensor(out=k0[:], in0=under[:], scalar=float(P), in1=kh[:],
                                                    op0=ALU.is_ge, op1=ALU.add))
                then(nc.vector.tensor_scalar(klim[:, 0:1], klo[:], -float(G * LAG_LO), 0.0, ALU.add, ALU.max))
                then(nc.vector.tensor_scalar(klim[:, 1:2], klo[:], float(G * (LAG_HI + 1) - WIN),
                                             float(NT - WIN), ALU.add, ALU.min))
                then(nc.vector.tensor_scalar(k0[:], k0[:], klim[:, 0:1], klim[:, 1:2], ALU.max, ALU.min))
                for c in range(G):
                    for i in range(WIN):
                        then(nc.vector.tensor_scalar(wki[:, c * WIN + i:c * WIN + i + 1], k0[:, c:c + 1],
                                                     float(i), None, ALU.add))
                dve.sem_inc(wk_ready, 1)
                then(nc.vector.tensor_scalar(woff[:], wki[:], RING * G - 1, None, ALU.bitwise_and))
                then(nc.vector.tensor_scalar(woff[:], woff[:], float(D + 1), None, ALU.mult), k0_ready)
                dve.wait_ge(wrows_in, 16 * G * WIN)
                for c in range(G):
                    then(nc.vector.tensor_scalar(wrows[0:NG, c * WIN:(c + 1) * WIN, :],
                                                 wrows[0:NG, c * WIN:(c + 1) * WIN, :],
                                                 jfirst[0:NG, c:c + 1], None, ALU.subtract))
                dve.sem_inc(wrel_ready, 1)
                held = rows[0:NG, :, :].rearrange("p c e -> p (c e)")
                wr = wrows[0:NG, :, :].rearrange("p w e -> p (w e)")
                then(nc.vector.memset(total[:], 0.0))
                for c in range(WIN):
                    cut = wr[:, c * G * P:(c + 1) * G * P]
                    then(nc.vector.tensor_scalar(held, cut, 0.0, None, ALU.is_ge))
                    then(nc.vector.scalar_tensor_tensor(out=held, in0=cut, scalar=float(P), in1=held,
                                                        op0=ALU.is_lt, op1=ALU.mult))
                    then(nc.vector.tensor_reduce(total[0:NG, c:c + 1], held, AX.X, ALU.add))
                then(nc.vector.tensor_reduce(total[:, WIN:WIN + 1], total[:, 0:WIN], AX.X, ALU.add), total_ready)
                dve.wait_ge(summed, 1)
                then(nc.vector.tensor_scalar(general[:], piv[0:1, 0:1], float(E), None, ALU.not_equal), general_ready)
                dve.wait_ge(wturned, 1)
                for c in range(G * WIN):
                    then(nc.vector.tensor_copy(dst_win[:, c:NT * WIN:G * WIN], wtp[c // G][:, c % G, 0:NG]))
                dve.wait_ge(weights_in, weights_all)
                then(nc.vector.tensor_scalar(ope[:], epsc[:], 1.0, None, ALU.add))
                with dve.If(dve.value_load(general[0:1, 0:1], min_val=0, max_val=1) > 0):
                    dve.wait_ge(win_in, 16)
                    nc.vector.memset(dst_win[:], FAR).then_inc(own_set, 1)
                    then(nc.vector.tensor_scalar(own_i[:], own_i[:], float(NT - WIN), None, ALU.min))
                    then(nc.vector.tensor_tensor(own_i[:], own_i[:], step_i[:], ALU.add))
                    then(nc.vector.tensor_scalar(own_i[:], own_i[:], RING * G - 1, None, ALU.bitwise_and))
                    nc.vector.tensor_scalar(win_off[:], own_i[:].rearrange("p j w -> p (j w)"), float(D + 1), None,
                                            ALU.mult).then_inc(own_set, 1)
                    dve.wait_ge(own_set, 2)
                    nc.vector.tensor_copy(dst_win[:, 0:(NT - WIN) * WIN:WIN],
                                          pidx[:, 0:1].to_broadcast([P, NT - WIN])).then_inc(own_set, 1)
                    for i in range(WIN):
                        j = NT - WIN + i
                        nc.vector.tensor_copy(dst_win[:, j * WIN + i:j * WIN + i + 1], pidx[:]).then_inc(own_set, 1)
                with dve.Else():
                    dve.sem_inc(own_set, 1)

            @block.tensor
            def _(pe):
                pe.wait_ge(lists_f, 1)
                pe.wait_ge(ident_ready, 1)
                for i in range(3):
                    for c in range(G):
                        ins = nc.tensor.transpose(tp[i][:, c, 0:NG], natf[i][:, c, :], ident[0:NG, 0:NG])
                    ins.then_inc(turned, 1)
                pe.wait_ge(cols_ready, 1)
                nc.tensor.matmul(piv[:, 0:NT], ones[0:1, :], dst_col[0:1, :], start=True,
                                 stop=True).then_inc(pivots, 1)
                pe.wait_ge(wrel_ready, 1)
                for c in range(G * WIN):
                    ins = nc.tensor.transpose(wtp[c // G][:, c % G, 0:NG], wrows[0:NG, c, :], ident[0:NG, 0:NG])
                ins.then_inc(wturned, 1)
                pe.wait_ge(total_ready, 1)
                nc.tensor.matmul(piv[:, 0:1], ones[:], total[:, WIN:WIN + 1], start=True, stop=True).then_inc(summed, 1)

        def idx_gather(pool, q, m, idx_ring, idx_all, tabs, idx_in, slot_sem, turn):
            nc.gpsimd.tensor_copy(idx_ring[:, m * G:(m + 1) * G], idx_all[:, bass.ds(q * G, G)]).then_inc(idx_in, 1)
            pool.wait_ge(idx_in, q + 1)
            pool.sem_inc(turn, 1)
            for t in range(G):
                k = m * G + t
                nc.gpsimd.indirect_dma_start(
                    out=tabs[0][:, k, 0:D], out_offset=None, in_=tabs[1][:, :],
                    in_offset=bass.IndirectOffsetOnAxis(ap=idx_ring[:, k:k + 1], axis=0),
                    bounds_check=N - 1, oob_is_err=False).then_inc(slot_sem, 16)

        def windows(q):
            return nc.values_load_multi_w_load_instructions(
                win_off[0:1, bass.ds(q * (G * WIN), G * WIN)], engines=[mybir.EngineType.PE], min_val=0,
                max_val=(RING * G - 1) * (D + 1),
                skip_runtime_bounds_check_because="setup takes them modulo the ring's size")[1]

        def window_sums(where, sel, ring, sums, done):
            rows = ring[:].rearrange("p k w -> p (k w)")
            for t in range(G):
                for i in range(WIN):
                    ins = nc.tensor.matmul(sums[t], sel[:, t * WIN + i, :],
                                           rows[:, bass.ds(where[t * WIN + i], sums[t].shape[-1])],
                                           start=(i == 0), stop=(i == WIN - 1))
            ins.then_inc(done, 1)

        def fill_ring(pool, tabs, slots, idx_ring, idx_in, turn, free, width):
            def gather(s, m, on):
                if on(0):
                    free(s, m, on)
                    idx_gather(pool, s, m, idx_ring, src_idx, tabs, idx_in, slots[m], turn)

            def load(s, m, on):
                if on(0):
                    free(s, m, on)
                    nc.gpsimd.dma_start(tabs[0][:, m * G:(m + 1) * G, 0:width],
                                        grouped(agg_t, s)[:, :, 0:width]).then_inc(slots[m], 16 * G)

            with pool.If(pool.value_load(general[0:1, 0:1], min_val=0, max_val=1) > 0):
                sweep(load, 0)(pool)
            with pool.Else():
                sweep(gather, 0)(pool)

        def build_sel(q, sel, done):
            nc.vector.tensor_tensor(
                sel[:], dst_win[:, bass.ds(q * (G * WIN), G * WIN)].unsqueeze(2).to_broadcast([P, G * WIN, P]),
                iota_row[:].unsqueeze(1).to_broadcast([P, G * WIN, P]), ALU.is_equal).then_inc(done, 1)

        def row_stats(dve, q, rows, st, mv, rvar, step, passed):
            for t in range(G):
                nc.vector.bn_stats(st[:, t, :], rows[:, t, :]).then_inc(step, 1)
            dve.wait_ge(step, q * 10 + 4)
            dve.sem_inc(passed, 1)
            for t in range(G):
                nc.vector.bn_aggr(mv[:, t, :], st[:, t, :]).then_inc(step, 1)
            dve.wait_ge(step, q * 10 + 8)
            nc.vector.tensor_scalar(rvar[:], mv[:, :, 1], LN_EPS, None, ALU.add).then_inc(step, 1)
            dve.wait_ge(step, q * 10 + 9)
            nc.vector.reciprocal(rvar[:], rvar[:]).then_inc(step, 1)

        def tiles(a):
            return a[:].unsqueeze(1).to_broadcast([P, G, D])

        def flat(a):
            return a.rearrange("p t d -> p (t d)")

        def general_sums(n, from_t, by_edge):
          with ExitStack() as ctx:
            sem, open_block = phase(ctx)

            def sb(name, shape, dt=F32):
                return ctx.enter_context(nc.sbuf_tensor(f"any{n}_{name}", shape, dt))

            zeros = sb("zeros", [P, G, D + 1])
            rows, now, new = sb("rows", [P, D + 1]), sb("now", [P, D + 1]), sb("new", [P, D + 1])
            sidx, didx, widx = (sb(i, [P, 1], I32) for i in ("sidx", "didx", "widx"))
            col, dups, to = sb("col", [P, 1]), sb("dups", [P, 1]), sb("to", [P, 1])
            wide, same, before = sb("wide", [P, P]), sb("same", [P, P]), sb("before", [P, P])
            row_p = ctx.enter_context(nc.psum_tensor(f"any{n}_row", [P, P], F32))
            sum_p = ctx.enter_context(nc.psum_tensor(f"any{n}_sum", [P, D + 1], F32))
            zero_set, zeroed, idx_in, turn, round_open, dve_step, passed, rowed, summed, new_ready, copied = (
                sem(f"any{n}_" + i) for i in ("zero_set", "zeroed", "idx_in", "turn", "round_open", "dve_step", "passed", "rowed",
                                              "summed", "new_ready", "copied"))
            before_n = n * NT * 16
            block = open_block()

            @block.sync
            def _(sp):
                with sp.If(sp.value_load(general[0:1, 0:1], min_val=0, max_val=1) > 0):
                    sp.wait_ge(zero_set, 3)
                    for q in range(NG):
                        sp.dma_start(grouped(agg_t, q), zeros[:]).then_inc(zeroed, 16)
                    sp.wait_ge(zeroed, 16 * NG)
                    if by_edge:
                        sp.wait_ge(any_put, before_n + 16 * NT)
                        sp.dma_start(from_t[:, :], agg_t[:, 0:D]).then_inc(copied, 16)
                        sp.wait_ge(copied, 16)
                with sp.Else():
                    sp.sem_inc(passed, 1)

            @block.gpsimd
            def _(pool):
                with pool.If(pool.value_load(general[0:1, 0:1], min_val=0, max_val=1) > 0):
                    pool.wait_ge(zero_set, 3)
                    pool.wait_ge(zeroed, 16 * NG)
                    pool.sem_inc(round_open, 1)
                    with pool.Fori(0, NT, 1) as k:
                        nc.gpsimd.tensor_copy(sidx[:], src_idx[:, bass.ds(k, 1)]).then_inc(idx_in, 1)
                        nc.gpsimd.tensor_copy(didx[:], dst_idx[:, bass.ds(k, 1)]).then_inc(idx_in, 1)
                        pool.wait_ge(idx_in, 2 * k + 2)
                        pool.sem_inc(turn, 1)
                        if by_edge:
                            nc.gpsimd.dma_start(rows[:, 0:D], from_t[bass.ds(k * P, P), :]).then_inc(any_rows, 16)
                        else:
                            nc.gpsimd.indirect_dma_start(
                                out=rows[:, 0:D], out_offset=None, in_=from_t[:, :],
                                in_offset=bass.IndirectOffsetOnAxis(ap=sidx[:, 0:1], axis=0),
                                bounds_check=N - 1, oob_is_err=False).then_inc(any_rows, 16)
                        nc.gpsimd.indirect_dma_start(
                            out=now[:], out_offset=None, in_=agg_t[:, :],
                            in_offset=bass.IndirectOffsetOnAxis(ap=didx[:, 0:1], axis=0),
                            bounds_check=N - 1, oob_is_err=False).then_inc(any_now, 16)
                        pool.wait_ge(new_ready, k + 1)
                        pool.sem_inc(turn, 1)
                        nc.gpsimd.indirect_dma_start(
                            out=agg_t[:, :], out_offset=bass.IndirectOffsetOnAxis(ap=widx[:, 0:1], axis=0),
                            in_=new[:], in_offset=None, bounds_check=N - 1, oob_is_err=False).then_inc(any_put, 16)
                        pool.wait_ge(any_put, before_n + 16 * k + 16)
                        pool.sem_inc(round_open, 1)
                with pool.Else():
                    pool.sem_inc(turn, 1)

            @block.tensor
            def _(pe):
                with pe.If(pe.value_load(general[0:1, 0:1], min_val=0, max_val=1) > 0):
                    with pe.Fori(0, NT, 1) as k:
                        pe.wait_ge(dve_step, 7 * k + 2)
                        nc.tensor.transpose(row_p[:], wide[:], ident[:]).then_inc(rowed, 1)
                        pe.wait_ge(dve_step, 7 * k + 3)
                        pe.wait_ge(any_rows, before_n + 16 * k + 16)
                        nc.tensor.matmul(sum_p[:], same[:], rows[:], start=True, stop=True).then_inc(summed, 1)
                with pe.Else():
                    pe.sem_inc(rowed, 1)

            @block.vector
            def _(dve):
                with dve.If(dve.value_load(general[0:1, 0:1], min_val=0, max_val=1) > 0):
                    nc.vector.memset(zeros[:], 0.0).then_inc(zero_set, 1)
                    nc.vector.memset(rows[:, D:D + 1], 1.0).then_inc(zero_set, 1)
                    nc.vector.tensor_scalar(before[:], iota_row[:], pidx[:, 0:1], None, ALU.is_lt).then_inc(zero_set, 1)
                    dve.wait_ge(zero_set, 3)
                    with dve.Fori(0, NT, 1) as k:
                        def then(i, ins):
                            ins.then_inc(dve_step, 1)
                            dve.wait_ge(dve_step, 7 * k + i)
                            dve.sem_inc(passed, 1)
                        dve.wait_ge(round_open, k + 1)
                        dve.sem_inc(passed, 1)
                        then(1, nc.vector.tensor_copy(col[:], dst_col[:, bass.ds(k, 1)]))
                        then(2, nc.vector.tensor_copy(wide[:], col[:, 0:1].to_broadcast([P, P])))
                        dve.wait_ge(rowed, k + 1)
                        dve.sem_inc(passed, 1)
                        then(3, nc.vector.tensor_scalar(same[:], row_p[:], col[:, 0:1], None, ALU.is_equal))
                        then(4, nc.vector.tensor_tensor(wide[:], same[:], before[:], ALU.mult))
                        then(5, nc.vector.tensor_reduce(dups[:], wide[:], AX.X, ALU.add))
                        then(6, nc.vector.scalar_tensor_tensor(out=to[:], in0=dups[:], scalar=FAR, in1=col[:],
                                                               op0=ALU.mult, op1=ALU.add))
                        then(7, nc.vector.tensor_copy(widx[:], to[:]))
                        dve.wait_ge(summed, k + 1)
                        dve.wait_ge(any_now, before_n + 16 * k + 16)
                        dve.sem_inc(passed, 1)
                        nc.vector.tensor_tensor(new[:], now[:], sum_p[:], ALU.add).then_inc(new_ready, 1)
                with dve.Else():
                    dve.sem_inc(passed, 1)

        def gin_layer():
          W = D + 1
          with ExitStack() as ctx:
            sem, open_block = phase(ctx)

            def sb(name, shape, dt=F32):
                return ctx.enter_context(nc.sbuf_tensor("gin_" + name, shape, dt))

            def ps(name, shape):
                return ctx.enter_context(nc.psum_tensor("gin_" + name, shape, F32))

            ring = sb("ring", [P, RING * G, D + 1])
            idx = sb("idx", [P, RING * G], I32)
            xin = sb("xin", [P, RING, G, D])
            sel = [sb(f"sel{i}", [P, G * WIN, P]) for i in range(2)]
            z = [sb(f"z{i}", [P, G, D]) for i in range(2)]
            zT = [sb(f"zT{i}", [P, G * P]) for i in range(2)]
            hT = [sb(f"hT{i}", [P, G * P]) for i in range(2)]
            r = [sb(f"r{i}", [P, G, D]) for i in range(2)]
            xn = [sb(f"xn{i}", [P, G, D]) for i in range(2)]
            u = [sb(f"u{i}", [P, G, D]) for i in range(2)]
            yo = [sb(f"yo{i}", [P, G, D]) for i in range(2)]
            small = lambda n, k=1: [sb(f"{n}{i}", [P, G * k]) for i in range(2)]
            stA, stB = ([sb(f"st{n}{i}", [P, G, 6]) for i in range(2)] for n in "AB")
            mvA, mvB = ([sb(f"mv{n}{i}", [P, G, 2]) for i in range(2)] for n in "AB")
            rvA, rvB, rsA, rsB, nmA, nmB, rdB = (small(n) for n in ("rvA", "rvB", "rsA", "rsB", "nmA", "nmB", "rdB"))
            deg, rdeg = small("deg"), small("rdeg")
            sums = [ps(f"sums{i}", [P, 2, 512]) for i in range(2)]
            zTp, hTp, rp = ps("zTp", [P, G * P]), ps("hTp", [P, G * P]), ps("rp", [P, G, D])
            (ring_ones, idx_in, turn, sel_ready, sums_ready, z_steps, zT_turned, zT_ready, h_done, hT_ready,
             r_done, r_ready, statA, rsA_ready, nmA_ready, xn_ready, mix, statB, rsB_ready, nmB_ready, y_ready,
             deg_ready, dinv_ready, x_tail) = (sem("gin_" + n) for n in (
                "ring_ones", "idx_in", "turn", "sel_ready", "sums_ready", "z_steps", "zT_turned", "zT_ready",
                "h_done", "hT_ready", "r_done", "r_ready", "statA", "rsA_ready", "nmA_ready", "xn_ready", "mix",
                "statB", "rsB_ready", "nmB_ready", "y_ready", "deg_ready", "dinv_ready", "x_tail"))
            gathered = landed
            x_in = [sem(f"gin_x_in{i}") for i in range(RING)]
            y_out = [sem(f"gin_y_out{i}") for i in range(2)]
            passed, act_passed = sem("gin_dve_passed"), sem("gin_act_passed")
            block = open_block()
            LOAD, SEL, SUM, TURN, HID, RES, NORM_A, MIX, NORM_B, STORE = 1, 1, 2, 3, 4, 5, 7, 8, 9, 10

            @block.sync
            def _(sp):
                def step(s, m, on):
                    if on(LOAD):
                        q, slot = s - LOAD, (m - LOAD) % RING
                        if on(LOAD + RING):
                            sp.wait_ge(mix, 3 * (q - RING) + 3)
                        if isinstance(q, int) and q == NG - 1:
                            sp.dma_start(xin[:, slot, 0:FULL, :], grouped(x, q, FULL * P)).then_inc(x_in[slot], 16)
                            sp.dma_start(xin[0:REST, slot, FULL, :], x[(q * G + FULL) * P:N, :]).then_inc(x_tail, 16)
                        else:
                            sp.dma_start(xin[:, slot, :, :], grouped(x, q)).then_inc(x_in[slot], 16)
                    if on(STORE):
                        q, b = s - STORE, (m - STORE) % 2
                        sp.wait_ge(y_ready, G * (q + 1))
                        sp.dma_start(grouped(y1_t, q), yo[b][:]).then_inc(y_out[b], 16)
                sweep(step, STORE)(sp)
                for b in range(2):
                    sp.wait_ge(y_out[b], 16 * NG // 2)

            @block.gpsimd
            def _(pool):
                nc.gpsimd.memset(ring[:, :, D:W], 1.0).then_inc(ring_ones, 1)
                pool.wait_ge(ring_ones, 1)

                def free(s, m, on):
                    if on(RING):
                        pool.wait_ge(sums_ready, s - RING + LAG_LO + 1)
                        pool.sem_inc(turn, 1)
                fill_ring(pool, (ring, x), gathered, idx, idx_in, turn, free, W)

            @block.tensor
            def _(pe):
                pe.wait_ge(ring_ones, 1)

                def step(s, m, on):
                    if on(SUM):
                        q, b = s - SUM, m % 2
                        where = windows(q)
                        if on(0):
                            pe.wait_ge(gathered[m], base[m] + nth(s, m, RING, 16 * G))
                        pe.wait_ge(sel_ready, q + 1)
                        if on(SUM + 2):
                            pe.wait_ge(z_steps, 3 * (q - 1))
                        window_sums(where, sel[b], ring, [sums[b][:, t // 2, t % 2 * W:(t % 2 + 1) * W] for t in range(G)],
                                    sums_ready)
                    if on(TURN):
                        q, b = s - TURN, (m - TURN) % 2
                        pe.wait_ge(z_steps, 3 * q + 2)
                        if on(TURN + 1):
                            pe.wait_ge(zT_ready, q)
                        for t in range(G):
                            ins = nc.tensor.transpose(zTp[:, t * P:(t + 1) * P], z[b][:, t, :], ident[:])
                        ins.then_inc(zT_turned, 1)
                    if on(HID):
                        q, b = s - HID, (m - HID) % 2
                        pe.wait_ge(zT_ready, q + 1)
                        if on(HID + 1):
                            pe.wait_ge(hT_ready, q)
                        nc.tensor.matmul(hTp[:], w1[:], zT[b][:], start=True, stop=True).then_inc(h_done, 1)
                    if on(RES):
                        q, b = s - RES, (m - RES) % 2
                        pe.wait_ge(hT_ready, q + 1)
                        if on(RES + 1):
                            pe.wait_ge(r_ready, q)
                        for t in range(G):
                            nc.tensor.matmul(rp[:, t, :], ones[0:1, :], b2r[:], start=True, stop=False)
                            ins = nc.tensor.matmul(rp[:, t, :], hT[b][:, t * P:(t + 1) * P], w2[:], start=False,
                                                   stop=True)
                        ins.then_inc(r_done, 1)
                sweep(step, RES)(pe)

            @block.scalar
            def _(act):
                def step(s, m, on):
                    if on(NORM_A):
                        q, b = s - NORM_A, (m - NORM_A) % 2
                        act.wait_ge(nmA_ready, q + 1)
                        if on(NORM_A + 2):
                            act.wait_ge(mix, 3 * (q - 2) + 1)
                        for t in range(G):
                            nc.scalar.activation(xn[b][:, t, :], r[b][:, t, :], ACT.Identity, bias=nmA[b][:, t:t + 1],
                                                 scale=rsA[b][:, t:t + 1]).then_inc(xn_ready, 1)
                    if on(NORM_B):
                        q, b = s - NORM_B, (m - NORM_B) % 2
                        act.wait_ge(nmB_ready, 2 * (q + 1))
                        if on(NORM_B + 2):
                            act.wait_ge(y_out[b], nth(q - 2, b, 2))
                        for t in range(G):
                            nc.scalar.activation(yo[b][:, t, :], u[b][:, t, :], ACT.Identity, bias=nmB[b][:, t:t + 1],
                                                 scale=rdB[b][:, t:t + 1]).then_inc(y_ready, 1)
                    if on(TURN):
                        q, b = s - TURN, (m - TURN) % 2
                        act.wait_ge(zT_turned, q + 1)
                        if on(TURN + 2):
                            act.wait_ge(h_done, q - 1)
                        nc.scalar.copy(zT[b][:], zTp[:]).then_inc(zT_ready, 1)
                        act.wait_ge(deg_ready, 2 * q + 2)
                        act.sem_inc(act_passed, 1)
                        nc.scalar.activation(dinv[:, bass.ds(q * G, G)], rdeg[b][:], ACT.Sqrt).then_inc(dinv_ready, 1)
                        nc.scalar.activation(sdeg[:, bass.ds(q * G, G)], deg[b][:],
                                             ACT.Sqrt).then_inc(dinv_ready, 1)
                    if on(HID):
                        q, b = s - HID, (m - HID) % 2
                        act.wait_ge(h_done, q + 1)
                        if on(HID + 2):
                            act.wait_ge(r_done, q - 1)
                        nc.scalar.activation(hT[b][:], hTp[:], ACT.Relu, bias=b1c[:, 0:1]).then_inc(hT_ready, 1)
                    if on(NORM_A - 1):
                        q, b = s - NORM_A + 1, (m - NORM_A + 1) % 2
                        act.wait_ge(statA, 10 * (q + 1))
                        nc.scalar.activation(rsA[b][:], rvA[b][:], ACT.Sqrt).then_inc(rsA_ready, 1)
                    if on(MIX):
                        q, b = s - MIX, (m - MIX) % 2
                        act.wait_ge(statB, 10 * (q + 1))
                        nc.scalar.activation(rsB[b][:], rvB[b][:], ACT.Sqrt).then_inc(rsB_ready, 1)
                sweep(step, NORM_B)(act)

            @block.vector
            def _(dve):
                def step(s, m, on):
                    if on(NORM_A):
                        q, b = s - NORM_A, (m - NORM_A) % 2
                        dve.wait_ge(rsA_ready, q + 1)
                        nc.vector.scalar_tensor_tensor(out=nmA[b][:], in0=mvA[b][:, :, 0], scalar=-1.0, in1=rsA[b][:],
                                                       op0=ALU.mult, op1=ALU.mult).then_inc(nmA_ready, 1)
                    if on(NORM_B):
                        q, b = s - NORM_B, (m - NORM_B) % 2
                        dve.wait_ge(rsB_ready, q + 1)
                        dve.wait_ge(dinv_ready, 2 * (q + 1))
                        if on(NORM_B + 2):
                            dve.wait_ge(y_ready, G * (q - 1))
                        nc.vector.tensor_tensor(rdB[b][:], rsB[b][:], dinv[:, bass.ds(q * G, G)],
                                                ALU.mult).then_inc(nmB_ready, 1)
                        dve.wait_ge(nmB_ready, 2 * q + 1)
                        nc.vector.scalar_tensor_tensor(out=nmB[b][:], in0=mvB[b][:, :, 0], scalar=-1.0, in1=rdB[b][:],
                                                       op0=ALU.mult, op1=ALU.mult).then_inc(nmB_ready, 1)
                    if on(SEL):
                        q, b = s - SEL, (m - SEL) % 2
                        if on(SEL + 2):
                            dve.wait_ge(sums_ready, q - 1)
                        build_sel(q, sel[b], sel_ready)
                    if on(TURN):
                        q, b, slot = s - TURN, (m - TURN) % 2, (m - TURN) % RING
                        dve.wait_ge(sums_ready, q + 1)
                        dve.wait_ge(x_in[slot], nth(q, slot, RING))
                        if isinstance(q, int) and q == NG - 1:
                            dve.wait_ge(x_tail, 16)
                        if on(TURN + 2):
                            dve.wait_ge(zT_turned, q - 1)
                            dve.wait_ge(dinv_ready, 2 * (q - 1))
                        pair = lambda h: sums[b][:, h, 0:2 * W].rearrange("p (t w) -> p t w", w=W)
                        for h in range(2):
                            nc.vector.scalar_tensor_tensor(
                                out=z[b][:, 2 * h:2 * h + 2, :], in0=xin[:, slot, 2 * h:2 * h + 2, :],
                                scalar=ope[:, 0:1], in1=pair(h)[:, :, 0:D], op0=ALU.mult,
                                op1=ALU.add).then_inc(z_steps, 1)
                        nc.vector.tensor_copy(
                            cnt[:, bass.ds(q * G, G)].rearrange("p (h t) -> p h t", t=2),
                            sums[b][:, :, 0:2 * W].rearrange("p h (t w) -> p h t w", w=W)[:, :, :, D]).then_inc(z_steps, 1)
                        dve.wait_ge(z_steps, 3 * q + 3)
                        nc.vector.tensor_scalar(deg[b][:], cnt[:, bass.ds(q * G, G)], 1.0, None,
                                                ALU.add).then_inc(deg_ready, 1)
                        dve.wait_ge(deg_ready, 2 * q + 1)
                        nc.vector.reciprocal(rdeg[b][:], deg[b][:]).then_inc(deg_ready, 1)
                    if on(NORM_A - 1):
                        q, b, slot = s - NORM_A + 1, (m - NORM_A + 1) % 2, (m - NORM_A + 1) % RING
                        dve.wait_ge(r_done, q + 1)
                        if on(NORM_A + 1):
                            dve.wait_ge(xn_ready, G * (q - 1))
                        nc.vector.tensor_tensor(r[b][:], rp[:], xin[:, slot, :, :], ALU.add).then_inc(r_ready, 1)
                        dve.wait_ge(r_ready, q + 1)
                        row_stats(dve, q, r[b], stA[b], mvA[b], rvA[b], statA, passed)
                    if on(MIX):
                        q, b, slot = s - MIX, (m - MIX) % 2, (m - MIX) % RING
                        dve.wait_ge(xn_ready, G * (q + 1))
                        if on(MIX + 2):
                            dve.wait_ge(y_ready, G * (q - 1))
                        nc.vector.tensor_tensor(u[b][:], xn[b][:], tiles(gam), ALU.mult).then_inc(mix, 1)
                        dve.wait_ge(mix, 3 * q + 1)
                        nc.vector.tensor_tensor(u[b][:], u[b][:], tiles(bet), ALU.add).then_inc(mix, 1)
                        dve.wait_ge(mix, 3 * q + 2)
                        nc.vector.scalar_tensor_tensor(out=u[b][:], in0=u[b][:], scalar=0.0, in1=xin[:, slot, :, :],
                                                       op0=ALU.max, op1=ALU.add).then_inc(mix, 1)
                        dve.wait_ge(mix, 3 * q + 3)
                        row_stats(dve, q, u[b], stB[b], mvB[b], rvB[b], statB, passed)
                sweep(step, NORM_B)(dve)

        general_sums(0, x, False)
        gin_layer()
        count_gathers(RING)
        def gcn_hidden():
          with ExitStack() as ctx:
            sem, open_block = phase(ctx)

            def sb(name, shape, dt=F32):
                return ctx.enter_context(nc.sbuf_tensor("gcn_" + name, shape, dt))

            def ps(name, shape):
                return ctx.enter_context(nc.psum_tensor("gcn_" + name, shape, F32))

            ring = sb("ring", [P, RING * G, D + 1])
            idx = sb("idx", [P, RING * G], I32)
            yin = sb("yin", [P, RING, G, D])
            sel = [sb(f"sel{i}", [P, G * WIN, P]) for i in range(2)]
            own = [sb(f"own{i}", [P, G, D]) for i in range(2)]
            a = [sb(f"a{i}", [P, G, D]) for i in range(2)]
            aT = [sb(f"aT{i}", [P, G * P]) for i in range(2)]
            hT = [sb(f"hT{i}", [P, H2, G * P]) for i in range(2)]
            yo = [sb(f"yo{i}", [P, G, D]) for i in range(2)]
            sums = [ps(f"sums{i}", [P, G, D]) for i in range(2)]
            aTp, hTp, zp = ps("aTp", [P, G * P]), ps("hTp", [P, H2, G * P]), ps("zp", [P, G, D])
            (idx_in, turn, sel_ready, sums_ready, own_ready, a_ready, aT_turned, aT_ready, h_done, hT_ready, z_done,
             y_ready) = (sem("gcn_" + n) for n in (
                "idx_in", "turn", "sel_ready", "sums_ready", "own_ready", "a_ready", "aT_turned", "aT_ready",
                "h_done", "hT_ready", "z_done", "y_ready"))
            gathered = landed
            y_in = [sem(f"gcn_y_in{i}") for i in range(RING)]
            y_out = [sem(f"gcn_y_out{i}") for i in range(2)]
            act_passed = sem("gcn_act_passed")
            block = open_block()
            LOAD, SEL, SUM, TURN, HID, OUT, STORE = 1, 1, 2, 3, 4, 5, 6

            @block.sync
            def _(sp):
                def step(s, m, on):
                    if on(LOAD):
                        q, slot = s - LOAD, (m - LOAD) % RING
                        if on(LOAD + RING):
                            sp.wait_ge(own_ready, G * (q - RING + 1))
                        sp.dma_start(yin[:, slot, :, :], grouped(y1_t, q)).then_inc(y_in[slot], 16)
                    if on(STORE):
                        q, b = s - STORE, (m - STORE) % 2
                        sp.wait_ge(y_ready, G * (q + 1))
                        sp.dma_start(grouped(yz_t, q), yo[b][:]).then_inc(y_out[b], 16)
                sweep(step, STORE)(sp)
                for b in range(2):
                    sp.wait_ge(y_out[b], 16 * NG // 2)

            @block.gpsimd
            def _(pool):
                def free(s, m, on):
                    if on(RING):
                        pool.wait_ge(sums_ready, s - RING + LAG_LO + 1)
                        pool.sem_inc(turn, 1)
                fill_ring(pool, (ring, y1_t), gathered, idx, idx_in, turn, free, D)

            @block.tensor
            def _(pe):
                def step(s, m, on):
                    if on(SUM):
                        q, b = s - SUM, m % 2
                        where = windows(q)
                        if on(0):
                            pe.wait_ge(gathered[m], base[m] + nth(s, m, RING, 16 * G))
                        pe.wait_ge(sel_ready, q + 1)
                        if on(SUM + 2):
                            pe.wait_ge(a_ready, G * (q - 1))
                        window_sums(where, sel[b], ring, [sums[b][:, t, :] for t in range(G)], sums_ready)
                    if on(TURN):
                        q, b = s - TURN, (m - TURN) % 2
                        pe.wait_ge(a_ready, G * (q + 1))
                        if on(TURN + 1):
                            pe.wait_ge(aT_ready, q)
                        for t in range(G):
                            ins = nc.tensor.transpose(aTp[:, t * P:(t + 1) * P], a[b][:, t, :], ident[:])
                        ins.then_inc(aT_turned, 1)
                    if on(HID):
                        q, b = s - HID, (m - HID) % 2
                        pe.wait_ge(aT_ready, q + 1)
                        if on(HID + 1):
                            pe.wait_ge(hT_ready, H2 * q)
                        for h in range(H2):
                            nc.tensor.matmul(hTp[:, h, :], cw1[:, h * P:(h + 1) * P], aT[b][:], start=True,
                                             stop=True).then_inc(h_done, 1)
                    if on(OUT):
                        q, b = s - OUT, (m - OUT) % 2
                        pe.wait_ge(hT_ready, H2 * (q + 1))
                        if on(OUT + 1):
                            pe.wait_ge(y_ready, G * q)
                        for t in range(G):
                            for h in range(H2):
                                ins = nc.tensor.matmul(zp[:, t, :], hT[b][:, h, t * P:(t + 1) * P], cw2[:, h, :],
                                                       start=(h == 0), stop=(h == H2 - 1))
                        ins.then_inc(z_done, 1)
                sweep(step, OUT)(pe)

            @block.scalar
            def _(act):
                def step(s, m, on):
                    if on(SUM):
                        q, b, slot = s - SUM, m % 2, (m - SUM) % RING
                        act.wait_ge(y_in[slot], nth(q, slot, RING))
                        if on(SUM + 2):
                            act.wait_ge(a_ready, G * (q - 1))
                        act.sem_inc(act_passed, 1)
                        for t in range(G):
                            nc.scalar.activation(own[b][:, t, :], yin[:, slot, t, :], ACT.Copy,
                                                 scale=dinv[:, bass.ds(q * G + t, 1)]).then_inc(own_ready, 1)
                    if on(TURN):
                        q, b = s - TURN, (m - TURN) % 2
                        act.wait_ge(aT_turned, q + 1)
                        if on(TURN + 2):
                            act.wait_ge(h_done, H2 * (q - 1))
                        nc.scalar.copy(aT[b][:], aTp[:]).then_inc(aT_ready, 1)
                    if on(HID):
                        q, b = s - HID, (m - HID) % 2
                        if on(HID + 2):
                            act.wait_ge(z_done, q - 1)
                        for h in range(H2):
                            act.wait_ge(h_done, H2 * q + h + 1)
                            nc.scalar.activation(hT[b][:, h, :], hTp[:, h, :], ACT.Relu,
                                                 bias=cb1c[:, h:h + 1]).then_inc(hT_ready, 1)
                    if on(OUT):
                        q, b = s - OUT, (m - OUT) % 2
                        act.wait_ge(z_done, q + 1)
                        if on(OUT + 2):
                            act.wait_ge(y_out[b], nth(q - 2, b, 2))
                        act.sem_inc(act_passed, 1)
                        for t in range(G):
                            nc.scalar.activation(yo[b][:, t, :], zp[:, t, :], ACT.Copy,
                                                 scale=dinv[:, bass.ds(q * G + t, 1)]).then_inc(y_ready, 1)
                sweep(step, OUT)(act)

            @block.vector
            def _(dve):
                def step(s, m, on):
                    if on(SEL):
                        q, b = s - SEL, (m - SEL) % 2
                        if on(SEL + 2):
                            dve.wait_ge(sums_ready, q - 1)
                        build_sel(q, sel[b], sel_ready)
                    if on(TURN):
                        q, b = s - TURN, (m - TURN) % 2
                        dve.wait_ge(sums_ready, q + 1)
                        dve.wait_ge(own_ready, G * (q + 1))
                        if on(TURN + 2):
                            dve.wait_ge(aT_turned, q - 1)
                        for t in range(G):
                            nc.vector.scalar_tensor_tensor(
                                out=a[b][:, t, :], in0=sums[b][:, t, :], scalar=dinv[:, bass.ds(q * G + t, 1)],
                                in1=own[b][:, t, :], op0=ALU.mult, op1=ALU.add).then_inc(a_ready, 1)
                sweep(step, TURN)(dve)

        general_sums(1, y1_t, False)
        gcn_hidden()
        count_gathers(RING)

        def propagate(pre, from_t, res_t, to_t, keep):
          bias_form = keep is None
          with ExitStack() as ctx:
            sem, open_block = phase(ctx)

            def sb(name, shape, dt=F32):
                return ctx.enter_context(nc.sbuf_tensor(pre + name, shape, dt))

            def ps(name, shape):
                return ctx.enter_context(nc.psum_tensor(pre + name, shape, F32))

            ring = sb("ring", [P, RING * G, D + 1])
            idx = sb("idx", [P, RING * G], I32)
            yin = sb("yin", [P, RING, G, D])
            rin = sb("rin", [P, RING, G, D]) if bias_form else yin
            sel = [sb(f"sel{i}", [P, G * WIN, P]) for i in range(2)]
            a = [sb(f"a{i}", [P, G, D]) for i in range(2)]
            v = [sb(f"v{i}", [P, G, D]) for i in range(2)]
            xr = sb("xr", [P, 4, G, D])
            u = [sb(f"u{i}", [P, G, D]) for i in range(2)]
            yo = [sb(f"yo{i}", [P, G, D]) for i in range(2)]
            small = lambda n: [sb(f"{n}{i}", [P, G]) for i in range(2)]
            st = [sb(f"st{i}", [P, G, 6]) for i in range(2)]
            mv = [sb(f"mv{i}", [P, G, 2]) for i in range(2)]
            rv, rs, rd, nm = small("rv"), small("rs"), small("rd"), small("nm")
            dscale = sb("dscale", [P, NT])
            rscale = sb("rscale", [P, NT])
            copies = 1.0 if bias_form else 2.0
            sums = [ps(f"sums{i}", [P, G, D]) for i in range(2)]
            (idx_in, turn, sel_ready, sums_ready, xr_ready, a_ready, v_ready, mix, stat, rs_ready, nm_ready, y_ready,
             scale_ready) = (sem(pre + n) for n in (
                "idx_in", "turn", "sel_ready", "sums_ready", "xr_ready", "a_ready", "v_ready", "mix", "stat",
                "rs_ready", "nm_ready", "y_ready", "scale_ready"))
            gathered = landed
            y_in = [sem(f"{pre}y_in{i}") for i in range(RING)]
            r_in = [sem(f"{pre}r_in{i}") for i in range(RING)] if bias_form else y_in
            y_out = [sem(f"{pre}y_out{i}") for i in range(2)]
            passed, act_passed = sem(pre + "dve_passed"), sem(pre + "act_passed")
            block = open_block()
            LOAD, SEL, SUM, ADD, MIX, NORM, STORE = 1, 1, 2, 3, 4, 6, 7

            @block.sync
            def _(sp):
                def step(s, m, on):
                    if on(LOAD):
                        q, slot = s - LOAD, (m - LOAD) % RING
                        if on(LOAD + RING):
                            sp.wait_ge(xr_ready, G * (q - RING + 1))
                            sp.wait_ge(a_ready, q - RING + 1)
                        sp.dma_start(yin[:, slot, :, :], grouped(from_t, q)).then_inc(y_in[slot], 16)
                        if bias_form:
                            sp.dma_start(rin[:, slot, :, :], grouped(res_t, q)).then_inc(r_in[slot], 16)
                    if on(STORE):
                        q, b = s - STORE, (m - STORE) % 2
                        sp.wait_ge(y_ready, G * (q + 1))
                        sp.dma_start(grouped(to_t, q), yo[b][:]).then_inc(y_out[b], 16)
                sweep(step, STORE)(sp)
                for b in range(2):
                    sp.wait_ge(y_out[b], 16 * NG // 2)

            @block.gpsimd
            def _(pool):
                def free(s, m, on):
                    if on(RING):
                        pool.wait_ge(sums_ready, s - RING + LAG_LO + 1)
                        pool.sem_inc(turn, 1)
                fill_ring(pool, (ring, from_t), gathered, idx, idx_in, turn, free, D)

            @block.tensor
            def _(pe):
                def step(s, m, on):
                    if on(SUM):
                        q, b = s - SUM, m % 2
                        where = windows(q)
                        if on(0):
                            pe.wait_ge(gathered[m], base[m] + nth(s, m, RING, 16 * G))
                        pe.wait_ge(sel_ready, q + 1)
                        if on(SUM + 2):
                            pe.wait_ge(a_ready, q - 1)
                        window_sums(where, sel[b], ring, [sums[b][:, t, :] for t in range(G)], sums_ready)
                sweep(step, SUM)(pe)

            @block.scalar
            def _(act):
                act.wait_ge(scale_ready, 2)

                def step(s, m, on):
                    if on(NORM):
                        q, b = s - NORM, (m - NORM) % 2
                        act.wait_ge(nm_ready, 2 * (q + 1))
                        if on(NORM + 2):
                            act.wait_ge(y_out[b], nth(q - 2, b, 2))
                        for t in range(G):
                            nc.scalar.activation(yo[b][:, t, :], u[b][:, t, :], ACT.Identity, bias=nm[b][:, t:t + 1],
                                                 scale=rd[b][:, t:t + 1]).then_inc(y_ready, 1)
                    if on(SUM):
                        q, slot = s - SUM, (m - SUM) % RING
                        act.wait_ge(r_in[slot], nth(q, slot, RING))
                        if on(SUM + 4):
                            act.wait_ge(mix, 2 * (q - 3))
                        act.sem_inc(act_passed, 1)
                        for t in range(G):
                            nc.scalar.activation(xr[:, slot % 4, t, :], rin[:, slot, t, :], ACT.Copy,
                                                 scale=rscale[:, bass.ds(q * G + t, 1)]).then_inc(xr_ready, 1)
                    if on(ADD):
                        q, b = s - ADD, (m - ADD) % 2
                        act.wait_ge(a_ready, q + 1)
                        if on(ADD + 2):
                            act.wait_ge(mix, 2 * (q - 2) + 1)
                        act.sem_inc(act_passed, 1)
                        for t in range(G):
                            nc.scalar.activation(v[b][:, t, :], a[b][:, t, :], ACT.Copy,
                                                 scale=dscale[:, bass.ds(q * G + t, 1)]).then_inc(v_ready, 1)
                    if on(MIX):
                        q, b = s - MIX, (m - MIX) % 2
                        act.wait_ge(stat, 10 * (q + 1))
                        nc.scalar.activation(rs[b][:], rv[b][:], ACT.Sqrt).then_inc(rs_ready, 1)
                sweep(step, NORM)(act)

            @block.vector
            def _(dve):
                nc.vector.tensor_scalar(dscale[:], dinv[:], 1.0 if bias_form else keep, None,
                                        ALU.mult).then_inc(scale_ready, 1)
                nc.vector.tensor_scalar(rscale[:], sdeg[:], copies, None, ALU.mult).then_inc(scale_ready, 1)

                def step(s, m, on):
                    if on(NORM - 1):
                        q, b = s - NORM + 1, (m - NORM + 1) % 2
                        dve.wait_ge(rs_ready, q + 1)
                        if on(NORM + 1):
                            dve.wait_ge(y_ready, G * (q - 1))
                        if bias_form:
                            nc.vector.tensor_tensor(rd[b][:], rs[b][:], dinv[:, bass.ds(q * G, G)],
                                                    ALU.mult).then_inc(nm_ready, 1)
                        else:
                            nc.vector.tensor_copy(rd[b][:], rs[b][:]).then_inc(nm_ready, 1)
                        dve.wait_ge(nm_ready, 2 * q + 1)
                        nc.vector.scalar_tensor_tensor(out=nm[b][:], in0=mv[b][:, :, 0], scalar=-1.0, in1=rd[b][:],
                                                       op0=ALU.mult, op1=ALU.mult).then_inc(nm_ready, 1)
                    if on(SEL):
                        q, b = s - SEL, (m - SEL) % 2
                        if on(SEL + 2):
                            dve.wait_ge(sums_ready, q - 1)
                        build_sel(q, sel[b], sel_ready)
                    if on(ADD):
                        q, b, slot = s - ADD, (m - ADD) % 2, (m - ADD) % RING
                        dve.wait_ge(sums_ready, q + 1)
                        dve.wait_ge(y_in[slot], nth(q, slot, RING))
                        if on(ADD + 2):
                            dve.wait_ge(v_ready, G * (q - 1))
                        nc.vector.tensor_tensor(a[b][:], sums[b][:], yin[:, slot, :, :], ALU.add).then_inc(a_ready, 1)
                    if on(MIX):
                        q, b, slot = s - MIX, (m - MIX) % 2, (m - MIX) % RING
                        dve.wait_ge(v_ready, G * (q + 1))
                        dve.wait_ge(xr_ready, G * (q + 1))
                        if on(MIX + 2):
                            dve.wait_ge(y_ready, G * (q - 1))
                        if bias_form:
                            nc.vector.tensor_tensor(u[b][:], v[b][:], tiles(cb2r), ALU.add).then_inc(mix, 1)
                        else:
                            nc.vector.scalar_tensor_tensor(out=u[b][:], in0=xr[:, slot % 4, :, :], scalar=(1.0 - keep) / copies,
                                                           in1=v[b][:], op0=ALU.mult, op1=ALU.add).then_inc(mix, 1)
                        dve.wait_ge(mix, 2 * q + 1)
                        nc.vector.scalar_tensor_tensor(out=u[b][:], in0=u[b][:], scalar=0.0,
                                                       in1=xr[:, slot % 4, :, :], op0=ALU.max,
                                                       op1=ALU.add).then_inc(mix, 1)
                        dve.wait_ge(mix, 2 * q + 2)
                        row_stats(dve, q, u[b], st[b], mv[b], rv[b], stat, passed)
                sweep(step, NORM - 1)(dve)

        general_sums(2, yz_t, False)
        propagate("gcn2_", yz_t, y1_t, y2_t, None)
        count_gathers(RING)
        general_sums(3, y2_t, False)
        propagate("appnp_", y2_t, y2_t, x3_t, 0.9)
        count_gathers(RING)

        def messages():
          SLOTS = 4
          with ExitStack() as ctx:
            sem, open_block = phase(ctx)

            def sb(name, shape, dt=F32):
                return ctx.enter_context(nc.sbuf_tensor("msg_" + name, shape, dt))

            def ps(name, shape):
                return ctx.enter_context(nc.psum_tensor("msg_" + name, shape, F32))

            rs, rd, ra = sb("rs", [R, D]), sb("rd", [R, D]), sb("ra", [R, 2 * EA + 1])
            rT = sb("rT", [P, 3, R])
            rh = sb("rh", [R, D])
            score, alpha, ab2c = (sb(n, [R, 1]) for n in ("score", "alpha", "ab2c"))
            aw2r = sb("aw2r", [R, D])
            comp_s, acomp = sb("comp_s", [R, B]), sb("acomp", [R, B])
            fold_i, fold = sb("fold_i", [P, G, R], I32), sb("fold", [P, G, R])
            band_i, band, inside = sb("band_i", [P, G], I32), sb("band", [P, G]), sb("inside", [P, G])
            table4 = sb("table4", [G * R, G, B])
            wa_s, wa_d = sb("wa_s", [D, D]), sb("wa_d", [D, D])
            wa_e = sb("wa_e", [2 * EA + 1, D])
            relw = sb("relw", [P, B, D])
            xs = sb("xs", [P, SLOTS * G, D])
            sidx = sb("sidx", [P, SLOTS * G], I32)
            hot = [sb(f"hot{i}", [P, G, R]) for i in range(2)]
            hotT = [sb(f"hotT{i}", [G * R, P]) for i in range(2)]
            xsT = sb("xsT", [P, 4, G * P])
            coef = sb("coef", [P, 4, G, B])
            DV = B // 2
            even, odd = ([sb(f"{n}{i}", [P, G, D]) for i in range(4)] for n in ("even", "odd"))
            parts = [sb(f"parts{i}", [P, B - DV, G, D]) for i in range(2)]
            rest = [sb(f"rest{i}", [P, G, D]) for i in range(2)]
            mo = [sb(f"mo{i}", [P, G, D]) for i in range(2)]
            xT_p = [ps(f"xT_p{i}", [P, G * P]) for i in range(2)]
            hot_p, coef_p = ps("hot_p", [P, 512]), ps("coef_p", [P, 512])
            rel = [ps(f"rel{i}", [P, B, D]) for i in range(2)]
            (w_in, consts, dve_step, r_turned, r_copied, r_hid, r_alpha, folded, idx_in, turn, passed, hot_ready,
             turned, xT_ready, hotT_ready, coef_done, coef_ready, rel_done, acc) = (sem("msg_" + n) for n in (
                "w_in", "consts", "dve_step", "r_turned", "r_copied", "r_hid", "r_alpha", "folded", "idx_in",
                "turn", "passed", "hot_ready", "turned", "xT_ready", "hotT_ready", "coef_done", "coef_ready",
                "rel_done", "acc"))
            turned_hot, scaled, rested, final = (sem("msg_" + n) for n in ("turned_hot", "scaled", "rested", "final"))
            m_out = [sem(f"msg_out{i}") for i in range(2)]
            src_in, r_in = landed[:SLOTS], landed[SLOTS]
            block = open_block()
            HOT, TURN, COEF, REL, REST, FINAL, STORE = 1, 2, 3, 4, 5, 6, 7
            WEIGHTS = 11

            @block.sync
            def _(sp):
                row = lambda a: a.rearrange("(p c) -> p c", p=1)
                for to, of in ((wa_s[:], aw1[0:D, :]), (wa_d[:], aw1[D:2 * D, :]), (wa_e[0:2 * EA, :], aw1[2 * D:, :]),
                               (wa_e[2 * EA:2 * EA + 1, :], row(ab1)), (ra[:, 0:EA], ea1[0:R, :]),
                               (ra[:, EA:2 * EA], ea2[0:R, :]), (comp_s[:], comp),
                               (aw2r[:], aw2.rearrange("d o -> o d").to_broadcast([R, D])),
                               (ab2c[:], row(ab2).to_broadcast([R, 1])),
                               (relw[:, 0:B // 2, :], rel_w[0:B // 2].rearrange("b d o -> d b o")),
                               (relw[:, B // 2:B, :], rel_w[B // 2:B].rearrange("b d o -> d b o"))):
                    sp.dma_start(to, of).then_inc(w_in, 16)

                def step(s, m, on):
                    if on(STORE):
                        q, b = s - STORE, (m - STORE) % 2
                        sp.wait_ge(final, 2 * (q + 1))
                        sp.dma_start(grouped(msg_t, q), mo[b][:]).then_inc(m_out[b], 16)
                sweep(step, STORE)(sp)
                for b in range(2):
                    sp.wait_ge(m_out[b], 16 * NG // 2)

            @block.gpsimd
            def _(pool):
                for rows, idx in ((rs, src_idx), (rd, dst_idx)):
                    nc.gpsimd.indirect_dma_start(
                        out=rows[:], out_offset=None, in_=x3_t[:, :],
                        in_offset=bass.IndirectOffsetOnAxis(ap=idx[0:R, 0:1], axis=0),
                        bounds_check=N - 1, oob_is_err=False).then_inc(r_in, 16)
                nc.gpsimd.iota(fold_i[:], pattern=[[0, G], [1, R]], base=0, channel_multiplier=0).then_inc(consts, 1)
                nc.gpsimd.iota(band_i[:], pattern=[[-R, G]], base=0, channel_multiplier=1).then_inc(consts, 1)

                def step(s, m, on):
                    if on(0):
                        slot = m % SLOTS
                        if on(SLOTS):
                            pool.wait_ge(turned, s - SLOTS + 1)
                        idx_gather(pool, s, slot, sidx, src_idx, (xs, x3_t), idx_in, src_in[slot], turn)
                    if on(REST):
                        q, b = s - REST, (m - REST) % 2
                        pool.wait_ge(scaled, (B - DV) * G * (q + 1))
                        if on(REST + 2):
                            pool.wait_ge(final, 2 * (q - 1))
                        half = parts[b][:, 0:2, :, :]
                        nc.gpsimd.tensor_tensor(half, half, parts[b][:, 2:4, :, :], ALU.add).then_inc(rested, 1)
                        pool.wait_ge(rested, 2 * q + 1)
                        nc.gpsimd.tensor_tensor(rest[b][:], parts[b][:, 0, :, :], parts[b][:, 1, :, :],
                                                ALU.add).then_inc(rested, 1)
                sweep(step, REST)(pool)

            @block.tensor
            def _(pe):
                pe.wait_ge(r_in, base[SLOTS] + 32)
                pe.wait_ge(w_in, 16 * WEIGHTS)
                pe.wait_ge(dve_step, 2)
                nc.tensor.transpose(xT_p[0][:, 0:R], rs[:], ident[0:R, 0:R])
                nc.tensor.transpose(xT_p[0][:, R:2 * R], rd[:], ident[0:R, 0:R])
                nc.tensor.transpose(xT_p[0][0:2 * EA + 1, 2 * R:3 * R], ra[:], ident[0:R, 0:R]).then_inc(r_turned, 1)
                pe.wait_ge(r_copied, 2)
                nc.tensor.matmul(xT_p[1][0:R, 0:D], rT[:, 0, :], wa_s[:], start=True, stop=False)
                nc.tensor.matmul(xT_p[1][0:R, 0:D], rT[:, 1, :], wa_d[:], start=False, stop=False)
                nc.tensor.matmul(xT_p[1][0:R, 0:D], rT[0:2 * EA + 1, 2, :], wa_e[:], start=False,
                                 stop=True).then_inc(r_hid, 1)
                pe.wait_ge(folded, 1)
                nc.tensor.matmul(coef_p[0:G * R, 0:B], fold[0:R, :, :].rearrange("p t r -> p (t r)"), acomp[:],
                                 start=True, stop=True).then_inc(r_hid, 1)

                def step(s, m, on):
                    if on(TURN):
                        q, b, slot = s - TURN, (m - TURN) % 2, (m - TURN) % SLOTS
                        pe.wait_ge(src_in[slot], base[slot] + nth(q, slot, SLOTS, 16 * G))
                        if on(TURN + 2):
                            pe.wait_ge(xT_ready, q - 1)
                        for t in range(G):
                            ins = nc.tensor.transpose(xT_p[b][:, t * P:(t + 1) * P], xs[:, slot * G + t, :], ident[:])
                        ins.then_inc(turned, 1)
                        pe.wait_ge(hot_ready, q + 1)
                        if on(TURN + 1):
                            pe.wait_ge(hotT_ready, q)
                        pe.sem_inc(passed, 1)
                        nc.tensor.transpose(hot_p[0:G * R, 0:P], hot[b][:].rearrange("p t r -> p (t r)"),
                                            ident[:]).then_inc(turned_hot, 1)
                    if on(COEF):
                        q, b = s - COEF, (m - COEF) % 2
                        pe.wait_ge(hotT_ready, q + 1)
                        if on(COEF + 1):
                            pe.wait_ge(coef_ready, q)
                        else:
                            pe.wait_ge(folded, 2)
                        nc.tensor.matmul(coef_p[:, 0:G * B], hotT[b][:], table4[:].rearrange("p t b -> p (t b)"),
                                         start=True, stop=True).then_inc(coef_done, 1)
                    if on(REL):
                        q, c = s - REL, (m - REL) % 4
                        pe.wait_ge(xT_ready, q + 1)
                        for t in range(G):
                            if on(REL + 1) or t >= 2:
                                pe.wait_ge(acc, DV * (G * q + t - 1))
                                pe.wait_ge(scaled, (B - DV) * (G * q + t - 1))
                            for h in range(2):
                                ins = nc.tensor.matmul(
                                    rel[t % 2][:, h * B // 2:(h + 1) * B // 2, :].rearrange("p b d -> p (b d)"),
                                    xsT[:, c, t * P:(t + 1) * P],
                                    relw[:, h * B // 2:(h + 1) * B // 2, :].rearrange("p b d -> p (b d)"),
                                    start=True, stop=True)
                            ins.then_inc(rel_done, 1)
                sweep(step, REL)(pe)

            @block.scalar
            def _(act):
                act.wait_ge(r_turned, 1)
                nc.scalar.copy(rT[:, 0:2, :], xT_p[0][:, 0:2 * R].rearrange("p (a r) -> p a r", a=2)).then_inc(r_copied, 1)
                nc.scalar.copy(rT[0:2 * EA + 1, 2, :], xT_p[0][0:2 * EA + 1, 2 * R:3 * R]).then_inc(r_copied, 1)
                act.wait_ge(r_hid, 1)
                nc.scalar.activation(rh[:], xT_p[1][0:R, 0:D], ACT.Relu).then_inc(r_alpha, 1)
                act.wait_ge(dve_step, 8)
                act.wait_ge(w_in, 16 * WEIGHTS)
                nc.scalar.activation(alpha[:], score[:], ACT.Sigmoid, bias=ab2c[:, 0:1]).then_inc(r_alpha, 1)

                def step(s, m, on):
                    if on(TURN):
                        q, b, c = s - TURN, (m - TURN) % 2, (m - TURN) % 4
                        act.wait_ge(turned, q + 1)
                        if on(TURN + 4):
                            act.wait_ge(rel_done, G * (q - 3))
                        nc.scalar.copy(xsT[:, c, :], xT_p[b][:]).then_inc(xT_ready, 1)
                        act.wait_ge(turned_hot, q + 1)
                        if on(TURN + 2):
                            act.wait_ge(coef_done, q - 1)
                        nc.scalar.copy(hotT[b][:], hot_p[0:G * R, 0:P]).then_inc(hotT_ready, 1)
                    if on(COEF):
                        q, c = s - COEF, (m - COEF) % 4
                        act.wait_ge(coef_done, q + 1)
                        if on(COEF + 4):
                            act.wait_ge(acc, DV * G * (q - 3))
                        nc.scalar.copy(coef[:, c, :, :], coef_p[:, 0:G * B].rearrange("p (t b) -> p t b", t=G)
                                       ).then_inc(coef_ready, 1)
                    if on(REL):
                        q, b, c = s - REL, (m - REL) % 2, (m - REL) % 4
                        act.wait_ge(coef_ready, q + 1)
                        if on(REL + 2):
                            act.wait_ge(rested, 2 * (q - 1))
                        for t in range(G):
                            act.wait_ge(rel_done, G * q + t + 1)
                            for i in range(DV, B):
                                nc.scalar.activation(parts[b][:, i - DV, t, :], rel[t % 2][:, i, :], ACT.Copy,
                                                     scale=coef[:, c, t, i:i + 1]).then_inc(scaled, 1)
                sweep(step, REL)(act)

            @block.vector
            def _(dve):
                n = [0]

                def then(ins):
                    n[0] += 1
                    ins.then_inc(dve_step, 1)
                    dve.wait_ge(dve_step, n[0])

                then(nc.vector.memset(ra[:, 2 * EA:2 * EA + 1], 1.0))
                dve.wait_ge(consts, 2)
                then(nc.vector.tensor_copy(fold[:], fold_i[:]))
                then(nc.vector.tensor_copy(band[:], band_i[:]))
                then(nc.vector.tensor_scalar(fold[:], fold[:], pidx[:, 0:1], None, ALU.is_equal))
                then(nc.vector.tensor_scalar(inside[:], band[:], 0.0, None, ALU.is_ge))
                then(nc.vector.scalar_tensor_tensor(out=inside[:], in0=band[:], scalar=float(R), in1=inside[:],
                                                    op0=ALU.is_lt, op1=ALU.mult))
                dve.wait_ge(r_alpha, 1)
                dve.wait_ge(w_in, 16 * WEIGHTS)
                then(nc.vector.tensor_tensor(rh[:], rh[:], aw2r[:], ALU.mult))
                then(nc.vector.tensor_reduce(score[:], rh[:], AX.X, ALU.add))
                dve.wait_ge(r_alpha, 2)
                nc.vector.tensor_scalar(acomp[:], comp_s[:], alpha[:, 0:1], None, ALU.mult).then_inc(folded, 1)
                dve.wait_ge(r_hid, 2)
                for t in range(G):
                    ins = nc.vector.tensor_scalar(table4[:, t, :], coef_p[0:G * R, 0:B], inside[0:G * R, t:t + 1], None,
                                                  ALU.mult)
                ins.then_inc(folded, 1)

                def step(s, m, on):
                    if on(HOT):
                        q, b = s - HOT, (m - HOT) % 2
                        if on(HOT + 2):
                            dve.wait_ge(turned_hot, q - 1)
                        nc.vector.tensor_tensor(
                            hot[b][:], typ[:, bass.ds(q * G, G)].unsqueeze(2).to_broadcast([P, G, R]),
                            iota_row[:, 0:R].unsqueeze(1).to_broadcast([P, G, R]), ALU.is_equal).then_inc(hot_ready, 1)
                    if on(FINAL):
                        q, b = s - FINAL, (m - FINAL) % 2
                        w = (m - FINAL) % 4
                        if on(FINAL + 2):
                            dve.wait_ge(m_out[b], nth(q - 2, b, 2))
                        dve.wait_ge(acc, DV * G * (q + 1))
                        nc.vector.tensor_tensor(mo[b][:], even[w][:], odd[w][:], ALU.add).then_inc(final, 1)
                        dve.wait_ge(final, 2 * q + 1)
                        dve.wait_ge(rested, 2 * (q + 1))
                        nc.vector.tensor_tensor(mo[b][:], mo[b][:], rest[b][:], ALU.add).then_inc(final, 1)
                    if on(REL):
                        q, b, c = s - REL, (m - REL) % 2, (m - REL) % 4
                        w = c
                        dve.wait_ge(coef_ready, q + 1)
                        for t in range(G):
                            dve.wait_ge(rel_done, G * q + t + 1)
                            for i in range(DV):
                                to = (even, odd)[i % 2][w][:, t, :]
                                if i < 2:
                                    ins = nc.vector.tensor_scalar(to, rel[t % 2][:, i, :], coef[:, c, t, i:i + 1], None,
                                                                  ALU.mult)
                                else:
                                    dve.wait_ge(acc, DV * (G * q + t) + i - 1)
                                    ins = nc.vector.scalar_tensor_tensor(
                                        out=to, in0=rel[t % 2][:, i, :], scalar=coef[:, c, t, i:i + 1], in1=to,
                                        op0=ALU.mult, op1=ALU.add)
                                ins.then_inc(acc, 1)
                sweep(step, FINAL)(dve)

        messages()
        general_sums(4, msg_t, True)

        def collect():
          with ExitStack() as ctx:
            sem, open_block = phase(ctx)

            def sb(name, shape, dt=F32):
                return ctx.enter_context(nc.sbuf_tensor("col_" + name, shape, dt))

            def ps(name, shape):
                return ctx.enter_context(nc.psum_tensor("col_" + name, shape, F32))

            ring = sb("ring", [P, RING * G, D + 1])
            xin = sb("xin", [P, RING, G, D])
            sel = [sb(f"sel{i}", [P, G * WIN, P]) for i in range(2)]
            xT = [sb(f"xT{i}", [P, G * P]) for i in range(2)]
            mc = [sb(f"mc{i}", [P, G, D]) for i in range(4)]
            u = [sb(f"u{i}", [P, G, D]) for i in range(2)]
            yo = [sb(f"yo{i}", [P, G, D]) for i in range(2)]
            small = lambda n: [sb(f"{n}{i}", [P, G]) for i in range(2)]
            st = [sb(f"st{i}", [P, G, 6]) for i in range(2)]
            mv = [sb(f"mv{i}", [P, G, 2]) for i in range(2)]
            rv, rs, nm = small("rv"), small("rs"), small("nm")
            sums = [ps(f"sums{i}", [P, G, D]) for i in range(2)]
            xTp, dp = ps("xTp", [P, G * P]), ps("dp", [P, G, D])
            (sel_ready, sums_ready, mc_ready, x_turned, xT_ready, d_done, d_read, mix, stat, rs_ready,
             nm_ready, y_ready, y_tail) = (sem("col_" + n) for n in (
                "sel_ready", "sums_ready", "mc_ready", "x_turned", "xT_ready", "d_done", "d_read", "mix",
                "stat", "rs_ready", "nm_ready", "y_ready", "y_tail"))
            msg_in = [sem(f"col_msg_in{i}") for i in range(RING)]
            x_in = [sem(f"col_x_in{i}") for i in range(RING)]
            y_out = [sem(f"col_y_out{i}") for i in range(2)]
            passed = sem("col_dve_passed")
            block = open_block()
            LOAD, SEL, SUM, TURN, UPD, MIX, NORM, STORE = 1, 1, 2, 3, 4, 5, 7, 8

            @block.sync
            def _(sp):
                def step(s, m, on):
                    if on(0):
                        if on(RING):
                            sp.wait_ge(sums_ready, s - RING + LAG_LO + 1)
                        sp.dma_start(ring[:, m * G:(m + 1) * G, 0:D], grouped(msg_t, s)).then_inc(msg_in[m], 16)
                    if on(LOAD):
                        q, slot = s - LOAD, (m - LOAD) % RING
                        if on(LOAD + RING):
                            sp.wait_ge(mix, q - RING + 1)
                        sp.dma_start(xin[:, slot, :, :], grouped(x3_t, q)).then_inc(x_in[slot], 16)
                    if on(STORE):
                        q, b = s - STORE, (m - STORE) % 2
                        sp.wait_ge(y_ready, G * (q + 1))
                        if isinstance(q, int) and q == NG - 1:
                            sp.dma_start(grouped(out, q, FULL * P), yo[b][:, 0:FULL, :]).then_inc(y_out[b], 16)
                            sp.dma_start(out[(q * G + FULL) * P:N, :], yo[b][0:REST, FULL, :]).then_inc(y_tail, 16)
                        else:
                            sp.dma_start(grouped(out, q), yo[b][:]).then_inc(y_out[b], 16)
                sweep(step, STORE)(sp)
                for b in range(2):
                    sp.wait_ge(y_out[b], 16 * NG // 2)
                sp.wait_ge(y_tail, 16)

            @block.tensor
            def _(pe):
                def step(s, m, on):
                    if on(SUM):
                        q, b = s - SUM, m % 2
                        where = windows(q)
                        if on(0):
                            pe.wait_ge(msg_in[m], nth(s, m, RING))
                        pe.wait_ge(sel_ready, q + 1)
                        if on(SUM + 2):
                            pe.wait_ge(mc_ready, q - 1)
                        window_sums(where, sel[b], ring, [sums[b][:, t, :] for t in range(G)], sums_ready)
                    if on(TURN):
                        q, slot = s - TURN, (m - TURN) % RING
                        pe.wait_ge(x_in[slot], nth(q, slot, RING))
                        if on(TURN + 1):
                            pe.wait_ge(xT_ready, q)
                        for t in range(G):
                            ins = nc.tensor.transpose(xTp[:, t * P:(t + 1) * P], xin[:, slot, t, :], ident[:])
                        ins.then_inc(x_turned, 1)
                    if on(UPD):
                        q, b = s - UPD, (m - UPD) % 2
                        pe.wait_ge(xT_ready, q + 1)
                        if on(UPD + 1):
                            pe.wait_ge(d_read, G * q)
                        for t in range(G):
                            ins = nc.tensor.matmul(dp[:, t, :], xT[b][:, t * P:(t + 1) * P], upd[:], start=True, stop=True)
                        ins.then_inc(d_done, 1)
                sweep(step, UPD)(pe)

            @block.scalar
            def _(act):
                def step(s, m, on):
                    if on(NORM):
                        q, b = s - NORM, (m - NORM) % 2
                        act.wait_ge(nm_ready, q + 1)
                        if on(NORM + 2):
                            act.wait_ge(y_out[b], nth(q - 2, b, 2))
                        for t in range(G):
                            nc.scalar.activation(yo[b][:, t, :], u[b][:, t, :], ACT.Identity, bias=nm[b][:, t:t + 1],
                                                 scale=rs[b][:, t:t + 1]).then_inc(y_ready, 1)
                    if on(TURN):
                        q, b, c = s - TURN, (m - TURN) % 2, (m - TURN) % 4
                        act.wait_ge(sums_ready, q + 1)
                        if on(TURN + 4):
                            act.wait_ge(d_read, G * (q - 3))
                        nc.scalar.copy(mc[c][:], sums[b][:]).then_inc(mc_ready, 1)
                        act.wait_ge(x_turned, q + 1)
                        if on(TURN + 2):
                            act.wait_ge(d_done, q - 1)
                        nc.scalar.copy(xT[b][:], xTp[:]).then_inc(xT_ready, 1)
                    if on(MIX):
                        q, b = s - MIX, (m - MIX) % 2
                        act.wait_ge(stat, 10 * (q + 1))
                        nc.scalar.activation(rs[b][:], rv[b][:], ACT.Sqrt).then_inc(rs_ready, 1)
                sweep(step, NORM)(act)

            @block.vector
            def _(dve):
                def step(s, m, on):
                    if on(NORM - 1):
                        q, b = s - NORM + 1, (m - NORM + 1) % 2
                        dve.wait_ge(rs_ready, q + 1)
                        nc.vector.scalar_tensor_tensor(out=nm[b][:], in0=mv[b][:, :, 0], scalar=-1.0, in1=rs[b][:],
                                                       op0=ALU.mult, op1=ALU.mult).then_inc(nm_ready, 1)
                    if on(SEL):
                        q, b = s - SEL, (m - SEL) % 2
                        if on(SEL + 2):
                            dve.wait_ge(sums_ready, q - 1)
                        build_sel(q, sel[b], sel_ready)
                    if on(MIX):
                        q, b, c, slot = s - MIX, (m - MIX) % 2, (m - MIX) % 4, (m - MIX) % RING
                        dve.wait_ge(d_done, q + 1)
                        dve.wait_ge(mc_ready, q + 1)
                        if on(MIX + 2):
                            dve.wait_ge(y_ready, G * (q - 1))
                        for t in range(G):
                            nc.vector.scalar_tensor_tensor(
                                out=u[b][:, t, :], in0=dp[:, t, :], scalar=cnt[:, bass.ds(q * G + t, 1)],
                                in1=mc[c][:, t, :], op0=ALU.mult, op1=ALU.add).then_inc(d_read, 1)
                        dve.wait_ge(d_read, G * (q + 1))
                        dve.wait_ge(x_in[slot], nth(q, slot, RING))
                        nc.vector.scalar_tensor_tensor(out=u[b][:], in0=u[b][:], scalar=0.0, in1=xin[:, slot, :, :],
                                                       op0=ALU.max, op1=ALU.add).then_inc(mix, 1)
                        dve.wait_ge(mix, q + 1)
                        row_stats(dve, q, u[b], st[b], mv[b], rv[b], stat, passed)
                sweep(step, NORM - 1)(dve)

        collect()


_OUT = ((50000, 128), "float32")


def kernel(**inputs):
    import numpy as _np
    import concourse.bacc as _bacc
    from concourse import mybir as _mybir
    from concourse.bass_utils import run_bass_kernel_spmd as _run

    nc = _bacc.Bacc("TRN2", target_bir_lowering=False, num_devices=1)
    names = ["x", "src", "dst", "edge_attr_32", "edge_attr_32_n2", "edge_type_16", "L0_gnn_eps", "L0_gnn_W1",
             "L0_gnn_b1", "L0_gnn_W2", "L0_gnn_b2", "L0_gnn_gamma", "L0_gnn_beta", "L1_gnn_W1", "L1_gnn_b1",
             "L1_gnn_W2", "L1_gnn_b2", "L3_gnn_weight", "L3_gnn_comp", "L3_gnn_attn_w1", "L3_gnn_attn_b1",
             "L3_gnn_attn_w2", "L3_gnn_attn_b2", "L3_gnn_update"]
    arrays, args = {}, []
    for name in names:
        a = _np.ascontiguousarray(inputs[name])
        if name == "L0_gnn_eps":
            a = a.reshape(1, 1)
        arrays["in_" + name] = a
        args.append(nc.dram_tensor("in_" + name, a.shape, _mybir.dt.from_np(a.dtype), kind="ExternalInput").ap())
    out = nc.dram_tensor("out_0", inputs["x"].shape, F32, kind="ExternalOutput").ap()
    build(nc, *args, out)
    r = _run(nc, [arrays], core_ids=[0])
    return r.results[0]["out_0"]
```

```python
from contextlib import ExitStack

import concourse.bass as bass
from concourse import mybir

F32 = mybir.dt.float32
I32 = mybir.dt.int32
ALU = mybir.AluOpType
ACT = mybir.ActivationFunctionType
AX = mybir.AxisListType

P = 128
G = 4
WIN = 3
RING = 8
UNROLL = 8
HEAD = 10
LAG_LO, LAG_HI = 1, 2
FAR = float(1 << 20)
LN_EPS = 1e-5


def build(nc, x, src, dst, ea1, ea2, etype, eps, W1, b1, W2, b2, gamma, beta,
          cW1, cb1, cW2, cb2, rel_w, comp, aw1, ab1, aw2, ab2, update, out):
    N, D = x.shape
    E = src.shape[0]
    R, B = comp.shape
    NG = -(-N // (P * G))
    NT = NG * G
    H2 = cW1.shape[1] // P
    EA = ea1.shape[1]
    assert D == P and B == 8 and NG == -(-E // (P * G)) and NG <= P and (NG - HEAD) % UNROLL == 0 and N == E
    FULL = N // P - (NG - 1) * G
    REST = N - (N // P) * P

    def table(name, width=D):
        return nc.dram_tensor(name, (NT * P, width), F32).ap()

    y1_t, yz_t, y2_t, x3_t, msg_t = (table(n) for n in ("y1_t", "yz_t", "y2_t", "x3_t", "msg_t"))
    agg_t = table("agg_t", D + 1)
    dstp_t = nc.dram_tensor("dst_rows", (NT, P), F32).ap()

    def grouped(ap2, q, rows=P * G):
        return ap2[bass.ds(q * (P * G), rows), :].rearrange("(t p) d -> p t d", p=P)

    def sweep(step, depth, head=HEAD):
        def at(s):
            step(s, s % UNROLL, lambda lag: 0 <= s - lag < NG)
        def run(eng):
            for s in range(head):
                at(s)
            with eng.Fori(head, NG - (UNROLL - 1), UNROLL) as s0:
                for u in range(UNROLL):
                    step(s0 + u, (head + u) % UNROLL, lambda lag: True)
            for s in range(NG, NG + depth):
                at(s)
        return run

    def nth(q, slot, ring, inc=16):
        return (q - slot) * (inc // ring) + inc

    with ExitStack() as whole:
        def hold(name, shape, dt=F32):
            return whole.enter_context(nc.sbuf_tensor(name, shape, dt))

        landed = [whole.enter_context(nc.semaphore(f"gathered{i}")) for i in range(RING)]
        any_rows, any_now, any_put = (whole.enter_context(nc.semaphore(n)) for n in ("any_rows", "any_now", "any_put"))
        base = [16 * G, 16 * G * WIN] + [0] * (RING - 2)

        def count_gathers(ring, first=0):
            for q in range(NG):
                base[first + q % ring] += 16 * G

        def phase(ctx):
            held = []

            def sem(name):
                held.append(ctx.enter_context(nc.semaphore(name)))
                return held[-1]

            def clear():
                for s in held:
                    nc.gpsimd.sem_clear(s)
                nc.all_engine_barrier()

            def open_block():
                ctx.callback(clear)
                return ctx.enter_context(nc.Block())
            return sem, open_block

        ident = hold("ident", [P, P])
        iota_row = hold("iota_row", [P, P])
        dst_win = hold("dst_win", [P, NT * WIN])
        src_idx = hold("src_idx", [P, NT + G * 2], I32)
        dst_idx = hold("dst_idx", [P, NT], I32)
        dst_col = hold("dst_col", [P, NT])
        typ = hold("typ", [P, NT])
        general = hold("general", [1, 1], I32)
        win_off = hold("win_off", [1, NG, G * WIN + 1], I32)
        cnt = hold("cnt", [P, NT])
        dinv = hold("dinv", [P, NT])
        sdeg = hold("sdeg", [P, NT])
        ones = hold("ones", [P, P])
        pidx = hold("pidx", [P, 1])
        ope = hold("ope", [P, 1])
        ope_i = hold("ope_i", [P, P])
        w1 = hold("w1", [P, D])
        w2 = hold("w2", [P, D])
        b1c = hold("b1c", [P, 1])
        b2r = hold("b2r", [P, D])
        gam = hold("gam", [P, D])
        bet = hold("bet", [P, D])
        cw1 = hold("cw1", [P, H2 * P])
        cw2 = hold("cw2", [P, H2, D])
        cb1c = hold("cb1c", [P, H2])
        cb2r = hold("cb2r", [P, D])
        upd = hold("upd", [P, D])

        with ExitStack() as ctx:
            sem, open_block = phase(ctx)

            def sb(name, shape, dt=F32):
                return ctx.enter_context(nc.sbuf_tensor(name, shape, dt))

            nat = [sb(n, [NG, G, P], I32) for n in ("nat_dst", "nat_src", "nat_typ")]
            natf = [sb(n, [NG, G, P]) for n in ("natf_dst", "natf_src", "natf_typ")]
            src_col = sb("src_col", [P, NT])
            iota_i = sb("iota_i", [P, P], I32)
            pidx_i = sb("pidx_i", [P, 1], I32)
            jfirst_i = sb("jfirst_i", [P, G], I32)
            jfirst = sb("jfirst", [P, G])
            klo_i = sb("klo_i", [P, 1], I32)
            klo = sb("klo", [P, 1])
            klim = sb("klim", [P, 2])
            total = sb("total", [P, WIN + 1])
            less = sb("less", [P, max(NT, P)])
            kh = sb("kh", [P, G])
            khi = sb("khi", [P, G], I32)
            rows = sb("rows", [P, G, P])
            under = sb("under", [P, G])
            k0 = sb("k0", [P, G])
            woff = sb("woff", [P, G * WIN + 1], I32)
            own_i, step_i = sb("own_i", [1, NT, WIN], I32), sb("step_i", [1, NT, WIN], I32)
            wki = sb("wki", [P, G * WIN], I32)
            wrows = sb("wrows", [P, G * WIN, P])
            epsc = sb("epsc", [P, 1])
            tp = [ctx.enter_context(nc.psum_tensor(f"tp{i}", [P, G, P], F32)) for i in range(3)]
            wtp = [ctx.enter_context(nc.psum_tensor(f"wtp{i}", [P, G, P], F32)) for i in range(3)]
            piv = ctx.enter_context(nc.psum_tensor("piv", [P, 512], F32))

            weights_in = sem("weights_in")
            pads_set = sem("pads_set")
            lists_in = sem("lists_in")
            consts_i = sem("consts_i")
            dve_step = sem("dve_step")
            ident_ready, lists_f, cols_ready, kh_ready, k0_ready, wk_ready, wrel_ready = (
                sem(n) for n in ("ident_ready", "lists_f", "cols_ready", "kh_ready", "k0_ready",
                                 "wk_ready", "wrel_ready"))
            turned = sem("turned")
            dst_rows_out = sem("dst_rows_out")
            pivots = sem("pivots")
            total_ready, summed, general_ready, own_set = (sem(n) for n in ("total_ready", "summed", "general_ready",
                                                                             "own_set"))
            rows_in, wrows_in = landed[0], landed[1]
            wturned = sem("wturned")
            win_in = sem("win_in")
            weights_all = 16 * (11 + H2)
            block = open_block()

            @block.sync
            def _(sp):
                sp.wait_ge(pads_set, 3)
                for a, t in zip((dst, src, etype), nat):
                    whole_rows = (E // P) - (G - 1) * NG
                    for c in range(G - 1):
                        sp.dma_start(t[:, c, :], a[c * NG * P:(c + 1) * NG * P].rearrange("(k e) -> k e", e=P)
                                     ).then_inc(lists_in, 16)
                    o = (G - 1) * NG * P
                    sp.dma_start(t[0:whole_rows, G - 1, :],
                                 a[o:o + whole_rows * P].rearrange("(k e) -> k e", e=P)).then_inc(lists_in, 16)
                    o += whole_rows * P
                    sp.dma_start(t[whole_rows:whole_rows + 1, G - 1, 0:REST],
                                 a[o:o + REST].rearrange("(k e) -> k e", k=1)).then_inc(lists_in, 16)

                def weight(to, of):
                    sp.dma_start(to, of).then_inc(weights_in, 16)

                col = lambda a: a.rearrange("(p c) -> p c", c=1)
                row = lambda a: a.rearrange("(p c) -> p c", p=1)
                spread = lambda a: row(a).to_broadcast([P, D])
                weight(w1[:], W1)
                weight(w2[:], W2)
                weight(b1c[:], col(b1))
                weight(b2r[:], spread(b2))
                weight(gam[:], spread(gamma))
                weight(bet[:], spread(beta))
                weight(epsc[:], eps.to_broadcast([P, 1]))
                weight(cw1[:], cW1)
                weight(cw2[:], cW2.rearrange("(h p) d -> p h d", p=P))
                for h in range(H2):
                    weight(cb1c[:, h:h + 1], col(cb1[h * P:(h + 1) * P]))
                weight(cb2r[:], spread(cb2))
                weight(upd[:], update)
                sp.wait_ge(lists_f, 1)
                sp.dma_start(dstp_t.rearrange("(c k) e -> k c e", k=NG), natf[0][:]).then_inc(dst_rows_out, 16)
                sp.wait_ge(weights_in, weights_all)
                sp.wait_ge(total_ready, 1)
                sp.dma_start(win_off[0:1, :, :], woff[0:NG, :]).then_inc(win_in, 16)
                sp.wait_ge(win_in, 16)

            @block.gpsimd
            def _(pool):
                nc.gpsimd.iota(iota_i[:], pattern=[[1, P]], base=0, channel_multiplier=0).then_inc(consts_i, 1)
                nc.gpsimd.iota(pidx_i[:], pattern=[[0, 1]], base=0, channel_multiplier=1).then_inc(consts_i, 1)
                nc.gpsimd.iota(jfirst_i[:], pattern=[[P, G]], base=0, channel_multiplier=P * G).then_inc(consts_i, 1)
                nc.gpsimd.iota(klo_i[:], pattern=[[0, 1]], base=0, channel_multiplier=G).then_inc(consts_i, 1)
                nc.gpsimd.iota(own_i[:], pattern=[[1, NT], [0, WIN]], base=0, channel_multiplier=0).then_inc(consts_i, 1)
                nc.gpsimd.iota(step_i[:], pattern=[[0, NT], [1, WIN]], base=0, channel_multiplier=0).then_inc(consts_i, 1)
                nc.gpsimd.memset(nat[0][:], int(FAR)).then_inc(pads_set, 1)
                nc.gpsimd.memset(nat[1][:], 0).then_inc(pads_set, 1)
                nc.gpsimd.memset(nat[2][:], 0).then_inc(pads_set, 1)
                pool.wait_ge(dst_rows_out, 16)
                pool.wait_ge(kh_ready, 1)
                for c in range(G):
                    nc.gpsimd.indirect_dma_start(
                        out=rows[0:NG, c, :], out_offset=None, in_=dstp_t[:, :],
                        in_offset=bass.IndirectOffsetOnAxis(ap=khi[0:NG, c:c + 1], axis=0),
                        bounds_check=NT - 1, oob_is_err=False).then_inc(rows_in, 16)
                pool.wait_ge(wk_ready, 1)
                for c in range(G * WIN):
                    nc.gpsimd.indirect_dma_start(
                        out=wrows[0:NG, c, :], out_offset=None, in_=dstp_t[:, :],
                        in_offset=bass.IndirectOffsetOnAxis(ap=wki[0:NG, c:c + 1], axis=0),
                        bounds_check=NT - 1, oob_is_err=False).then_inc(wrows_in, 16)
                pool.wait_ge(wrows_in, 16 * G * WIN)

            @block.vector
            def _(dve):
                n = [0]

                def then(ins, *ready):
                    n[0] += 1
                    ins.then_inc(dve_step, 1)
                    dve.wait_ge(dve_step, n[0])
                    for s in ready:
                        dve.sem_inc(s, 1)

                dve.wait_ge(consts_i, 6)
                then(nc.vector.tensor_copy(iota_row[:], iota_i[:]))
                then(nc.vector.tensor_copy(pidx[:], pidx_i[:]))
                then(nc.vector.tensor_scalar(ident[:], iota_row[:], pidx[:, 0:1], None, ALU.is_equal), ident_ready)
                then(nc.vector.tensor_copy(jfirst[:], jfirst_i[:]))
                then(nc.vector.tensor_copy(klo[:], klo_i[:]))
                then(nc.vector.memset(ones[:], 1.0))
                dve.wait_ge(lists_in, 16 * 3 * (G + 1))
                for i in range(3):
                    then(nc.vector.tensor_copy(natf[i][:], nat[i][:]), *([lists_f] if i == 2 else []))
                dve.wait_ge(turned, 3)
                for to, of in ((dst_col, tp[0]), (src_col, tp[1]), (typ, tp[2])):
                    then(nc.vector.tensor_copy(to[:].rearrange("e (c k) -> e c k", c=G), of[:, :, 0:NG]))
                then(nc.vector.memset(src_idx[:, NT:], 0))
                then(nc.vector.tensor_copy(src_idx[:, 0:NT], src_col[:]), cols_ready)
                then(nc.vector.tensor_scalar(dst_idx[:], dst_col[:], float(N - 1), None, ALU.min))
                dve.wait_ge(pivots, 1)
                for c in range(G):
                    then(nc.vector.tensor_scalar(less[:, 0:NT], piv[:, 0:NT], jfirst[:, c:c + 1], None, ALU.is_lt))
                    then(nc.vector.tensor_reduce(kh[:, c:c + 1], less[:, 0:NT], AX.X, ALU.add))
                then(nc.vector.tensor_scalar(kh[:], kh[:], -1.0, 0.0, ALU.add, ALU.max))
                then(nc.vector.tensor_copy(khi[:], kh[:]), kh_ready)
                then(nc.vector.memset(under[:], 0.0))
                dve.wait_ge(rows_in, 16 * G)
                for c in range(G):
                    then(nc.vector.tensor_scalar(less[0:NG, 0:P], rows[0:NG, c, :], jfirst[0:NG, c:c + 1], None,
                                                 ALU.is_lt))
                    then(nc.vector.tensor_reduce(under[0:NG, c:c + 1], less[0:NG, 0:P], AX.X, ALU.add))
                then(nc.vector.scalar_tensor_tensor(out=k0[:], in0=under[:], scalar=float(P), in1=kh[:],
                                                    op0=ALU.is_ge, op1=ALU.add))
                then(nc.vector.tensor_scalar(klim[:, 0:1], klo[:], -float(G * LAG_LO), 0.0, ALU.add, ALU.max))
                then(nc.vector.tensor_scalar(klim[:, 1:2], klo[:], float(G * (LAG_HI + 1) - WIN),
                                             float(NT - WIN), ALU.add, ALU.min))
                then(nc.vector.tensor_scalar(k0[:], k0[:], klim[:, 0:1], klim[:, 1:2], ALU.max, ALU.min))
                for c in range(G):
                    for i in range(WIN):
                        then(nc.vector.tensor_scalar(wki[:, c * WIN + i:c * WIN + i + 1], k0[:, c:c + 1],
                                                     float(i), None, ALU.add))
                dve.sem_inc(wk_ready, 1)
                offs = woff[:, 0:G * WIN]
                then(nc.vector.tensor_scalar(offs, wki[:], RING * G - 1, None, ALU.bitwise_and))
                then(nc.vector.tensor_scalar(offs, offs, float(D + 1), None, ALU.mult))
                dve.wait_ge(wrows_in, 16 * G * WIN)
                for c in range(G):
                    then(nc.vector.tensor_scalar(wrows[0:NG, c * WIN:(c + 1) * WIN, :],
                                                 wrows[0:NG, c * WIN:(c + 1) * WIN, :],
                                                 jfirst[0:NG, c:c + 1], None, ALU.subtract))
                dve.sem_inc(wrel_ready, 1)
                held = rows[0:NG, :, :]
                then(nc.vector.memset(total[:], 0.0))
                for i in range(WIN):
                    cut = wrows[0:NG, i:G * WIN:WIN, :]
                    then(nc.vector.tensor_scalar(held, cut, 0.0, None, ALU.is_ge))
                    then(nc.vector.scalar_tensor_tensor(out=held, in0=cut, scalar=float(P), in1=held,
                                                        op0=ALU.is_lt, op1=ALU.mult))
                    then(nc.vector.tensor_reduce(total[0:NG, i:i + 1], held.rearrange("p c e -> p (c e)"), AX.X,
                                                 ALU.add))
                then(nc.vector.tensor_copy(woff[:, G * WIN:], total[:, WIN - 1:WIN]))
                then(nc.vector.tensor_reduce(total[:, WIN:WIN + 1], total[:, 0:WIN], AX.X, ALU.add), total_ready)
                dve.wait_ge(summed, 1)
                then(nc.vector.tensor_scalar(general[:], piv[0:1, 0:1], float(E), None, ALU.not_equal), general_ready)
                dve.wait_ge(wturned, 1)
                for c in range(G * WIN):
                    to = c % WIN * G + c // WIN
                    then(nc.vector.tensor_copy(dst_win[:, to:NT * WIN:G * WIN], wtp[c // G][:, c % G, 0:NG]))
                dve.wait_ge(weights_in, weights_all)
                then(nc.vector.tensor_scalar(ope[:], epsc[:], 1.0, None, ALU.add))
                then(nc.vector.tensor_scalar(ope_i[:], ident[:], ope[:, 0:1], None, ALU.mult))
                with dve.If(dve.value_load(general[0:1, 0:1], min_val=0, max_val=1) > 0):
                    dve.wait_ge(win_in, 16)
                    nc.vector.memset(dst_win[:], FAR).then_inc(own_set, 1)
                    then(nc.vector.tensor_scalar(own_i[:], own_i[:], float(NT - WIN), None, ALU.min))
                    then(nc.vector.tensor_tensor(own_i[:], own_i[:], step_i[:], ALU.add))
                    then(nc.vector.tensor_scalar(own_i[:], own_i[:], RING * G - 1, None, ALU.bitwise_and))
                    nc.vector.tensor_scalar(win_off[:, :, 0:G * WIN],
                                            own_i[:].rearrange("p (g c) w -> p g (c w)", c=G), float(D + 1), None,
                                            ALU.mult).then_inc(own_set, 1)
                    nc.vector.memset(win_off[:, :, G * WIN:], 1).then_inc(own_set, 1)
                    dve.wait_ge(own_set, 3)
                    groups = dst_win[:].rearrange("p (g c) -> p g c", g=NG)
                    nc.vector.tensor_copy(groups[:, 0:NG - 1, 0:G],
                                          pidx[:, 0:1].unsqueeze(2).to_broadcast([P, NG - 1, G])).then_inc(own_set, 1)
                    for c in range(G):
                        i = max(0, c - (G - WIN))
                        to = (NG - 1) * G * WIN + i * G + c
                        nc.vector.tensor_copy(dst_win[:, to:to + 1], pidx[:]).then_inc(own_set, 1)
                with dve.Else():
                    dve.sem_inc(own_set, 1)

            @block.tensor
            def _(pe):
                pe.wait_ge(lists_f, 1)
                pe.wait_ge(ident_ready, 1)
                for i in range(3):
                    for c in range(G):
                        ins = nc.tensor.transpose(tp[i][:, c, 0:NG], natf[i][:, c, :], ident[0:NG, 0:NG])
                    ins.then_inc(turned, 1)
                pe.wait_ge(cols_ready, 1)
                nc.tensor.matmul(piv[:, 0:NT], ones[0:1, :], dst_col[0:1, :], start=True,
                                 stop=True).then_inc(pivots, 1)
                pe.wait_ge(wrel_ready, 1)
                for c in range(G * WIN):
                    ins = nc.tensor.transpose(wtp[c // G][:, c % G, 0:NG], wrows[0:NG, c, :], ident[0:NG, 0:NG])
                ins.then_inc(wturned, 1)
                pe.wait_ge(total_ready, 1)
                nc.tensor.matmul(piv[:, 0:1], ones[:], total[:, WIN:WIN + 1], start=True, stop=True).then_inc(summed, 1)

        def idx_gather(pool, q, u, m, idx, tabs, idx_in, slot_sem, turn):
            if u % 2 == 1 and (not isinstance(q, int) or q == HEAD - 1):
                to = (u + 1) % UNROLL * G
                nc.gpsimd.tensor_copy(idx[:, to:to + 2 * G], src_idx[:, bass.ds((q + 1) * G, 2 * G)]).then_inc(idx_in, 2)
            if not isinstance(q, int) and u % 2 == 0:
                pool.wait_ge(idx_in, q - (HEAD - 2))
                pool.sem_inc(turn, 1)
            for t in range(G):
                column = src_idx[:, q * G + t:q * G + t + 1] if isinstance(q, int) else idx[:, u * G + t:u * G + t + 1]
                nc.gpsimd.indirect_dma_start(
                    out=tabs[0][:, m * G + t, 0:D], out_offset=None, in_=tabs[1][:, :],
                    in_offset=bass.IndirectOffsetOnAxis(ap=column, axis=0),
                    bounds_check=N - 1, oob_is_err=False).then_inc(slot_sem, 16)

        def windows(q):
            return nc.values_load_multi_w_load_instructions(
                win_off[0:1, bass.ds(q, 1), :].rearrange("p g w -> p (g w)"), engines=[mybir.EngineType.PE], min_val=0,
                max_val=(RING * G - 1) * (D + 1),
                skip_runtime_bounds_check_because="setup takes them modulo the ring's size")[1]

        def first_groups(pe, q, slots, values):
            if isinstance(q, int) and q == 0:
                for slot, value in zip(slots, values):
                    pe.wait_ge(slot, value)

        def window_sums(pe, where, sel, ring, sums, done, own=None):
            rows = ring[:].rearrange("p k w -> p (k w)")

            def products(tiles_read):
                for t in range(G):
                    for i in range(tiles_read):
                        ins = nc.tensor.matmul(sums[t], sel[:, i * G + t, :],
                                               rows[:, bass.ds(where[t * WIN + i], sums[t].shape[-1])],
                                               start=(i == 0), stop=(i == tiles_read - 1 and own is None))
                    if own is not None:
                        ins = nc.tensor.matmul(sums[t], *own(t), start=False, stop=True)
                ins.then_inc(done, 1)
            with pe.If(where[G * WIN] > 0):
                products(WIN)
            with pe.Else():
                products(WIN - 1)

        def fill_ring(pool, tabs, slots, idx, idx_in, turn, free, width, beside=None, depth=0):
            def gather(s, m, on):
                if beside is not None:
                    beside(s, m, on)
                if on(0):
                    free(s, m, on)
                    idx_gather(pool, s, m, m, idx, tabs, idx_in, slots[m], turn)

            def load(s, m, on):
                if beside is not None:
                    beside(s, m, on)
                if on(0):
                    free(s, m, on)
                    nc.gpsimd.dma_start(tabs[0][:, m * G:(m + 1) * G, 0:width],
                                        grouped(agg_t, s)[:, :, 0:width]).then_inc(slots[m], 16 * G)

            with pool.If(pool.value_load(general[0:1, 0:1], min_val=0, max_val=1) > 0):
                sweep(load, depth)(pool)
            with pool.Else():
                sweep(gather, depth)(pool)

        def build_sel(dve, q, sel, done):
            def compare(first, n):
                return nc.vector.tensor_tensor(
                    sel[:, first:first + n, :],
                    dst_win[:, bass.ds(q * (G * WIN) + first, n)].unsqueeze(2).to_broadcast([P, n, P]),
                    iota_row[:].unsqueeze(1).to_broadcast([P, n, P]), ALU.is_equal)
            compare(0, G * (WIN - 1))
            last = win_off[0:1, bass.ds(q, 1), G * WIN:].rearrange("p g w -> p (g w)")
            with dve.If(dve.value_load(last, min_val=0, max_val=P * G) > 0):
                compare(G * (WIN - 1), G).then_inc(done, 1)
            with dve.Else():
                nc.vector.memset(sel[:, G * WIN - 1, 0:1], 0.0).then_inc(done, 1)

        def tile_stats(rows, st, step):
            for t in range(G):
                nc.vector.bn_stats(st[:, t, :], rows[:, t, :]).then_inc(step, 1)

        def merge_stats(dve, q, st, mv, step, passed):
            dve.wait_ge(step, q * 10 + 4)
            dve.sem_inc(passed, 1)
            for t in range(G):
                nc.vector.bn_aggr(mv[:, t, :], st[:, t, :]).then_inc(step, 1)

        def guard_var(dve, q, mv, rvar, step):
            dve.wait_ge(step, q * 10 + 8)
            nc.vector.tensor_scalar(rvar[:], mv[:, :, 1], LN_EPS, None, ALU.add).then_inc(step, 1)

        def invert_var(dve, q, rvar, step):
            dve.wait_ge(step, q * 10 + 9)
            nc.vector.reciprocal(rvar[:], rvar[:]).then_inc(step, 1)

        def tiles(a):
            return a[:].unsqueeze(1).to_broadcast([P, G, D])

        def flat(a):
            return a.rearrange("p t d -> p (t d)")

        def general_sums(n, from_t, by_edge):
          with ExitStack() as ctx:
            sem, open_block = phase(ctx)

            def sb(name, shape, dt=F32):
                return ctx.enter_context(nc.sbuf_tensor(f"any{n}_{name}", shape, dt))

            zeros = sb("zeros", [P, G, D + 1])
            rows, now, new = sb("rows", [P, D + 1]), sb("now", [P, D + 1]), sb("new", [P, D + 1])
            sidx, didx, widx = (sb(i, [P, 1], I32) for i in ("sidx", "didx", "widx"))
            col, dups, to = sb("col", [P, 1]), sb("dups", [P, 1]), sb("to", [P, 1])
            wide, same, before = sb("wide", [P, P]), sb("same", [P, P]), sb("before", [P, P])
            row_p = ctx.enter_context(nc.psum_tensor(f"any{n}_row", [P, P], F32))
            sum_p = ctx.enter_context(nc.psum_tensor(f"any{n}_sum", [P, D + 1], F32))
            zero_set, zeroed, idx_in, turn, round_open, dve_step, passed, rowed, summed, new_ready, copied = (
                sem(f"any{n}_" + i) for i in ("zero_set", "zeroed", "idx_in", "turn", "round_open", "dve_step", "passed", "rowed",
                                              "summed", "new_ready", "copied"))
            before_n = n * NT * 16
            block = open_block()

            @block.sync
            def _(sp):
                with sp.If(sp.value_load(general[0:1, 0:1], min_val=0, max_val=1) > 0):
                    sp.wait_ge(zero_set, 3)
                    for q in range(NG):
                        sp.dma_start(grouped(agg_t, q), zeros[:]).then_inc(zeroed, 16)
                    sp.wait_ge(zeroed, 16 * NG)
                    if by_edge:
                        sp.wait_ge(any_put, before_n + 16 * NT)
                        sp.dma_start(from_t[:, :], agg_t[:, 0:D]).then_inc(copied, 16)
                        sp.wait_ge(copied, 16)
                with sp.Else():
                    sp.sem_inc(passed, 1)

            @block.gpsimd
            def _(pool):
                with pool.If(pool.value_load(general[0:1, 0:1], min_val=0, max_val=1) > 0):
                    pool.wait_ge(zero_set, 3)
                    pool.wait_ge(zeroed, 16 * NG)
                    pool.sem_inc(round_open, 1)
                    with pool.Fori(0, NT, 1) as k:
                        nc.gpsimd.tensor_copy(sidx[:], src_idx[:, bass.ds(k, 1)]).then_inc(idx_in, 1)
                        nc.gpsimd.tensor_copy(didx[:], dst_idx[:, bass.ds(k, 1)]).then_inc(idx_in, 1)
                        pool.wait_ge(idx_in, 2 * k + 2)
                        pool.sem_inc(turn, 1)
                        if by_edge:
                            nc.gpsimd.dma_start(rows[:, 0:D], from_t[bass.ds(k * P, P), :]).then_inc(any_rows, 16)
                        else:
                            nc.gpsimd.indirect_dma_start(
                                out=rows[:, 0:D], out_offset=None, in_=from_t[:, :],
                                in_offset=bass.IndirectOffsetOnAxis(ap=sidx[:, 0:1], axis=0),
                                bounds_check=N - 1, oob_is_err=False).then_inc(any_rows, 16)
                        nc.gpsimd.indirect_dma_start(
                            out=now[:], out_offset=None, in_=agg_t[:, :],
                            in_offset=bass.IndirectOffsetOnAxis(ap=didx[:, 0:1], axis=0),
                            bounds_check=N - 1, oob_is_err=False).then_inc(any_now, 16)
                        pool.wait_ge(new_ready, k + 1)
                        pool.sem_inc(turn, 1)
                        nc.gpsimd.indirect_dma_start(
                            out=agg_t[:, :], out_offset=bass.IndirectOffsetOnAxis(ap=widx[:, 0:1], axis=0),
                            in_=new[:], in_offset=None, bounds_check=N - 1, oob_is_err=False).then_inc(any_put, 16)
                        pool.wait_ge(any_put, before_n + 16 * k + 16)
                        pool.sem_inc(round_open, 1)
                with pool.Else():
                    pool.sem_inc(turn, 1)

            @block.tensor
            def _(pe):
                with pe.If(pe.value_load(general[0:1, 0:1], min_val=0, max_val=1) > 0):
                    with pe.Fori(0, NT, 1) as k:
                        pe.wait_ge(dve_step, 7 * k + 2)
                        nc.tensor.transpose(row_p[:], wide[:], ident[:]).then_inc(rowed, 1)
                        pe.wait_ge(dve_step, 7 * k + 3)
                        pe.wait_ge(any_rows, before_n + 16 * k + 16)
                        nc.tensor.matmul(sum_p[:], same[:], rows[:], start=True, stop=True).then_inc(summed, 1)
                with pe.Else():
                    pe.sem_inc(rowed, 1)

            @block.vector
            def _(dve):
                with dve.If(dve.value_load(general[0:1, 0:1], min_val=0, max_val=1) > 0):
                    nc.vector.memset(zeros[:], 0.0).then_inc(zero_set, 1)
                    nc.vector.memset(rows[:, D:D + 1], 1.0).then_inc(zero_set, 1)
                    nc.vector.tensor_scalar(before[:], iota_row[:], pidx[:, 0:1], None, ALU.is_lt).then_inc(zero_set, 1)
                    dve.wait_ge(zero_set, 3)
                    with dve.Fori(0, NT, 1) as k:
                        def then(i, ins):
                            ins.then_inc(dve_step, 1)
                            dve.wait_ge(dve_step, 7 * k + i)
                            dve.sem_inc(passed, 1)
                        dve.wait_ge(round_open, k + 1)
                        dve.sem_inc(passed, 1)
                        then(1, nc.vector.tensor_copy(col[:], dst_col[:, bass.ds(k, 1)]))
                        then(2, nc.vector.tensor_copy(wide[:], col[:, 0:1].to_broadcast([P, P])))
                        dve.wait_ge(rowed, k + 1)
                        dve.sem_inc(passed, 1)
                        then(3, nc.vector.tensor_scalar(same[:], row_p[:], col[:, 0:1], None, ALU.is_equal))
                        then(4, nc.vector.tensor_tensor(wide[:], same[:], before[:], ALU.mult))
                        then(5, nc.vector.tensor_reduce(dups[:], wide[:], AX.X, ALU.add))
                        then(6, nc.vector.scalar_tensor_tensor(out=to[:], in0=dups[:], scalar=FAR, in1=col[:],
                                                               op0=ALU.mult, op1=ALU.add))
                        then(7, nc.vector.tensor_copy(widx[:], to[:]))
                        dve.wait_ge(summed, k + 1)
                        dve.wait_ge(any_now, before_n + 16 * k + 16)
                        dve.sem_inc(passed, 1)
                        nc.vector.tensor_tensor(new[:], now[:], sum_p[:], ALU.add).then_inc(new_ready, 1)
                with dve.Else():
                    dve.sem_inc(passed, 1)

        def gin_layer():
          W = D + 1
          with ExitStack() as ctx:
            sem, open_block = phase(ctx)

            def sb(name, shape, dt=F32):
                return ctx.enter_context(nc.sbuf_tensor("gin_" + name, shape, dt))

            def ps(name, shape):
                return ctx.enter_context(nc.psum_tensor("gin_" + name, shape, F32))

            ring = sb("ring", [P, RING * G, D + 1])
            idx = sb("idx", [P, UNROLL * G], I32)
            xin = sb("xin", [P, RING, G, D])
            bufs = lambda n, k, shape: [sb(f"{n}{i}", shape) for i in range(k)]
            sel = bufs("sel", 4, [P, G * WIN, P])
            agg = bufs("agg", 2, [P, G, W])
            xb = bufs("xb", 4, [P, G, D])
            zT, hT = bufs("zT", 2, [P, G * P]), bufs("hT", 2, [P, G * P])
            xn, yo = bufs("xn", 2, [P, G, D]), bufs("yo", 2, [P, G, D])
            u = bufs("u", 4, [P, G, D])
            st, mv = bufs("st", 2, [P, 2 * G, 6]), bufs("mv", 4, [P, 2 * G, 2])
            rv, rs = bufs("rv", 2, [P, 2 * G]), bufs("rs", 4, [P, 2 * G])
            nmA, nmB, rdB = bufs("nmA", 2, [P, G]), bufs("nmB", 2, [P, G]), bufs("rdB", 2, [P, G])
            sd, dv = bufs("sd", 2, [P, G]), bufs("dv", 2, [P, G])
            sums = ps("sums", [P, 2, 512])
            zTp, hTp = ps("zTp", [P, G * P]), ps("hTp", [P, G * P])
            rp = [ps(f"rp{i}", [P, G, D]) for i in range(4)]
            (ring_ones, idx_in, turn, sel_ready, sums_ready, agg_ready, cnt_ready, sd_ready, dinv_steps, xb_ready,
             zT_turned, zT_ready, h_done, hT_ready, r_done, stat, rs_ready, nmA_ready, nmB_ready, xn_ready, mix,
             y_ready, x_tail, sdeg_ready) = (sem("gin_" + n) for n in (
                "ring_ones", "idx_in", "turn", "sel_ready", "sums_ready", "agg_ready", "cnt_ready", "sd_ready",
                "dinv_steps", "xb_ready", "zT_turned", "zT_ready", "h_done", "hT_ready", "r_done", "stat", "rs_ready",
                "nmA_ready", "nmB_ready", "xn_ready", "mix", "y_ready", "x_tail", "sdeg_ready"))
            gathered = landed
            x_in = [sem(f"gin_x_in{i}") for i in range(RING)]
            y_out = [sem(f"gin_y_out{i}") for i in range(2)]
            passed, act_passed = sem("gin_dve_passed"), sem("gin_act_passed")
            block = open_block()
            LOAD, SEL, SUM, TURN, HID, RES, BIAS = 2, 1, 2, 3, 3, 4, 5
            STAT_A, NORM_A, MIX, STAT_B, NORM_B, STORE = 5, 6, 7, 8, 9, 10
            DEEP = HEAD + UNROLL

            def norms(on, later):
                return slice(0 if on(STAT_A + later) else G, 2 * G if on(STAT_B + later) else G)

            def x_landed(eng, q, slot):
                eng.wait_ge(x_in[slot], nth(q, slot, RING))
                if isinstance(q, int) and q == NG - 1:
                    eng.wait_ge(x_tail, 16)

            @block.sync
            def _(sp):
                def step(s, m, on):
                    if on(LOAD):
                        q, slot = s - LOAD, (m - LOAD) % RING
                        if on(LOAD + RING):
                            sp.wait_ge(mix, 3 * (q - RING) + 3)
                        if isinstance(q, int) and q == NG - 1:
                            sp.dma_start(xin[:, slot, 0:FULL, :], grouped(x, q, FULL * P)).then_inc(x_in[slot], 16)
                            sp.dma_start(xin[0:REST, slot, FULL, :], x[(q * G + FULL) * P:N, :]).then_inc(x_tail, 16)
                        else:
                            sp.dma_start(xin[:, slot, :, :], grouped(x, q)).then_inc(x_in[slot], 16)
                sweep(step, LOAD)(sp)

            @block.gpsimd
            def _(pool):
                nc.gpsimd.memset(ring[:, :, D:W], 1.0).then_inc(ring_ones, 1)
                pool.wait_ge(ring_ones, 1)

                def free(s, m, on):
                    if on(RING):
                        pool.wait_ge(sums_ready, s - RING + LAG_LO + 1)
                        pool.sem_inc(turn, 1)

                def biased(s, m, on):
                    if on(BIAS):
                        q, c, slot = s - BIAS, (m - BIAS) % 4, (m - BIAS) % RING
                        x_landed(pool, q, slot)
                        if on(BIAS + 4):
                            pool.wait_ge(r_done, q - 3)
                        nc.gpsimd.tensor_tensor(xb[c][:], xin[:, slot, :, :], tiles(b2r), ALU.add).then_inc(xb_ready, 1)
                fill_ring(pool, (ring, x), gathered, idx, idx_in, turn, free, W, biased, BIAS)

            @block.tensor
            def _(pe):
                pe.wait_ge(ring_ones, 1)

                def step(s, m, on):
                    if on(TURN):
                        q, b, slot = s - TURN, (m - TURN) % 2, (m - TURN) % RING
                        pe.wait_ge(agg_ready, q + 1)
                        x_landed(pe, q, slot)
                        if on(TURN + 1):
                            pe.wait_ge(zT_ready, q)
                        for t in range(G):
                            to = zTp[:, t * P:(t + 1) * P]
                            nc.tensor.matmul(to, agg[b][:, t, 0:D], ident[:], start=True, stop=False)
                            ins = nc.tensor.matmul(to, xin[:, slot, t, :], ope_i[:], start=False, stop=True)
                        ins.then_inc(zT_turned, 1)
                    if on(RES):
                        q, b, c = s - RES, (m - RES) % 2, (m - RES) % 4
                        pe.wait_ge(hT_ready, q + 1)
                        pe.wait_ge(xb_ready, q + 1)
                        if on(RES + 4):
                            pe.wait_ge(xn_ready, G * (q - 3))
                        for t in range(G):
                            nc.tensor.matmul(rp[c][:, t, :], ident[:], xb[c][:, t, :], start=True, stop=False)
                            ins = nc.tensor.matmul(rp[c][:, t, :], hT[b][:, t * P:(t + 1) * P], w2[:], start=False,
                                                   stop=True)
                        ins.then_inc(r_done, 1)
                    if on(SUM):
                        q = s - SUM
                        where = windows(q)
                        if on(0):
                            pe.wait_ge(gathered[m], base[m] + nth(s, m, RING, 16 * G))
                        first_groups(pe, q, gathered, [base[i] + 16 * G for i in range(LAG_HI)])
                        pe.wait_ge(sel_ready, q + 1)
                        if on(SUM + 1):
                            pe.wait_ge(agg_ready, q)
                        window_sums(pe, where, sel[(m - SUM) % 4], ring,
                                    [sums[:, t // 2, t % 2 * W:(t % 2 + 1) * W] for t in range(G)], sums_ready)
                    if on(HID):
                        q, b = s - HID, (m - HID) % 2
                        pe.wait_ge(zT_ready, q + 1)
                        if on(HID + 1):
                            pe.wait_ge(hT_ready, q)
                        nc.tensor.matmul(hTp[:], w1[:], zT[b][:], start=True, stop=True).then_inc(h_done, 1)
                sweep(step, RES)(pe)

            @block.scalar
            def _(act):
                def step(s, m, on):
                    if on(STORE):
                        q, b = s - STORE, (m - STORE) % 2
                        act.wait_ge(y_ready, G * (q + 1))
                        act.dma_start(grouped(y1_t, q), yo[b][:]).then_inc(y_out[b], 16)
                    if on(RES):
                        q, b = s - RES, (m - RES) % 2
                        act.wait_ge(h_done, q + 1)
                        if on(RES + 2):
                            act.wait_ge(r_done, q - 1)
                        nc.scalar.activation(hT[b][:], hTp[:], ACT.Relu, bias=b1c[:, 0:1]).then_inc(hT_ready, 1)
                    if on(NORM_A) or on(NORM_B):
                        k = s - NORM_A
                        now = norms(on, 1)
                        act.wait_ge(stat, 4 * (k + 1))
                        nc.scalar.activation(rs[(m - NORM_A) % 4][:, now], rv[(m - NORM_A) % 2][:, now],
                                             ACT.Sqrt).then_inc(rs_ready, 1)
                    if on(TURN):
                        q, b = s - TURN, (m - TURN) % 2
                        act.wait_ge(zT_turned, q + 1)
                        if on(TURN + 2):
                            act.wait_ge(h_done, q - 1)
                        nc.scalar.copy(zT[b][:], zTp[:]).then_inc(zT_ready, 1)
                        if on(TURN + 2):
                            act.wait_ge(dinv_steps, 2 * (q - 2) + 1)
                        nc.scalar.activation(sd[b][:], agg[b][:, :, D], ACT.Sqrt,
                                             bias=ones[:, 0:1]).then_inc(sd_ready, 1)
                    if on(NORM_A):
                        q, b, c = s - NORM_A, (m - NORM_A) % 2, (m - NORM_A) % 4
                        act.wait_ge(nmA_ready, q + 1)
                        if on(NORM_A + 2):
                            act.wait_ge(mix, 3 * (q - 2) + 1)
                        for t in range(G):
                            nc.scalar.activation(xn[b][:, t, :], rp[c][:, t, :], ACT.Identity, bias=nmA[b][:, t:t + 1],
                                                 scale=rs[c][:, t:t + 1]).then_inc(xn_ready, 1)
                    if on(NORM_B):
                        q, b = s - NORM_B, (m - NORM_B) % 2
                        act.wait_ge(nmB_ready, 2 * (q + 1))
                        if on(NORM_B + 2):
                            act.wait_ge(y_out[b], nth(q - 2, b, 2))
                        for t in range(G):
                            nc.scalar.activation(yo[b][:, t, :], u[(m - NORM_B) % 4][:, t, :], ACT.Identity,
                                                 bias=nmB[b][:, t:t + 1], scale=rdB[b][:, t:t + 1]).then_inc(y_ready, 1)
                    if on(SUM):
                        q, b = s - SUM, (m - SUM) % 2
                        act.wait_ge(sums_ready, q + 1)
                        if on(SUM + 2):
                            act.wait_ge(zT_turned, q - 1)
                            act.wait_ge(cnt_ready, q - 1)
                        nc.scalar.copy(agg[b][:].rearrange("p (h t) w -> p h (t w)", h=2),
                                       sums[:, :, 0:2 * W]).then_inc(agg_ready, 1)
                sweep(step, STORE, DEEP)(act)
                act.wait_ge(cnt_ready, NG)
                nc.scalar.activation(sdeg[:], cnt[:], ACT.Sqrt, bias=ones[:, 0:1]).then_inc(sdeg_ready, 1)
                act.wait_ge(sdeg_ready, 1)
                for b in range(2):
                    act.wait_ge(y_out[b], 16 * NG // 2)

            @block.vector
            def _(dve):
                def step(s, m, on):
                    k = s - STAT_A
                    now, any_stat = norms(on, 0), on(STAT_A) or on(STAT_B)
                    stk, mvk, rvk = st[(m - STAT_A) % 2], mv[(m - STAT_A) % 4], rv[(m - STAT_A) % 2]
                    mvl, rsl = mv[(m - NORM_A) % 4], rs[(m - NORM_A) % 4]
                    if on(SEL):
                        q = s - SEL
                        if on(SEL + 4):
                            dve.wait_ge(sums_ready, q - 3)
                        build_sel(dve, q, sel[(m - SEL) % 4], sel_ready)
                    if on(NORM_A) or on(NORM_B):
                        dve.wait_ge(rs_ready, s - NORM_A + 1)
                    if on(NORM_B):
                        q, b = s - NORM_B, (m - NORM_B) % 2
                        dve.wait_ge(dinv_steps, 2 * (q + 1))
                        if on(NORM_B + 2):
                            dve.wait_ge(y_ready, G * (q - 1))
                        nc.vector.tensor_tensor(rdB[b][:], rsl[:, G:], dinv[:, bass.ds(q * G, G)],
                                                ALU.mult).then_inc(nmB_ready, 1)
                    if on(NORM_A):
                        q, b = s - NORM_A, (m - NORM_A) % 2
                        if on(NORM_A + 2):
                            dve.wait_ge(xn_ready, G * (q - 1))
                        nc.vector.scalar_tensor_tensor(out=nmA[b][:], in0=mvl[:, 0:G, 0], scalar=-1.0, in1=rsl[:, 0:G],
                                                       op0=ALU.mult, op1=ALU.mult).then_inc(nmA_ready, 1)
                    if on(MIX):
                        q, b, c = s - MIX, (m - MIX) % 2, (m - MIX) % 4
                        dve.wait_ge(xn_ready, G * (q + 1))
                        if on(MIX + 4):
                            dve.wait_ge(y_ready, G * (q - 3))
                        nc.vector.tensor_tensor(u[c][:], xn[b][:], tiles(gam), ALU.mult).then_inc(mix, 1)
                    if on(NORM_B):
                        q, b = s - NORM_B, (m - NORM_B) % 2
                        dve.wait_ge(nmB_ready, 2 * q + 1)
                        nc.vector.scalar_tensor_tensor(out=nmB[b][:], in0=mvl[:, G:, 0], scalar=-1.0, in1=rdB[b][:],
                                                       op0=ALU.mult, op1=ALU.mult).then_inc(nmB_ready, 1)
                    if on(TURN):
                        q, b = s - TURN, (m - TURN) % 2
                        dve.wait_ge(agg_ready, q + 1)
                        nc.vector.tensor_copy(cnt[:, bass.ds(q * G, G)], agg[b][:, :, D]).then_inc(cnt_ready, 1)
                    if on(STAT_A):
                        q = s - STAT_A
                        dve.wait_ge(r_done, q + 1)
                        dve.sem_inc(passed, 1)
                        for t in range(G):
                            ins = nc.vector.bn_stats(stk[:, t, :], rp[(m - STAT_A) % 4][:, t, :])
                    if on(MIX):
                        q, c = s - MIX, (m - MIX) % 4
                        dve.wait_ge(mix, 3 * q + 1)
                        nc.vector.tensor_tensor(u[c][:], u[c][:], tiles(bet), ALU.add).then_inc(mix, 1)
                    if on(RES):
                        q, b = s - RES, (m - RES) % 2
                        dve.wait_ge(sd_ready, q + 1)
                        dve.sem_inc(passed, 1)
                        nc.vector.reciprocal(dv[b][:], sd[b][:]).then_inc(dinv_steps, 1)
                    if on(STAT_B):
                        q = s - STAT_B
                        dve.wait_ge(mix, 3 * (q + 1))
                        dve.sem_inc(passed, 1)
                        for t in range(G):
                            ins = nc.vector.bn_stats(stk[:, G + t, :], u[(m - STAT_B) % 4][:, t, :])
                    if any_stat:
                        ins.then_inc(stat, 1)
                    if on(MIX):
                        q, c, slot = s - MIX, (m - MIX) % 4, (m - MIX) % RING
                        dve.wait_ge(mix, 3 * q + 2)
                        nc.vector.scalar_tensor_tensor(out=u[c][:], in0=u[c][:], scalar=0.0, in1=xin[:, slot, :, :],
                                                       op0=ALU.max, op1=ALU.add).then_inc(mix, 1)
                    if any_stat:
                        dve.wait_ge(stat, 4 * k + 1)
                        dve.sem_inc(passed, 1)
                        for t in range(now.start, now.stop):
                            ins = nc.vector.bn_aggr(mvk[:, t, :], stk[:, t, :])
                        ins.then_inc(stat, 1)
                    if on(RES):
                        q, b = s - RES, (m - RES) % 2
                        dve.wait_ge(dinv_steps, 2 * q + 1)
                        nc.vector.tensor_copy(dinv[:, bass.ds(q * G, G)], dv[b][:]).then_inc(dinv_steps, 1)
                    if any_stat:
                        dve.wait_ge(stat, 4 * k + 2)
                        nc.vector.tensor_scalar(rvk[:, now], mvk[:, now, 1], LN_EPS, None, ALU.add).then_inc(stat, 1)
                        dve.wait_ge(stat, 4 * k + 3)
                        dve.sem_inc(passed, 1)
                        nc.vector.reciprocal(rvk[:, now], rvk[:, now]).then_inc(stat, 1)
                sweep(step, NORM_B, DEEP)(dve)

        general_sums(0, x, False)
        gin_layer()
        count_gathers(RING)
        def gcn_hidden():
          with ExitStack() as ctx:
            sem, open_block = phase(ctx)

            def sb(name, shape, dt=F32):
                return ctx.enter_context(nc.sbuf_tensor("gcn_" + name, shape, dt))

            def ps(name, shape):
                return ctx.enter_context(nc.psum_tensor("gcn_" + name, shape, F32))

            ring = sb("ring", [P, RING * G, D + 1])
            idx = sb("idx", [P, UNROLL * G], I32)
            yin = sb("yin", [P, RING, G, D])
            sel = [sb(f"sel{i}", [P, G * WIN, P]) for i in range(2)]
            own = [sb(f"own{i}", [P, G, D]) for i in range(2)]
            a = [sb(f"a{i}", [P, G, D]) for i in range(2)]
            aT = [sb(f"aT{i}", [P, G * P]) for i in range(2)]
            hT = [sb(f"hT{i}", [P, H2, G * P]) for i in range(2)]
            yo = [sb(f"yo{i}", [P, G, D]) for i in range(2)]
            sums = [ps(f"sums{i}", [P, G, D]) for i in range(2)]
            aTp, hTp, zp = ps("aTp", [P, G * P]), ps("hTp", [P, H2, G * P]), ps("zp", [P, G, D])
            (idx_in, turn, sel_ready, sums_ready, own_ready, a_ready, aT_turned, aT_ready, h_done, hT_ready, z_done,
             y_ready) = (sem("gcn_" + n) for n in (
                "idx_in", "turn", "sel_ready", "sums_ready", "own_ready", "a_ready", "aT_turned", "aT_ready",
                "h_done", "hT_ready", "z_done", "y_ready"))
            gathered = landed
            y_in = [sem(f"gcn_y_in{i}") for i in range(RING)]
            y_out = [sem(f"gcn_y_out{i}") for i in range(2)]
            act_passed = sem("gcn_act_passed")
            block = open_block()
            LOAD, SEL, SUM, TURN, HID, OUT, STORE = 1, 1, 2, 3, 4, 5, 6

            @block.sync
            def _(sp):
                def step(s, m, on):
                    if on(LOAD):
                        q, slot = s - LOAD, (m - LOAD) % RING
                        if on(LOAD + RING):
                            sp.wait_ge(own_ready, G * (q - RING + 1))
                        sp.dma_start(yin[:, slot, :, :], grouped(y1_t, q)).then_inc(y_in[slot], 16)
                sweep(step, LOAD)(sp)

            @block.gpsimd
            def _(pool):
                def free(s, m, on):
                    if on(RING):
                        pool.wait_ge(sums_ready, s - RING + LAG_LO + 1)
                        pool.sem_inc(turn, 1)
                fill_ring(pool, (ring, y1_t), gathered, idx, idx_in, turn, free, D)

            @block.tensor
            def _(pe):
                def step(s, m, on):
                    if on(SUM):
                        q, b = s - SUM, m % 2
                        where = windows(q)
                        if on(0):
                            pe.wait_ge(gathered[m], base[m] + nth(s, m, RING, 16 * G))
                        first_groups(pe, q, gathered, [base[i] + 16 * G for i in range(LAG_HI)])
                        pe.wait_ge(sel_ready, q + 1)
                        if on(SUM + 2):
                            pe.wait_ge(a_ready, G * (q - 1))
                        window_sums(pe, where, sel[b], ring, [sums[b][:, t, :] for t in range(G)], sums_ready)
                    if on(TURN):
                        q, b = s - TURN, (m - TURN) % 2
                        pe.wait_ge(a_ready, G * (q + 1))
                        if on(TURN + 1):
                            pe.wait_ge(aT_ready, q)
                        for t in range(G):
                            ins = nc.tensor.transpose(aTp[:, t * P:(t + 1) * P], a[b][:, t, :], ident[:])
                        ins.then_inc(aT_turned, 1)
                    if on(HID):
                        q, b = s - HID, (m - HID) % 2
                        pe.wait_ge(aT_ready, q + 1)
                        if on(HID + 1):
                            pe.wait_ge(hT_ready, H2 * q)
                        for h in range(H2):
                            nc.tensor.matmul(hTp[:, h, :], cw1[:, h * P:(h + 1) * P], aT[b][:], start=True,
                                             stop=True).then_inc(h_done, 1)
                    if on(OUT):
                        q, b = s - OUT, (m - OUT) % 2
                        pe.wait_ge(hT_ready, H2 * (q + 1))
                        if on(OUT + 1):
                            pe.wait_ge(y_ready, G * q)
                        for t in range(G):
                            for h in range(H2):
                                ins = nc.tensor.matmul(zp[:, t, :], hT[b][:, h, t * P:(t + 1) * P], cw2[:, h, :],
                                                       start=(h == 0), stop=(h == H2 - 1))
                        ins.then_inc(z_done, 1)
                sweep(step, OUT)(pe)

            @block.scalar
            def _(act):
                def step(s, m, on):
                    if on(STORE):
                        q, b = s - STORE, (m - STORE) % 2
                        act.wait_ge(y_ready, G * (q + 1))
                        act.dma_start(grouped(yz_t, q), yo[b][:]).then_inc(y_out[b], 16)
                    if on(SUM):
                        q, b, slot = s - SUM, m % 2, (m - SUM) % RING
                        act.wait_ge(y_in[slot], nth(q, slot, RING))
                        if on(SUM + 2):
                            act.wait_ge(a_ready, G * (q - 1))
                        act.sem_inc(act_passed, 1)
                        for t in range(G):
                            nc.scalar.activation(own[b][:, t, :], yin[:, slot, t, :], ACT.Copy,
                                                 scale=dinv[:, bass.ds(q * G + t, 1)]).then_inc(own_ready, 1)
                    if on(TURN):
                        q, b = s - TURN, (m - TURN) % 2
                        act.wait_ge(aT_turned, q + 1)
                        if on(TURN + 2):
                            act.wait_ge(h_done, H2 * (q - 1))
                        nc.scalar.copy(aT[b][:], aTp[:]).then_inc(aT_ready, 1)
                    if on(HID):
                        q, b = s - HID, (m - HID) % 2
                        if on(HID + 2):
                            act.wait_ge(z_done, q - 1)
                        for h in range(H2):
                            act.wait_ge(h_done, H2 * q + h + 1)
                            nc.scalar.activation(hT[b][:, h, :], hTp[:, h, :], ACT.Relu,
                                                 bias=cb1c[:, h:h + 1]).then_inc(hT_ready, 1)
                    if on(OUT):
                        q, b = s - OUT, (m - OUT) % 2
                        act.wait_ge(z_done, q + 1)
                        if on(OUT + 2):
                            act.wait_ge(y_out[b], nth(q - 2, b, 2))
                        act.sem_inc(act_passed, 1)
                        for t in range(G):
                            nc.scalar.activation(yo[b][:, t, :], zp[:, t, :], ACT.Copy,
                                                 scale=dinv[:, bass.ds(q * G + t, 1)]).then_inc(y_ready, 1)
                sweep(step, STORE)(act)
                for b in range(2):
                    act.wait_ge(y_out[b], 16 * NG // 2)

            @block.vector
            def _(dve):
                def step(s, m, on):
                    if on(SEL):
                        q, b = s - SEL, (m - SEL) % 2
                        if on(SEL + 2):
                            dve.wait_ge(sums_ready, q - 1)
                        build_sel(dve, q, sel[b], sel_ready)
                    if on(TURN):
                        q, b = s - TURN, (m - TURN) % 2
                        dve.wait_ge(sums_ready, q + 1)
                        dve.wait_ge(own_ready, G * (q + 1))
                        if on(TURN + 2):
                            dve.wait_ge(aT_turned, q - 1)
                        for t in range(G):
                            nc.vector.scalar_tensor_tensor(
                                out=a[b][:, t, :], in0=sums[b][:, t, :], scalar=dinv[:, bass.ds(q * G + t, 1)],
                                in1=own[b][:, t, :], op0=ALU.mult, op1=ALU.add).then_inc(a_ready, 1)
                sweep(step, TURN)(dve)

        general_sums(1, y1_t, False)
        gcn_hidden()
        count_gathers(RING)

        def propagate(pre, from_t, res_t, to_t, keep):
          bias_form = keep is None
          with ExitStack() as ctx:
            sem, open_block = phase(ctx)

            def sb(name, shape, dt=F32):
                return ctx.enter_context(nc.sbuf_tensor(pre + name, shape, dt))

            def ps(name, shape):
                return ctx.enter_context(nc.psum_tensor(pre + name, shape, F32))

            ring = sb("ring", [P, RING * G, D + 1])
            idx = sb("idx", [P, UNROLL * G], I32)
            yin = sb("yin", [P, RING, G, D])
            rin = sb("rin", [P, RING, G, D]) if bias_form else yin
            sel = [sb(f"sel{i}", [P, G * WIN, P]) for i in range(4)]
            v = [sb(f"v{i}", [P, G, D]) for i in range(2)]
            xr = sb("xr", [P, 4, G, D])
            u = [sb(f"u{i}", [P, G, D]) for i in range(4)]
            yo = [sb(f"yo{i}", [P, G, D]) for i in range(2)]
            small = lambda n: [sb(f"{n}{i}", [P, G]) for i in range(2)]
            st = [sb(f"st{i}", [P, G, 6]) for i in range(2)]
            mv = [sb(f"mv{i}", [P, G, 2]) for i in range(4)]
            rv, rs, rd, nm = small("rv"), small("rs"), small("rd"), small("nm")
            dscale = sb("dscale", [P, NT])
            rscale = sb("rscale", [P, NT])
            copies = 1.0 if bias_form else 2.0
            sums = [ps(f"sums{i}", [P, G, D]) for i in range(2)]
            (idx_in, turn, sel_ready, sums_ready, xr_ready, v_ready, mix, stat, rs_ready, nm_ready, y_ready,
             scale_ready) = (sem(pre + n) for n in (
                "idx_in", "turn", "sel_ready", "sums_ready", "xr_ready", "v_ready", "mix", "stat",
                "rs_ready", "nm_ready", "y_ready", "scale_ready"))
            gathered = landed
            y_in = [sem(f"{pre}y_in{i}") for i in range(RING)]
            r_in = [sem(f"{pre}r_in{i}") for i in range(RING)] if bias_form else y_in
            y_out = [sem(f"{pre}y_out{i}") for i in range(2)]
            passed, act_passed = sem(pre + "dve_passed"), sem(pre + "act_passed")
            block = open_block()
            LOAD, SEL, SUM, SCALE, MIX, STAT, ROOT, SHIFT, NORM, STORE = 1, 1, 2, 3, 4, 5, 6, 7, 8, 9

            @block.sync
            def _(sp):
                def step(s, m, on):
                    if on(LOAD):
                        q, slot = s - LOAD, (m - LOAD) % RING
                        if on(LOAD + RING):
                            sp.wait_ge(xr_ready, G * (q - RING + 1))
                            sp.wait_ge(sums_ready, q - RING + 1)
                        sp.dma_start(yin[:, slot, :, :], grouped(from_t, q)).then_inc(y_in[slot], 16)
                        if bias_form:
                            sp.dma_start(rin[:, slot, :, :], grouped(res_t, q)).then_inc(r_in[slot], 16)
                sweep(step, LOAD)(sp)

            @block.gpsimd
            def _(pool):
                def free(s, m, on):
                    if on(RING):
                        pool.wait_ge(sums_ready, s - RING + LAG_LO + 1)
                        pool.sem_inc(turn, 1)
                fill_ring(pool, (ring, from_t), gathered, idx, idx_in, turn, free, D)

            @block.tensor
            def _(pe):
                def step(s, m, on):
                    if on(SUM):
                        q, b, slot = s - SUM, m % 2, (m - SUM) % RING
                        where = windows(q)
                        if on(0):
                            pe.wait_ge(gathered[m], base[m] + nth(s, m, RING, 16 * G))
                        first_groups(pe, q, gathered, [base[i] + 16 * G for i in range(LAG_HI)])
                        pe.wait_ge(sel_ready, q + 1)
                        if on(SUM + 2):
                            pe.wait_ge(v_ready, G * (q - 1))
                        pe.wait_ge(y_in[slot], nth(q, slot, RING))
                        window_sums(pe, where, sel[(m - SUM) % 4], ring, [sums[b][:, t, :] for t in range(G)], sums_ready,
                                    lambda t: (ident[:], yin[:, slot, t, :]))
                sweep(step, SUM)(pe)

            @block.scalar
            def _(act):
                act.wait_ge(scale_ready, 2)

                def step(s, m, on):
                    if on(STORE):
                        q, b = s - STORE, (m - STORE) % 2
                        act.wait_ge(y_ready, G * (q + 1))
                        act.dma_start(grouped(to_t, q), yo[b][:]).then_inc(y_out[b], 16)
                    if on(NORM):
                        q, b, c = s - NORM, (m - NORM) % 2, (m - NORM) % 4
                        act.wait_ge(nm_ready, 2 * (q + 1))
                        if on(NORM + 2):
                            act.wait_ge(y_out[b], nth(q - 2, b, 2))
                        for t in range(G):
                            nc.scalar.activation(yo[b][:, t, :], u[c][:, t, :], ACT.Identity, bias=nm[b][:, t:t + 1],
                                                 scale=rd[b][:, t:t + 1]).then_inc(y_ready, 1)
                    if on(SUM):
                        q, slot = s - SUM, (m - SUM) % RING
                        act.wait_ge(r_in[slot], nth(q, slot, RING))
                        if on(SUM + 4):
                            act.wait_ge(mix, 2 * (q - 3))
                        act.sem_inc(act_passed, 1)
                        for t in range(G):
                            nc.scalar.activation(xr[:, slot % 4, t, :], rin[:, slot, t, :], ACT.Copy,
                                                 scale=rscale[:, bass.ds(q * G + t, 1)]).then_inc(xr_ready, 1)
                    if on(SCALE):
                        q, b = s - SCALE, (m - SCALE) % 2
                        act.wait_ge(sums_ready, q + 1)
                        if on(SCALE + 2):
                            act.wait_ge(mix, 2 * (q - 2) + 1)
                        act.sem_inc(act_passed, 1)
                        for t in range(G):
                            nc.scalar.activation(v[b][:, t, :], sums[b][:, t, :], ACT.Copy,
                                                 scale=dscale[:, bass.ds(q * G + t, 1)]).then_inc(v_ready, 1)
                    if on(ROOT):
                        q, b = s - ROOT, (m - ROOT) % 2
                        act.wait_ge(stat, 10 * (q + 1))
                        nc.scalar.activation(rs[b][:], rv[b][:], ACT.Sqrt).then_inc(rs_ready, 1)
                sweep(step, STORE)(act)
                for b in range(2):
                    act.wait_ge(y_out[b], 16 * NG // 2)

            @block.vector
            def _(dve):
                nc.vector.tensor_scalar(dscale[:], dinv[:], 1.0 if bias_form else keep, None,
                                        ALU.mult).then_inc(scale_ready, 1)
                nc.vector.tensor_scalar(rscale[:], sdeg[:], copies, None, ALU.mult).then_inc(scale_ready, 1)

                def step(s, m, on):
                    if on(SHIFT):
                        q, b = s - SHIFT, (m - SHIFT) % 2
                        dve.wait_ge(rs_ready, q + 1)
                        if on(SHIFT + 2):
                            dve.wait_ge(y_ready, G * (q - 1))
                        if bias_form:
                            nc.vector.tensor_tensor(rd[b][:], rs[b][:], dinv[:, bass.ds(q * G, G)],
                                                    ALU.mult).then_inc(nm_ready, 1)
                        else:
                            nc.vector.tensor_copy(rd[b][:], rs[b][:]).then_inc(nm_ready, 1)
                    if on(MIX):
                        q, b, c = s - MIX, (m - MIX) % 2, (m - MIX) % 4
                        dve.wait_ge(v_ready, G * (q + 1))
                        dve.wait_ge(xr_ready, G * (q + 1))
                        if on(MIX + 4):
                            dve.wait_ge(y_ready, G * (q - 3))
                        if bias_form:
                            nc.vector.tensor_tensor(u[c][:], v[b][:], tiles(cb2r), ALU.add).then_inc(mix, 1)
                        else:
                            nc.vector.scalar_tensor_tensor(out=u[c][:], in0=xr[:, c, :, :], scalar=(1.0 - keep) / copies,
                                                           in1=v[b][:], op0=ALU.mult, op1=ALU.add).then_inc(mix, 1)
                    if on(STAT):
                        q, b = s - STAT, (m - STAT) % 2
                        dve.wait_ge(mix, 2 * (q + 1))
                        dve.sem_inc(passed, 1)
                        tile_stats(u[(m - STAT) % 4], st[b], stat)
                    if on(SHIFT):
                        q, b = s - SHIFT, (m - SHIFT) % 2
                        dve.wait_ge(nm_ready, 2 * q + 1)
                        nc.vector.scalar_tensor_tensor(out=nm[b][:], in0=mv[(m - SHIFT) % 4][:, :, 0], scalar=-1.0,
                                                       in1=rd[b][:], op0=ALU.mult, op1=ALU.mult).then_inc(nm_ready, 1)
                    if on(STAT):
                        q, b, c = s - STAT, (m - STAT) % 2, (m - STAT) % 4
                        merge_stats(dve, q, st[b], mv[c], stat, passed)
                    if on(MIX):
                        q, c = s - MIX, (m - MIX) % 4
                        dve.wait_ge(mix, 2 * q + 1)
                        nc.vector.scalar_tensor_tensor(out=u[c][:], in0=u[c][:], scalar=0.0, in1=xr[:, c, :, :],
                                                       op0=ALU.max, op1=ALU.add).then_inc(mix, 1)
                    if on(STAT):
                        q, b, c = s - STAT, (m - STAT) % 2, (m - STAT) % 4
                        guard_var(dve, q, mv[c], rv[b], stat)
                    if on(SEL):
                        q = s - SEL
                        if on(SEL + 4):
                            dve.wait_ge(sums_ready, q - 3)
                        build_sel(dve, q, sel[(m - SEL) % 4], sel_ready)
                    if on(STAT):
                        q, b = s - STAT, (m - STAT) % 2
                        invert_var(dve, q, rv[b], stat)
                sweep(step, SHIFT)(dve)

        general_sums(2, yz_t, False)
        propagate("gcn2_", yz_t, y1_t, y2_t, None)
        count_gathers(RING)
        general_sums(3, y2_t, False)
        propagate("appnp_", y2_t, y2_t, x3_t, 0.9)
        count_gathers(RING)

        def messages():
          SLOTS = 4
          with ExitStack() as ctx:
            sem, open_block = phase(ctx)

            def sb(name, shape, dt=F32):
                return ctx.enter_context(nc.sbuf_tensor("msg_" + name, shape, dt))

            def ps(name, shape):
                return ctx.enter_context(nc.psum_tensor("msg_" + name, shape, F32))

            rs, rd, ra = sb("rs", [R, D]), sb("rd", [R, D]), sb("ra", [R, 2 * EA + 1])
            rT = sb("rT", [P, 3, R])
            rh = sb("rh", [R, D])
            score, alpha, ab2c = (sb(n, [R, 1]) for n in ("score", "alpha", "ab2c"))
            aw2r = sb("aw2r", [R, D])
            comp_s, acomp = sb("comp_s", [R, B]), sb("acomp", [R, B])
            fold_i, fold = sb("fold_i", [P, G, R], I32), sb("fold", [P, G, R])
            band_i, band, inside = sb("band_i", [P, G], I32), sb("band", [P, G]), sb("inside", [P, G])
            table4 = sb("table4", [G * R, G, B])
            wa_s, wa_d = sb("wa_s", [D, D]), sb("wa_d", [D, D])
            wa_e = sb("wa_e", [2 * EA + 1, D])
            relw = sb("relw", [P, B, D])
            xs = sb("xs", [P, SLOTS * G, D])
            sidx = sb("sidx", [P, UNROLL * G], I32)
            hot = [sb(f"hot{i}", [P, G, R]) for i in range(2)]
            hotT = [sb(f"hotT{i}", [G * R, P]) for i in range(2)]
            xsT = sb("xsT", [P, 4, G * P])
            coef = sb("coef", [P, 4, G, B])
            DV = B // 2
            even, odd = ([sb(f"{n}{i}", [P, G, D]) for i in range(4)] for n in ("even", "odd"))
            parts = [sb(f"parts{i}", [P, B - DV, G, D]) for i in range(4)]
            mo = [sb(f"mo{i}", [P, G, D]) for i in range(2)]
            xT_p = [ps(f"xT_p{i}", [P, G * P]) for i in range(2)]
            hot_p, coef_p = ps("hot_p", [P, 512]), ps("coef_p", [P, 512])
            rel = [ps(f"rel{i}", [P, B, D]) for i in range(2)]
            (w_in, consts, dve_step, r_turned, r_copied, r_hid, r_alpha, folded, idx_in, turn, passed, hot_ready,
             turned, xT_ready, hotT_ready, coef_done, coef_ready, rel_done, acc) = (sem("msg_" + n) for n in (
                "w_in", "consts", "dve_step", "r_turned", "r_copied", "r_hid", "r_alpha", "folded", "idx_in",
                "turn", "passed", "hot_ready", "turned", "xT_ready", "hotT_ready", "coef_done", "coef_ready",
                "rel_done", "acc"))
            turned_hot, scaled, rested, final = (sem("msg_" + n) for n in ("turned_hot", "scaled", "rested", "final"))
            m_out = [sem(f"msg_out{i}") for i in range(2)]
            src_in, r_in = landed[:SLOTS], landed[SLOTS]
            block = open_block()
            HOT, TURN, COEF, REL, REST, FINAL, STORE = 1, 2, 3, 4, 5, 6, 7
            WEIGHTS = 11

            @block.sync
            def _(sp):
                row = lambda a: a.rearrange("(p c) -> p c", p=1)
                for to, of in ((wa_s[:], aw1[0:D, :]), (wa_d[:], aw1[D:2 * D, :]), (wa_e[0:2 * EA, :], aw1[2 * D:, :]),
                               (wa_e[2 * EA:2 * EA + 1, :], row(ab1)), (ra[:, 0:EA], ea1[0:R, :]),
                               (ra[:, EA:2 * EA], ea2[0:R, :]), (comp_s[:], comp),
                               (aw2r[:], aw2.rearrange("d o -> o d").to_broadcast([R, D])),
                               (ab2c[:], row(ab2).to_broadcast([R, 1])),
                               (relw[:, 0:B // 2, :], rel_w[0:B // 2].rearrange("b d o -> d b o")),
                               (relw[:, B // 2:B, :], rel_w[B // 2:B].rearrange("b d o -> d b o"))):
                    sp.dma_start(to, of).then_inc(w_in, 16)

                def step(s, m, on):
                    if on(STORE):
                        q, b = s - STORE, (m - STORE) % 2
                        sp.wait_ge(final, 3 * (q + 1))
                        sp.dma_start(grouped(msg_t, q), mo[b][:]).then_inc(m_out[b], 16)
                sweep(step, STORE)(sp)
                for b in range(2):
                    sp.wait_ge(m_out[b], 16 * NG // 2)

            @block.gpsimd
            def _(pool):
                for rows, idx in ((rs, src_idx), (rd, dst_idx)):
                    nc.gpsimd.indirect_dma_start(
                        out=rows[:], out_offset=None, in_=x3_t[:, :],
                        in_offset=bass.IndirectOffsetOnAxis(ap=idx[0:R, 0:1], axis=0),
                        bounds_check=N - 1, oob_is_err=False).then_inc(r_in, 16)
                nc.gpsimd.iota(fold_i[:], pattern=[[0, G], [1, R]], base=0, channel_multiplier=0).then_inc(consts, 1)
                nc.gpsimd.iota(band_i[:], pattern=[[-R, G]], base=0, channel_multiplier=1).then_inc(consts, 1)

                def step(s, m, on):
                    if on(0):
                        slot = m % SLOTS
                        if on(SLOTS):
                            pool.wait_ge(turned, s - SLOTS + 1)
                            pool.sem_inc(turn, 1)
                        idx_gather(pool, s, m, slot, sidx, (xs, x3_t), idx_in, src_in[slot], turn)
                    if on(REST):
                        q, w = s - REST, (m - REST) % 4
                        pool.wait_ge(scaled, (B - DV) * G * (q + 1))
                        half = parts[w][:, 0:2, :, :]
                        nc.gpsimd.tensor_tensor(half, half, parts[w][:, 2:4, :, :], ALU.add).then_inc(rested, 1)
                sweep(step, REST)(pool)

            @block.tensor
            def _(pe):
                pe.wait_ge(r_in, base[SLOTS] + 32)
                pe.wait_ge(w_in, 16 * WEIGHTS)
                pe.wait_ge(dve_step, 2)
                nc.tensor.transpose(xT_p[0][:, 0:R], rs[:], ident[0:R, 0:R])
                nc.tensor.transpose(xT_p[0][:, R:2 * R], rd[:], ident[0:R, 0:R])
                nc.tensor.transpose(xT_p[0][0:2 * EA + 1, 2 * R:3 * R], ra[:], ident[0:R, 0:R]).then_inc(r_turned, 1)
                pe.wait_ge(r_copied, 2)
                nc.tensor.matmul(xT_p[1][0:R, 0:D], rT[:, 0, :], wa_s[:], start=True, stop=False)
                nc.tensor.matmul(xT_p[1][0:R, 0:D], rT[:, 1, :], wa_d[:], start=False, stop=False)
                nc.tensor.matmul(xT_p[1][0:R, 0:D], rT[0:2 * EA + 1, 2, :], wa_e[:], start=False,
                                 stop=True).then_inc(r_hid, 1)
                pe.wait_ge(folded, 1)
                nc.tensor.matmul(coef_p[0:G * R, 0:B], fold[0:R, :, :].rearrange("p t r -> p (t r)"), acomp[:],
                                 start=True, stop=True).then_inc(r_hid, 1)

                def step(s, m, on):
                    if on(TURN):
                        q, b, slot = s - TURN, (m - TURN) % 2, (m - TURN) % SLOTS
                        pe.wait_ge(src_in[slot], base[slot] + nth(q, slot, SLOTS, 16 * G))
                        if on(TURN + 2):
                            pe.wait_ge(xT_ready, q - 1)
                        for t in range(G):
                            ins = nc.tensor.transpose(xT_p[b][:, t * P:(t + 1) * P], xs[:, slot * G + t, :], ident[:])
                        ins.then_inc(turned, 1)
                        pe.wait_ge(hot_ready, q + 1)
                        if on(TURN + 1):
                            pe.wait_ge(hotT_ready, q)
                        pe.sem_inc(passed, 1)
                        nc.tensor.transpose(hot_p[0:G * R, 0:P], hot[b][:].rearrange("p t r -> p (t r)"),
                                            ident[:]).then_inc(turned_hot, 1)
                    if on(COEF):
                        q, b = s - COEF, (m - COEF) % 2
                        pe.wait_ge(hotT_ready, q + 1)
                        if on(COEF + 1):
                            pe.wait_ge(coef_ready, q)
                        else:
                            pe.wait_ge(folded, 2)
                        nc.tensor.matmul(coef_p[:, 0:G * B], hotT[b][:], table4[:].rearrange("p t b -> p (t b)"),
                                         start=True, stop=True).then_inc(coef_done, 1)
                    if on(REL):
                        q, c = s - REL, (m - REL) % 4
                        pe.wait_ge(xT_ready, q + 1)
                        for t in range(G):
                            if on(REL + 1) or t >= 2:
                                pe.wait_ge(acc, DV * (G * q + t - 1))
                                pe.wait_ge(scaled, (B - DV) * (G * q + t - 1))
                            for h in range(2):
                                ins = nc.tensor.matmul(
                                    rel[t % 2][:, h * B // 2:(h + 1) * B // 2, :].rearrange("p b d -> p (b d)"),
                                    xsT[:, c, t * P:(t + 1) * P],
                                    relw[:, h * B // 2:(h + 1) * B // 2, :].rearrange("p b d -> p (b d)"),
                                    start=True, stop=True)
                            ins.then_inc(rel_done, 1)
                sweep(step, REL)(pe)

            @block.scalar
            def _(act):
                act.wait_ge(r_turned, 1)
                nc.scalar.copy(rT[:, 0:2, :], xT_p[0][:, 0:2 * R].rearrange("p (a r) -> p a r", a=2)).then_inc(r_copied, 1)
                nc.scalar.copy(rT[0:2 * EA + 1, 2, :], xT_p[0][0:2 * EA + 1, 2 * R:3 * R]).then_inc(r_copied, 1)
                act.wait_ge(r_hid, 1)
                nc.scalar.activation(rh[:], xT_p[1][0:R, 0:D], ACT.Relu).then_inc(r_alpha, 1)
                act.wait_ge(dve_step, 8)
                act.wait_ge(w_in, 16 * WEIGHTS)
                nc.scalar.activation(alpha[:], score[:], ACT.Sigmoid, bias=ab2c[:, 0:1]).then_inc(r_alpha, 1)

                def step(s, m, on):
                    if on(TURN):
                        q, b, c = s - TURN, (m - TURN) % 2, (m - TURN) % 4
                        act.wait_ge(turned, q + 1)
                        if on(TURN + 4):
                            act.wait_ge(rel_done, G * (q - 3))
                        nc.scalar.copy(xsT[:, c, :], xT_p[b][:]).then_inc(xT_ready, 1)
                        act.wait_ge(turned_hot, q + 1)
                        if on(TURN + 2):
                            act.wait_ge(coef_done, q - 1)
                        nc.scalar.copy(hotT[b][:], hot_p[0:G * R, 0:P]).then_inc(hotT_ready, 1)
                    if on(COEF):
                        q, c = s - COEF, (m - COEF) % 4
                        act.wait_ge(coef_done, q + 1)
                        if on(COEF + 4):
                            act.wait_ge(acc, DV * G * (q - 3))
                        nc.scalar.copy(coef[:, c, :, :], coef_p[:, 0:G * B].rearrange("p (t b) -> p t b", t=G)
                                       ).then_inc(coef_ready, 1)
                    if on(REL):
                        q, c = s - REL, (m - REL) % 4
                        act.wait_ge(coef_ready, q + 1)
                        if on(REL + 4):
                            act.wait_ge(final, 3 * (q - 3))
                        for t in range(G):
                            act.wait_ge(rel_done, G * q + t + 1)
                            for i in range(DV, B):
                                nc.scalar.activation(parts[c][:, i - DV, t, :], rel[t % 2][:, i, :], ACT.Copy,
                                                     scale=coef[:, c, t, i:i + 1]).then_inc(scaled, 1)
                sweep(step, REL)(act)

            @block.vector
            def _(dve):
                n = [0]

                def then(ins):
                    n[0] += 1
                    ins.then_inc(dve_step, 1)
                    dve.wait_ge(dve_step, n[0])

                then(nc.vector.memset(ra[:, 2 * EA:2 * EA + 1], 1.0))
                dve.wait_ge(consts, 2)
                then(nc.vector.tensor_copy(fold[:], fold_i[:]))
                then(nc.vector.tensor_copy(band[:], band_i[:]))
                then(nc.vector.tensor_scalar(fold[:], fold[:], pidx[:, 0:1], None, ALU.is_equal))
                then(nc.vector.tensor_scalar(inside[:], band[:], 0.0, None, ALU.is_ge))
                then(nc.vector.scalar_tensor_tensor(out=inside[:], in0=band[:], scalar=float(R), in1=inside[:],
                                                    op0=ALU.is_lt, op1=ALU.mult))
                dve.wait_ge(r_alpha, 1)
                dve.wait_ge(w_in, 16 * WEIGHTS)
                then(nc.vector.tensor_tensor(rh[:], rh[:], aw2r[:], ALU.mult))
                then(nc.vector.tensor_reduce(score[:], rh[:], AX.X, ALU.add))
                dve.wait_ge(r_alpha, 2)
                nc.vector.tensor_scalar(acomp[:], comp_s[:], alpha[:, 0:1], None, ALU.mult).then_inc(folded, 1)
                dve.wait_ge(r_hid, 2)
                for t in range(G):
                    ins = nc.vector.tensor_scalar(table4[:, t, :], coef_p[0:G * R, 0:B], inside[0:G * R, t:t + 1], None,
                                                  ALU.mult)
                ins.then_inc(folded, 1)

                def step(s, m, on):
                    if on(HOT):
                        q, b = s - HOT, (m - HOT) % 2
                        if on(HOT + 2):
                            dve.wait_ge(turned_hot, q - 1)
                        nc.vector.tensor_tensor(
                            hot[b][:], typ[:, bass.ds(q * G, G)].unsqueeze(2).to_broadcast([P, G, R]),
                            iota_row[:, 0:R].unsqueeze(1).to_broadcast([P, G, R]), ALU.is_equal).then_inc(hot_ready, 1)
                    for t in range(G):
                        if on(REL):
                            q, c = s - REL, (m - REL) % 4
                            if t == 0:
                                dve.wait_ge(coef_ready, q + 1)
                            dve.wait_ge(rel_done, G * q + t + 1)
                            for i in range(DV):
                                to = (even, odd)[i % 2][c][:, t, :]
                                if i < 2:
                                    ins = nc.vector.tensor_scalar(to, rel[t % 2][:, i, :], coef[:, c, t, i:i + 1], None,
                                                                  ALU.mult)
                                else:
                                    dve.wait_ge(acc, DV * (G * q + t) + i - 1)
                                    ins = nc.vector.scalar_tensor_tensor(
                                        out=to, in0=rel[t % 2][:, i, :], scalar=coef[:, c, t, i:i + 1], in1=to,
                                        op0=ALU.mult, op1=ALU.add)
                                ins.then_inc(acc, 1)
                        if on(FINAL) and t < 3:
                            q, b, w = s - FINAL, (m - FINAL) % 2, (m - FINAL) % 4
                            if t == 0:
                                if on(FINAL + 2):
                                    dve.wait_ge(m_out[b], nth(q - 2, b, 2))
                                dve.wait_ge(acc, DV * G * (q + 1))
                                terms = even[w], odd[w][:]
                            else:
                                dve.wait_ge(final, 3 * q + t)
                                dve.wait_ge(rested, q + 1)
                                terms = mo[b], parts[w][:, t - 1, :, :]
                            nc.vector.tensor_tensor(mo[b][:], terms[0][:], terms[1], ALU.add).then_inc(final, 1)
                sweep(step, FINAL)(dve)

        messages()
        general_sums(4, msg_t, True)

        def collect():
          with ExitStack() as ctx:
            sem, open_block = phase(ctx)

            def sb(name, shape, dt=F32):
                return ctx.enter_context(nc.sbuf_tensor("col_" + name, shape, dt))

            def ps(name, shape):
                return ctx.enter_context(nc.psum_tensor("col_" + name, shape, F32))

            ring = sb("ring", [P, RING * G, D + 1])
            xin = sb("xin", [P, RING, G, D])
            sel = [sb(f"sel{i}", [P, G * WIN, P]) for i in range(4)]
            xc = [sb(f"xc{i}", [P, G, D]) for i in range(2)]
            xT = [sb(f"xT{i}", [P, G * P]) for i in range(2)]
            u = [sb(f"u{i}", [P, G, D]) for i in range(4)]
            yo = [sb(f"yo{i}", [P, G, D]) for i in range(2)]
            st = [sb(f"st{i}", [P, G, 6]) for i in range(2)]
            mv = [sb(f"mv{i}", [P, G, 2]) for i in range(4)]
            rv, rs, nm = ([sb(f"{n}{i}", [P, G]) for i in range(k)] for n, k in (("rv", 2), ("rs", 4), ("nm", 2)))
            sums, xTp = ([ps(f"{n}{i}", [P, G, D]) for i in range(2)] for n in ("sums", "xTp"))
            (sel_ready, sums_ready, xc_ready, x_turned, xT_ready, mix, stat, rs_ready, nm_ready, y_ready,
             y_tail) = (sem("col_" + n) for n in (
                "sel_ready", "sums_ready", "xc_ready", "x_turned", "xT_ready", "mix", "stat", "rs_ready", "nm_ready",
                "y_ready", "y_tail"))
            msg_in = [sem(f"col_msg_in{i}") for i in range(RING)]
            x_in = [sem(f"col_x_in{i}") for i in range(RING)]
            y_out = [sem(f"col_y_out{i}") for i in range(2)]
            passed = sem("col_dve_passed")
            block = open_block()
            COUNT, SEL, TURN, SUM, MIX, STAT, ROOT, SHIFT, NORM, STORE = 1, 1, 2, 3, 4, 5, 6, 7, 8, 9
            LATE = SUM - LAG_HI

            @block.sync
            def _(sp):
                def step(s, m, on):
                    if on(0):
                        if on(RING):
                            sp.wait_ge(mix, s - RING + 1)
                        sp.dma_start(xin[:, m, :, :], grouped(x3_t, s)).then_inc(x_in[m], 16)
                        if on(RING):
                            sp.wait_ge(sums_ready, s - RING + LAG_LO + 1)
                        sp.dma_start(ring[:, m * G:(m + 1) * G, 0:D], grouped(msg_t, s)).then_inc(msg_in[m], 16)
                sweep(step, 0)(sp)

            @block.gpsimd
            def _(pool):
                def step(s, m, on):
                    if on(COUNT):
                        q, b, slot = s - COUNT, (m - COUNT) % 2, (m - COUNT) % RING
                        pool.wait_ge(x_in[slot], nth(q, slot, RING))
                        if on(COUNT + 2):
                            pool.wait_ge(x_turned, q - 1)
                        nc.gpsimd.tensor_tensor(xc[b][:], xin[:, slot, :, :],
                                                cnt[:, bass.ds(q * G, G)].unsqueeze(2).to_broadcast([P, G, D]),
                                                ALU.mult).then_inc(xc_ready, 1)
                sweep(step, COUNT)(pool)

            @block.tensor
            def _(pe):
                def step(s, m, on):
                    if on(TURN):
                        q, b = s - TURN, (m - TURN) % 2
                        pe.wait_ge(xc_ready, q + 1)
                        if on(TURN + 2):
                            pe.wait_ge(xT_ready, q - 1)
                        for t in range(G):
                            ins = nc.tensor.transpose(xTp[b][:, t, :], xc[b][:, t, :], ident[:])
                        ins.then_inc(x_turned, 1)
                    if on(SUM):
                        q, b = s - SUM, (m - SUM) % 2
                        where = windows(q)
                        if on(LATE):
                            last = (m - LATE) % RING
                            pe.wait_ge(msg_in[last], nth(s - LATE, last, RING))
                        first_groups(pe, q, msg_in, [16] * LAG_HI)
                        pe.wait_ge(sel_ready, q + 1)
                        pe.wait_ge(xT_ready, q + 1)
                        if on(SUM + 2):
                            pe.wait_ge(mix, q - 1)
                        window_sums(pe, where, sel[(m - SUM) % 4], ring, [sums[b][:, t, :] for t in range(G)], sums_ready,
                                    lambda t: (xT[b][:, t * P:(t + 1) * P], upd[:]))
                sweep(step, SUM)(pe)

            @block.scalar
            def _(act):
                def step(s, m, on):
                    if on(STORE):
                        q, b = s - STORE, (m - STORE) % 2
                        act.wait_ge(y_ready, G * (q + 1))
                        if isinstance(q, int) and q == NG - 1:
                            act.dma_start(grouped(out, q, FULL * P), yo[b][:, 0:FULL, :]).then_inc(y_out[b], 16)
                            act.dma_start(out[(q * G + FULL) * P:N, :], yo[b][0:REST, FULL, :]).then_inc(y_tail, 16)
                        else:
                            act.dma_start(grouped(out, q), yo[b][:]).then_inc(y_out[b], 16)
                    if on(NORM):
                        q, b, c = s - NORM, (m - NORM) % 2, (m - NORM) % 4
                        act.wait_ge(nm_ready, q + 1)
                        if on(NORM + 2):
                            act.wait_ge(y_out[b], nth(q - 2, b, 2))
                        for t in range(G):
                            nc.scalar.activation(yo[b][:, t, :], u[c][:, t, :], ACT.Identity, bias=nm[b][:, t:t + 1],
                                                 scale=rs[c][:, t:t + 1]).then_inc(y_ready, 1)
                    if on(ROOT):
                        q, b = s - ROOT, (m - ROOT) % 2
                        act.wait_ge(stat, 10 * (q + 1))
                        nc.scalar.activation(rs[(m - ROOT) % 4][:], rv[b][:], ACT.Sqrt).then_inc(rs_ready, 1)
                    if on(TURN):
                        q, b = s - TURN, (m - TURN) % 2
                        act.wait_ge(x_turned, q + 1)
                        if on(TURN + 2):
                            act.wait_ge(sums_ready, q - 1)
                        nc.scalar.copy(xT[b][:], xTp[b][:].rearrange("p t d -> p (t d)")).then_inc(xT_ready, 1)
                sweep(step, STORE)(act)
                for b in range(2):
                    act.wait_ge(y_out[b], 16 * NG // 2)
                act.wait_ge(y_tail, 16)

            @block.vector
            def _(dve):
                def step(s, m, on):
                    if on(SEL):
                        q = s - SEL
                        if on(SEL + 4):
                            dve.wait_ge(sums_ready, q - 3)
                        build_sel(dve, q, sel[(m - SEL) % 4], sel_ready)
                    if on(MIX):
                        q, b, slot = s - MIX, (m - MIX) % 2, (m - MIX) % RING
                        dve.wait_ge(sums_ready, q + 1)
                        dve.wait_ge(x_in[slot], nth(q, slot, RING))
                        if on(MIX + 4):
                            dve.wait_ge(y_ready, G * (q - 3))
                        nc.vector.scalar_tensor_tensor(out=u[(m - MIX) % 4][:], in0=sums[b][:], scalar=0.0, in1=xin[:, slot, :, :],
                                                       op0=ALU.max, op1=ALU.add).then_inc(mix, 1)
                    if on(STAT):
                        q, b = s - STAT, (m - STAT) % 2
                        dve.wait_ge(mix, q + 1)
                        dve.sem_inc(passed, 1)
                        tile_stats(u[(m - STAT) % 4], st[b], stat)
                    if on(SHIFT):
                        q, b, c = s - SHIFT, (m - SHIFT) % 2, (m - SHIFT) % 4
                        dve.wait_ge(rs_ready, q + 1)
                        if on(SHIFT + 2):
                            dve.wait_ge(y_ready, G * (q - 1))
                        nc.vector.scalar_tensor_tensor(out=nm[b][:], in0=mv[c][:, :, 0], scalar=-1.0,
                                                       in1=rs[c][:], op0=ALU.mult, op1=ALU.mult).then_inc(nm_ready, 1)
                    if on(STAT):
                        q, b, c = s - STAT, (m - STAT) % 2, (m - STAT) % 4
                        merge_stats(dve, q, st[b], mv[c], stat, passed)
                        guard_var(dve, q, mv[c], rv[b], stat)
                    if on(STAT):
                        q, b = s - STAT, (m - STAT) % 2
                        invert_var(dve, q, rv[b], stat)
                sweep(step, SHIFT)(dve)

        collect()


_OUT = ((50000, 128), "float32")


def kernel(**inputs):
    import numpy as _np
    import concourse.bacc as _bacc
    from concourse import mybir as _mybir
    from concourse.bass_utils import run_bass_kernel_spmd as _run

    nc = _bacc.Bacc("TRN2", target_bir_lowering=False, num_devices=1)
    names = ["x", "src", "dst", "edge_attr_32", "edge_attr_32_n2", "edge_type_16", "L0_gnn_eps", "L0_gnn_W1",
             "L0_gnn_b1", "L0_gnn_W2", "L0_gnn_b2", "L0_gnn_gamma", "L0_gnn_beta", "L1_gnn_W1", "L1_gnn_b1",
             "L1_gnn_W2", "L1_gnn_b2", "L3_gnn_weight", "L3_gnn_comp", "L3_gnn_attn_w1", "L3_gnn_attn_b1",
             "L3_gnn_attn_w2", "L3_gnn_attn_b2", "L3_gnn_update"]
    arrays, args = {}, []
    for name in names:
        a = _np.ascontiguousarray(inputs[name])
        if name == "L0_gnn_eps":
            a = a.reshape(1, 1)
        arrays["in_" + name] = a
        args.append(nc.dram_tensor("in_" + name, a.shape, _mybir.dt.from_np(a.dtype), kind="ExternalInput").ap())
    out = nc.dram_tensor("out_0", inputs["x"].shape, F32, kind="ExternalOutput").ap()
    build(nc, *args, out)
    r = _run(nc, [arrays], core_ids=[0])
    return r.results[0]["out_0"]
```
